# Optimizing a Trainium2 kernel written in Bass

```python
import numpy as np
import jax
import jax.numpy as jnp

def _softmax(x, axis=-1):
    return jax.nn.softmax(x, axis=axis)

def _gelu(x):
    return jax.nn.gelu(x, approximate=True)

def _silu(x):
    return jax.nn.silu(x)

def _sigmoid(x):
    return jax.nn.sigmoid(x)

def _layernorm(x, axis=-1, eps=1e-05):
    m = jnp.mean(x, axis=axis, keepdims=True)
    v = jnp.var(x, axis=axis, keepdims=True)
    return (x - m) / jnp.sqrt(v + eps)

def _scatter_add(tgt, idx, src, axis=0):
    return tgt.at[idx].add(src)

def _segment_sum(src, seg, n):
    return jax.ops.segment_sum(src, seg, n)
kernel_name = 'mk_xattn_seq_d2_seqx_r4_8f3493'

def setup_inputs(seed: int=0):
    np.random.seed(seed)
    _w = jnp.asarray

    def _rec_inputs():
        import jax
        import jax.numpy as jnp
        _rk = jax.random.key(seed)
        x = 7.22e-05 + 1 * jax.random.normal(jax.random.fold_in(_rk, 1), (2, 1024, 256), jnp.float32)
        _lenS = 1024 - jax.random.randint(jax.random.fold_in(_rk, 7), (2,), 0, max(1, 1024 // 4) + 1, jnp.int32)
        _lenS2 = 77 - jax.random.randint(jax.random.fold_in(_rk, 8), (2,), 0, max(1, 77 // 4) + 1, jnp.int32)
        _ctx_768P = jax.random.normal(jax.random.fold_in(_rk, 11), (2, 16, 192), jnp.float32)
        _ctx_768c = jax.random.dirichlet(jax.random.fold_in(_rk, 511), 0.3 * jnp.ones((16,), jnp.float32), (2, 77))
        _ctx_768t = jnp.einsum('bsk,bkd->bsd', _ctx_768c, _ctx_768P)
        _ctx_768t = _ctx_768t * jax.lax.rsqrt(jnp.mean(jnp.square(_ctx_768t)) + 1e-12) * 0.953939
        ctx_768 = -0.00055796 + 0.999787 * (_ctx_768t + 0.3 * jax.random.normal(jax.random.fold_in(_rk, 611), (2, 77, 192), jnp.float32))
        _validS = jnp.arange(1024)[None, :] < _lenS[:, None]
        _validS2 = jnp.arange(77)[None, :] < _lenS2[:, None]
        _causal = jnp.tril(jnp.ones((1024, 1024), dtype=bool))
        mask_BxS_bf0 = jnp.logical_not(jnp.ones((2, 1024), dtype=bool))
        mask_BxS2_bf0 = jnp.logical_not(jnp.ones((2, 77), dtype=bool))
        return (x, ctx_768, mask_BxS_bf0, mask_BxS2_bf0)
    x, ctx_768, mask_BxS_bf0, mask_BxS2_bf0 = _rec_inputs()

    def _L0_xattn_setup():
        import jax, jax.numpy as jnp
        import numpy as np
        D_MODEL = 256
        D_COND = 192
        N_HEADS = 16
        D_HEAD = 64
        D_ATTN = N_HEADS * D_HEAD
        D_FF = 4 * D_MODEL

        def _layernorm(x, g, b, eps=1e-05):
            mu = jnp.mean(x, axis=-1, keepdims=True)
            var = jnp.var(x, axis=-1, keepdims=True)
            return (x - mu) * jax.lax.rsqrt(var + eps) * g + b

        def _attention(xq, xkv, wq, wk, wv, wo, bo):
            B, S, _ = xq.shape
            T = xkv.shape[1]
            q = (xq @ wq).reshape(B, S, N_HEADS, D_HEAD)
            k = (xkv @ wk).reshape(B, T, N_HEADS, D_HEAD)
            v = (xkv @ wv).reshape(B, T, N_HEADS, D_HEAD)
            scale = D_HEAD ** (-0.5)
            attn = jnp.einsum('bihd,bjhd->bhij', q, k) * scale
            attn = jax.nn.softmax(attn, axis=-1)
            out = jnp.einsum('bhij,bjhd->bihd', attn, v).reshape(B, S, D_ATTN)
            return out @ wo + bo
        key = jax.random.key(seed)
        ks = jax.random.split(key, 16)
        B, S, T = (8, 256, 64)
        n = jax.random.normal
        inp = {'x': n(ks[0], (B, S, D_MODEL), jnp.float32), 'cond_emb': n(ks[1], (B, T, D_COND), jnp.float32), 'ln1_g': jnp.ones((D_MODEL,), jnp.float32), 'ln1_b': jnp.zeros((D_MODEL,), jnp.float32), 'ln2_g': jnp.ones((D_MODEL,), jnp.float32), 'ln2_b': jnp.zeros((D_MODEL,), jnp.float32), 'ln3_g': jnp.ones((D_MODEL,), jnp.float32), 'ln3_b': jnp.zeros((D_MODEL,), jnp.float32), 'sa_wq': n(ks[2], (D_MODEL, D_ATTN), jnp.float32) * D_MODEL ** (-0.5), 'sa_wk': n(ks[3], (D_MODEL, D_ATTN), jnp.float32) * D_MODEL ** (-0.5), 'sa_wv': n(ks[4], (D_MODEL, D_ATTN), jnp.float32) * D_MODEL ** (-0.5), 'sa_wo': n(ks[5], (D_ATTN, D_MODEL), jnp.float32) * D_ATTN ** (-0.5), 'sa_bo': jnp.zeros((D_MODEL,), jnp.float32), 'ca_wq': n(ks[6], (D_MODEL, D_ATTN), jnp.float32) * D_MODEL ** (-0.5), 'ca_wk': n(ks[7], (D_COND, D_ATTN), jnp.float32) * D_COND ** (-0.5), 'ca_wv': n(ks[8], (D_COND, D_ATTN), jnp.float32) * D_COND ** (-0.5), 'ca_wo': n(ks[9], (D_ATTN, D_MODEL), jnp.float32) * D_ATTN ** (-0.5), 'ca_bo': jnp.zeros((D_MODEL,), jnp.float32), 'ff_w1': n(ks[10], (D_MODEL, 2 * D_FF), jnp.float32) * D_MODEL ** (-0.5), 'ff_b1': jnp.zeros((2 * D_FF,), jnp.float32), 'ff_w2': n(ks[11], (D_FF, D_MODEL), jnp.float32) * D_FF ** (-0.5), 'ff_b2': jnp.zeros((D_MODEL,), jnp.float32)}
        return inp
    _L0_xattn_all = _L0_xattn_setup()
    _L0_xattn_in = {k: v for k, v in _L0_xattn_all.items() if k in ('ln1_g', 'ln1_b', 'ln2_g', 'ln2_b', 'ln3_g', 'ln3_b', 'sa_wq', 'sa_wk', 'sa_wv', 'sa_wo', 'sa_bo', 'ca_wq', 'ca_wk', 'ca_wv', 'ca_wo', 'ca_bo', 'ff_w1', 'ff_b1', 'ff_w2', 'ff_b2')}
    del _L0_xattn_all

    def _L1_xattn_setup():
        import jax, jax.numpy as jnp
        import numpy as np
        D_DEC, D_ENC, H, D_MLP = (256, 192, 16, 1024)
        HD = D_DEC // H

        def _layernorm(x, w, b, eps=1e-05):
            m = x.mean(-1, keepdims=True)
            v = ((x - m) ** 2).mean(-1, keepdims=True)
            return (x - m) / jnp.sqrt(v + eps) * w + b

        def _decoder_block(x, enc, tgt_mask, enc_mask, ln1_w, ln1_b, qkv_w, qkv_b, proj_w, proj_b, ln2_w, ln2_b, q_w, q_b, k_w, k_b, v_w, v_b, out_w, out_b, ln3_w, ln3_b, mlp1_w, mlp1_b, mlp2_w, mlp2_b):
            B, T, C = x.shape
            S = enc.shape[1]
            scale = HD ** (-0.5)
            neg = jnp.asarray(-jnp.inf, x.dtype)
            h = _layernorm(x, ln1_w, ln1_b)
            qkv = (h @ qkv_w + qkv_b).reshape(B, T, 3, H, HD)
            q, k, v = [qkv[:, :, i].transpose(0, 2, 1, 3) for i in range(3)]
            attn = jnp.einsum('bhtd,bhsd->bhts', q, k) * scale
            causal = jnp.triu(jnp.ones((T, T), bool), 1)
            attn = jnp.where(causal[None, None], neg, attn)
            attn = jnp.where(tgt_mask[:, None, None, :], neg, attn)
            attn = jax.nn.softmax(attn, axis=-1)
            sa = jnp.einsum('bhts,bhsd->bhtd', attn, v).transpose(0, 2, 1, 3).reshape(B, T, C)
            x = x + sa @ proj_w + proj_b
            h = _layernorm(x, ln2_w, ln2_b)
            q = (h @ q_w + q_b).reshape(B, T, H, HD).transpose(0, 2, 1, 3)
            k = (enc @ k_w + k_b).reshape(B, S, H, HD).transpose(0, 2, 1, 3)
            v = (enc @ v_w + v_b).reshape(B, S, H, HD).transpose(0, 2, 1, 3)
            attn = jnp.einsum('bhtd,bhsd->bhts', q, k) * scale
            attn = jnp.where(enc_mask[:, None, None, :], neg, attn)
            attn = jax.nn.softmax(attn, axis=-1)
            ca = jnp.einsum('bhts,bhsd->bhtd', attn, v).transpose(0, 2, 1, 3).reshape(B, T, C)
            x = x + ca @ out_w + out_b
            h = _layernorm(x, ln3_w, ln3_b)
            h = jax.nn.gelu(h @ mlp1_w + mlp1_b, approximate=False)
            x = x + h @ mlp2_w + mlp2_b
            return x
        key = jax.random.key(seed)
        ks = jax.random.split(key, 16)
        B, T, S = (4, 256, 144)

        def lin(k, din, dout):
            kw, kb = jax.random.split(k)
            bound = 1.0 / np.sqrt(din)
            W = jax.random.uniform(kw, (din, dout), jnp.float32, -bound, bound)
            b = jax.random.uniform(kb, (dout,), jnp.float32, -bound, bound)
            return (W, b)
        qkv_w, qkv_b = lin(ks[0], D_DEC, 3 * D_DEC)
        proj_w, proj_b = lin(ks[1], D_DEC, D_DEC)
        q_w, q_b = lin(ks[2], D_DEC, D_DEC)
        k_w, k_b = lin(ks[3], D_ENC, D_DEC)
        v_w, v_b = lin(ks[4], D_ENC, D_DEC)
        out_w, out_b = lin(ks[5], D_DEC, D_DEC)
        mlp1_w, mlp1_b = lin(ks[6], D_DEC, D_MLP)
        mlp2_w, mlp2_b = lin(ks[7], D_MLP, D_DEC)
        return {'x': jax.random.normal(ks[8], (B, T, D_DEC), jnp.float32), 'enc': jax.random.normal(ks[9], (B, S, D_ENC), jnp.float32), 'tgt_key_padding_mask': jnp.zeros((B, T), bool), 'enc_padding_mask': jnp.zeros((B, S), bool), 'ln1_w': jnp.ones((D_DEC,)), 'ln1_b': jnp.zeros((D_DEC,)), 'qkv_w': qkv_w, 'qkv_b': qkv_b, 'proj_w': proj_w, 'proj_b': proj_b, 'ln2_w': jnp.ones((D_DEC,)), 'ln2_b': jnp.zeros((D_DEC,)), 'q_w': q_w, 'q_b': q_b, 'k_w': k_w, 'k_b': k_b, 'v_w': v_w, 'v_b': v_b, 'out_w': out_w, 'out_b': out_b, 'ln3_w': jnp.ones((D_DEC,)), 'ln3_b': jnp.zeros((D_DEC,)), 'mlp1_w': mlp1_w, 'mlp1_b': mlp1_b, 'mlp2_w': mlp2_w, 'mlp2_b': mlp2_b}
    _L1_xattn_all = _L1_xattn_setup()
    _L1_xattn_in = {k: v for k, v in _L1_xattn_all.items() if k in ('ln1_w', 'ln1_b', 'qkv_w', 'qkv_b', 'proj_w', 'proj_b', 'ln2_w', 'ln2_b', 'q_w', 'q_b', 'k_w', 'k_b', 'v_w', 'v_b', 'out_w', 'out_b', 'ln3_w', 'ln3_b', 'mlp1_w', 'mlp1_b', 'mlp2_w', 'mlp2_b')}
    del _L1_xattn_all
    return {'x': x, 'ctx_768': ctx_768, 'mask_BxS_bf0': mask_BxS_bf0, 'mask_BxS2_bf0': mask_BxS2_bf0, 'L0_xattn_ln1_g': _L0_xattn_in['ln1_g'], 'L0_xattn_ln1_b': _L0_xattn_in['ln1_b'], 'L0_xattn_ln2_g': _L0_xattn_in['ln2_g'], 'L0_xattn_ln2_b': _L0_xattn_in['ln2_b'], 'L0_xattn_ln3_g': _L0_xattn_in['ln3_g'], 'L0_xattn_ln3_b': _L0_xattn_in['ln3_b'], 'L0_xattn_sa_wq': _L0_xattn_in['sa_wq'], 'L0_xattn_sa_wk': _L0_xattn_in['sa_wk'], 'L0_xattn_sa_wv': _L0_xattn_in['sa_wv'], 'L0_xattn_sa_wo': _L0_xattn_in['sa_wo'], 'L0_xattn_sa_bo': _L0_xattn_in['sa_bo'], 'L0_xattn_ca_wq': _L0_xattn_in['ca_wq'], 'L0_xattn_ca_wk': _L0_xattn_in['ca_wk'], 'L0_xattn_ca_wv': _L0_xattn_in['ca_wv'], 'L0_xattn_ca_wo': _L0_xattn_in['ca_wo'], 'L0_xattn_ca_bo': _L0_xattn_in['ca_bo'], 'L0_xattn_ff_w1': _L0_xattn_in['ff_w1'], 'L0_xattn_ff_b1': _L0_xattn_in['ff_b1'], 'L0_xattn_ff_w2': _L0_xattn_in['ff_w2'], 'L0_xattn_ff_b2': _L0_xattn_in['ff_b2'], 'L1_xattn_ln1_w': _L1_xattn_in['ln1_w'], 'L1_xattn_ln1_b': _L1_xattn_in['ln1_b'], 'L1_xattn_qkv_w': _L1_xattn_in['qkv_w'], 'L1_xattn_qkv_b': _L1_xattn_in['qkv_b'], 'L1_xattn_proj_w': _L1_xattn_in['proj_w'], 'L1_xattn_proj_b': _L1_xattn_in['proj_b'], 'L1_xattn_ln2_w': _L1_xattn_in['ln2_w'], 'L1_xattn_ln2_b': _L1_xattn_in['ln2_b'], 'L1_xattn_q_w': _L1_xattn_in['q_w'], 'L1_xattn_q_b': _L1_xattn_in['q_b'], 'L1_xattn_k_w': _L1_xattn_in['k_w'], 'L1_xattn_k_b': _L1_xattn_in['k_b'], 'L1_xattn_v_w': _L1_xattn_in['v_w'], 'L1_xattn_v_b': _L1_xattn_in['v_b'], 'L1_xattn_out_w': _L1_xattn_in['out_w'], 'L1_xattn_out_b': _L1_xattn_in['out_b'], 'L1_xattn_ln3_w': _L1_xattn_in['ln3_w'], 'L1_xattn_ln3_b': _L1_xattn_in['ln3_b'], 'L1_xattn_mlp1_w': _L1_xattn_in['mlp1_w'], 'L1_xattn_mlp1_b': _L1_xattn_in['mlp1_b'], 'L1_xattn_mlp2_w': _L1_xattn_in['mlp2_w'], 'L1_xattn_mlp2_b': _L1_xattn_in['mlp2_b']}

def reference(x, ctx_768, mask_BxS_bf0, mask_BxS2_bf0, L0_xattn_ln1_g, L0_xattn_ln1_b, L0_xattn_ln2_g, L0_xattn_ln2_b, L0_xattn_ln3_g, L0_xattn_ln3_b, L0_xattn_sa_wq, L0_xattn_sa_wk, L0_xattn_sa_wv, L0_xattn_sa_wo, L0_xattn_sa_bo, L0_xattn_ca_wq, L0_xattn_ca_wk, L0_xattn_ca_wv, L0_xattn_ca_wo, L0_xattn_ca_bo, L0_xattn_ff_w1, L0_xattn_ff_b1, L0_xattn_ff_w2, L0_xattn_ff_b2, L1_xattn_ln1_w, L1_xattn_ln1_b, L1_xattn_qkv_w, L1_xattn_qkv_b, L1_xattn_proj_w, L1_xattn_proj_b, L1_xattn_ln2_w, L1_xattn_ln2_b, L1_xattn_q_w, L1_xattn_q_b, L1_xattn_k_w, L1_xattn_k_b, L1_xattn_v_w, L1_xattn_v_b, L1_xattn_out_w, L1_xattn_out_b, L1_xattn_ln3_w, L1_xattn_ln3_b, L1_xattn_mlp1_w, L1_xattn_mlp1_b, L1_xattn_mlp2_w, L1_xattn_mlp2_b):
    import jax
    import jax.numpy as jnp

    def _L0_xattn_ref(x, cond_emb, ln1_g, ln1_b, ln2_g, ln2_b, ln3_g, ln3_b, sa_wq, sa_wk, sa_wv, sa_wo, sa_bo, ca_wq, ca_wk, ca_wv, ca_wo, ca_bo, ff_w1, ff_b1, ff_w2, ff_b2):
        import jax, jax.numpy as jnp
        import numpy as np
        D_MODEL = 256
        D_COND = 192
        N_HEADS = 16
        D_HEAD = 64
        D_ATTN = N_HEADS * D_HEAD
        D_FF = 4 * D_MODEL

        def _layernorm(x, g, b, eps=1e-05):
            mu = jnp.mean(x, axis=-1, keepdims=True)
            var = jnp.var(x, axis=-1, keepdims=True)
            return (x - mu) * jax.lax.rsqrt(var + eps) * g + b

        def _attention(xq, xkv, wq, wk, wv, wo, bo):
            B, S, _ = xq.shape
            T = xkv.shape[1]
            q = (xq @ wq).reshape(B, S, N_HEADS, D_HEAD)
            k = (xkv @ wk).reshape(B, T, N_HEADS, D_HEAD)
            v = (xkv @ wv).reshape(B, T, N_HEADS, D_HEAD)
            scale = D_HEAD ** (-0.5)
            attn = jnp.einsum('bihd,bjhd->bhij', q, k) * scale
            attn = jax.nn.softmax(attn, axis=-1)
            out = jnp.einsum('bhij,bjhd->bihd', attn, v).reshape(B, S, D_ATTN)
            return out @ wo + bo
        h = _layernorm(x, ln1_g, ln1_b)
        x = _attention(h, h, sa_wq, sa_wk, sa_wv, sa_wo, sa_bo) + x
        h = _layernorm(x, ln2_g, ln2_b)
        x = _attention(h, cond_emb, ca_wq, ca_wk, ca_wv, ca_wo, ca_bo) + x
        h = _layernorm(x, ln3_g, ln3_b)
        p = h @ ff_w1 + ff_b1
        a, gate = (p[..., :D_FF], p[..., D_FF:])
        h = a * jax.nn.gelu(gate, approximate=False) @ ff_w2 + ff_b2
        return h + x

    def _L1_xattn_ref(x, enc, tgt_key_padding_mask, enc_padding_mask, ln1_w, ln1_b, qkv_w, qkv_b, proj_w, proj_b, ln2_w, ln2_b, q_w, q_b, k_w, k_b, v_w, v_b, out_w, out_b, ln3_w, ln3_b, mlp1_w, mlp1_b, mlp2_w, mlp2_b):
        import jax, jax.numpy as jnp
        import numpy as np
        D_DEC, D_ENC, H, D_MLP = (256, 192, 16, 1024)
        HD = D_DEC // H

        def _layernorm(x, w, b, eps=1e-05):
            m = x.mean(-1, keepdims=True)
            v = ((x - m) ** 2).mean(-1, keepdims=True)
            return (x - m) / jnp.sqrt(v + eps) * w + b

        def _decoder_block(x, enc, tgt_mask, enc_mask, ln1_w, ln1_b, qkv_w, qkv_b, proj_w, proj_b, ln2_w, ln2_b, q_w, q_b, k_w, k_b, v_w, v_b, out_w, out_b, ln3_w, ln3_b, mlp1_w, mlp1_b, mlp2_w, mlp2_b):
            B, T, C = x.shape
            S = enc.shape[1]
            scale = HD ** (-0.5)
            neg = jnp.asarray(-jnp.inf, x.dtype)
            h = _layernorm(x, ln1_w, ln1_b)
            qkv = (h @ qkv_w + qkv_b).reshape(B, T, 3, H, HD)
            q, k, v = [qkv[:, :, i].transpose(0, 2, 1, 3) for i in range(3)]
            attn = jnp.einsum('bhtd,bhsd->bhts', q, k) * scale
            causal = jnp.triu(jnp.ones((T, T), bool), 1)
            attn = jnp.where(causal[None, None], neg, attn)
            attn = jnp.where(tgt_mask[:, None, None, :], neg, attn)
            attn = jax.nn.softmax(attn, axis=-1)
            sa = jnp.einsum('bhts,bhsd->bhtd', attn, v).transpose(0, 2, 1, 3).reshape(B, T, C)
            x = x + sa @ proj_w + proj_b
            h = _layernorm(x, ln2_w, ln2_b)
            q = (h @ q_w + q_b).reshape(B, T, H, HD).transpose(0, 2, 1, 3)
            k = (enc @ k_w + k_b).reshape(B, S, H, HD).transpose(0, 2, 1, 3)
            v = (enc @ v_w + v_b).reshape(B, S, H, HD).transpose(0, 2, 1, 3)
            attn = jnp.einsum('bhtd,bhsd->bhts', q, k) * scale
            attn = jnp.where(enc_mask[:, None, None, :], neg, attn)
            attn = jax.nn.softmax(attn, axis=-1)
            ca = jnp.einsum('bhts,bhsd->bhtd', attn, v).transpose(0, 2, 1, 3).reshape(B, T, C)
            x = x + ca @ out_w + out_b
            h = _layernorm(x, ln3_w, ln3_b)
            h = jax.nn.gelu(h @ mlp1_w + mlp1_b, approximate=False)
            x = x + h @ mlp2_w + mlp2_b
            return x
        return _decoder_block(x, enc, tgt_key_padding_mask, enc_padding_mask, ln1_w, ln1_b, qkv_w, qkv_b, proj_w, proj_b, ln2_w, ln2_b, q_w, q_b, k_w, k_b, v_w, v_b, out_w, out_b, ln3_w, ln3_b, mlp1_w, mlp1_b, mlp2_w, mlp2_b)
    x = _L0_xattn_ref(x, ctx_768, L0_xattn_ln1_g, L0_xattn_ln1_b, L0_xattn_ln2_g, L0_xattn_ln2_b, L0_xattn_ln3_g, L0_xattn_ln3_b, L0_xattn_sa_wq, L0_xattn_sa_wk, L0_xattn_sa_wv, L0_xattn_sa_wo, L0_xattn_sa_bo, L0_xattn_ca_wq, L0_xattn_ca_wk, L0_xattn_ca_wv, L0_xattn_ca_wo, L0_xattn_ca_bo, L0_xattn_ff_w1, L0_xattn_ff_b1, L0_xattn_ff_w2, L0_xattn_ff_b2)
    x = _L1_xattn_ref(x, ctx_768, mask_BxS_bf0, mask_BxS2_bf0, L1_xattn_ln1_w, L1_xattn_ln1_b, L1_xattn_qkv_w, L1_xattn_qkv_b, L1_xattn_proj_w, L1_xattn_proj_b, L1_xattn_ln2_w, L1_xattn_ln2_b, L1_xattn_q_w, L1_xattn_q_b, L1_xattn_k_w, L1_xattn_k_b, L1_xattn_v_w, L1_xattn_v_b, L1_xattn_out_w, L1_xattn_out_b, L1_xattn_ln3_w, L1_xattn_ln3_b, L1_xattn_mlp1_w, L1_xattn_mlp1_b, L1_xattn_mlp2_w, L1_xattn_mlp2_b)
    return x

_drawn_inputs = setup_inputs


def setup_inputs(seed=0):
    import zlib

    import numpy as np

    out = dict(_drawn_inputs(seed))
    spreads = {'L0_xattn_ln1_g': (1.0, 0.2),
     'L0_xattn_ln1_b': (0.0, 0.1),
     'L0_xattn_ln2_g': (1.0, 0.2),
     'L0_xattn_ln2_b': (0.0, 0.314),
     'L0_xattn_ln3_g': (1.0, 0.2),
     'L0_xattn_ln3_b': (0.0, 0.1),
     'L0_xattn_sa_bo': (0.0, 0.1),
     'L0_xattn_ca_bo': (0.0, 0.1),
     'L0_xattn_ff_b1': (0.0, 0.1),
     'L0_xattn_ff_b2': (0.0, 0.1),
     'L1_xattn_ln1_w': (1.0, 0.6),
     'L1_xattn_ln1_b': (0.0, 0.341),
     'L1_xattn_ln2_w': (1.0, 0.6),
     'L1_xattn_ln2_b': (0.0, 0.8),
     'L1_xattn_ln3_w': (1.0, 0.594),
     'L1_xattn_ln3_b': (0.0, 0.585)}
    factors = {'L1_xattn_qkv_b': 4.276,
     'L1_xattn_q_w': 3.464,
     'L1_xattn_q_b': 8.0,
     'L1_xattn_k_w': 3.392,
     'L1_xattn_k_b': 8.0,
     'L1_xattn_v_b': 3.238,
     'L1_xattn_mlp1_b': 6.072,
     'L1_xattn_mlp2_b': 4.396}
    for name, (base, spread) in spreads.items():
        noise = np.random.default_rng([zlib.crc32(name.encode()), seed]).standard_normal(out[name].shape)
        drawn = base * np.exp(spread * noise) if base else spread * noise
        out[name] = jnp.asarray(drawn.astype(out[name].dtype))
    for name, factor in factors.items():
        out[name] = (out[name] * factor).astype(out[name].dtype)
    return out
```

```python
from contextlib import ExitStack

import concourse.bass as bass
from concourse import mybir

F32 = mybir.dt.float32
F32R = mybir.dt.float32r
BF16 = mybir.dt.bfloat16
U8 = mybir.dt.uint8
ALU = mybir.AluOpType
ACT = mybir.ActivationFunctionType
AX = mybir.AxisListType

P = 128
B, T, D = 2, 1024, 256
TC, DC = 77, 192
NT = B * T
TT = NT // P
KD = D // P
KC, CW = 2, DC // 2
HEADS = 16
EPS = 1e-5
LOW = -1e30
HALF = 512
DMA = 16
QT = T // P


def lin(g, b, per, k):
    return g * (2 * per) + (b * per + k)


class Step:

    def __init__(self, sem):
        self.sem, self.n = sem, 0

    def __call__(self, ins):
        self.n += 1
        return ins.then_inc(self.sem, 1)

    def wait(self, eng):
        eng.wait_ge(self.sem, self.n)


def attention(nc, name, cfg, hT, ctxT, ident, ones, w, oT, spare=None):
    G, dh, causal, cross, biased = cfg["G"], cfg["dh"], cfg["causal"], cfg["cross"], cfg["biased"]
    wide = dh == 64
    NG = HEADS // G
    GD = G * dh
    KT = 1 if cross else T // P
    KW = P if cross else T
    NK = TC if cross else T
    NQ = 2 if wide else 1
    MROW = 64 if wide else 96
    KMAX = P if wide else 96
    VW = P // G
    SCALE = float(dh) ** -0.5
    NE = G * KT
    NP = 2 * G
    NADD = G * (KT - 2) if wide and KT > 1 else 0
    joint = not wide and not cross

    proj = [("qk", c) for c in range(2)] if joint else [("q", c) for c in range(2)] + (
        [("k", 0)] if cross else [("k", c) for c in range(2)])
    vs = [("v", c) for c in range(1 if cross or not wide else 2)]
    if cross:
        maxes = [("m", j, 4 * c, 0, TC) for j in range(G) for c in range(2)]
    elif causal:
        maxes = [("m", j, qt, h, min(HALF, (qt + 1) * P - h * HALF))
                 for j in range(G) for qt in range(QT) for h in range(2) if (qt + 1) * P > h * HALF]
    else:
        maxes = [("m", j, qt, h, HALF) for j in range(G) for qt in range(QT) for h in range(2)]
    items = proj + vs + maxes + [("t",)]
    NF = len(items)
    NDEN = 2 if wide else 0
    NCH = NF + NDEN
    IV = len(proj) + len(vs) - 1

    back = []
    for kt in range(KT):
        back += [("s", j, kt) for j in range(G)]
        if kt:
            back.append(("pv", kt - 1))
    back.append(("pv", KT - 1))

    def woven():
        nb = len(back)
        lead = len(proj) + len(vs)
        first_m = 2 if cross else min(6, nb - 2)
        last_m = nb - 2 if cross else nb - 5
        out, at = [], 0
        for i, piece in enumerate(back):
            out.append(("back", piece, None))
            if i < first_m:
                want = lead * (i + 1) // first_m
            elif i >= last_m:
                want = NF
            else:
                want = lead + len(maxes) * (i - first_m + 1) // max(1, last_m - first_m)
                want = min(want, NF - 1)
            while at < want:
                out.append(("front", items[at], at))
                at += 1
        return out

    WOVEN = woven()
    FRONT = [("front", it, i) for i, it in enumerate(items)]
    BACK = [("back", piece, None) for piece in back]

    def walk(eng, front, both, tail):
        front(0, 0)
        both(0, 0)
        both(0, 1)
        if NG > 4:
            with eng.Fori(1, NG - 1, 1) as g:
                both(g, 0)
                both(g, 1)
        else:
            for g in range(1, NG - 1):
                both(g, 0)
                both(g, 1)
        both(NG - 1, 0)
        tail(NG - 1, 1)

    def after(g, b):
        return (g, 1) if b == 0 else (g + 1, 0)

    def front_chunk(g, b, i):
        if isinstance(g, int) and (g, b) == (0, 0):
            return i
        return lin(g, b, NCH, NF - NCH + i)

    def den_chunk(g, b, c):
        last = isinstance(g, int) and (g, b) == (NG - 1, 1)
        return lin(g, b, NCH, NF + (0 if last else NF) + c)

    def front_bank(g, b, i):
        return i % 2 if isinstance(g, int) and (g, b) == (0, 0) else (b * NCH + NF - NCH + i) % 2

    def den_bank(g, b, c):
        last = isinstance(g, int) and (g, b) == (NG - 1, 1)
        return (b * NCH + NF + (0 if last else NF) + c) % 2

    def spans(kt):
        q0 = kt * P if causal else 0
        return [(max(q0, lo), lo + HALF) for lo in (0, HALF) if q0 < lo + HALF]

    with ExitStack() as ctx:
        def sb(n, shape, dt=F32):
            return ctx.enter_context(nc.sbuf_tensor(f"{name}_{n}", shape, dt))

        def ps(n, shape):
            return ctx.enter_context(nc.psum_tensor(f"{name}_{n}", shape, F32))

        def sem(n):
            return ctx.enter_context(nc.semaphore(f"{name}_{n}"))

        q_stage = sb("q_stage", [P, 2, G, NQ, T], F32R)
        k_stage = sb("k_stage", [P, 2, G, NQ, KW], F32R)
        v_buf = sb("v_buf", [P, 2, KT, P])
        q_hi, q_lo = sb("q_hi", [P, T], F32R), sb("q_lo", [P, T], F32R)
        if joint:
            k_hi, k_lo = q_hi, q_lo
        else:
            k_hi, k_lo = sb("k_hi", [P, KW], F32R), sb("k_lo", [P, KW], F32R)
        p_buf = sb("p_buf", [P, NP, T])
        if spare is None:
            acc, recip = None, sb("recip", [P, T])
        else:
            acc = spare[:].rearrange("p t d -> p (t d)")[:, 0:G * T].rearrange("p (g t) -> p g t", g=G)
            recip = spare[:].rearrange("p t d -> p (t d)")[:, G * T:(G + 1) * T]
        KDk = KC if cross else KD
        wq = sb("wq", [P, KD, P])
        wk = None if joint else sb("wk", [P, KDk, P])
        wv = sb("wv", [P, KDk, GD])
        bq = sb("bq", [P, 1]) if biased else None
        bk = sb("bk", [P, 1]) if biased and cross else None
        bv = sb("bv", [P, GD]) if biased else None
        mx = sb("mx", [P, 2, G, QT, 2])
        m_row = sb("m_row", [P, G, QT])
        m_hi = sb("m_hi", [P, G, QT], F32R)
        m_parts = sb("m_parts", [P, G, 2, QT])
        m_turned = sb("m_turned", [2 * G * QT, P], F32R)
        junk = sb("junk", [P, 2, HALF], BF16 if causal else F32) if biased else None

        front_ps = [ps(f"front{i}", [P, HALF]) for i in range(2)]
        score_ps = [ps(f"score{i}", [P, T]) for i in range(2)]
        out_ps = ps("out", [P, T])

        cleared = sem("cleared")
        w_in = sem("w_in")
        front_full = sem("front_full")
        hi_done = sem("hi_done")
        drained = sem("drained")
        stage_in = sem("stage_in")
        max_in = sem("max_in")
        m_step = sem("m_step")
        score_full = sem("score_full")
        exp_done = sem("exp_done")
        diag_done = sem("diag_done") if causal else None
        added = sem("added") if NADD else None
        pv_done = sem("pv_done")
        masked = sem("masked") if cross and biased else None
        norm = sem("norm")
        out_done = sem("out_done")

        w_dmas = []

        def cols(ap, g, width, start=0):
            return ap[:, :, bass.ds(g * width + start, width)]

        if joint:
            w_dmas.append((wq[:, :, 0:GD], lambda g: cols(w["q"], g, GD)))
            w_dmas.append((wq[:, :, GD:2 * GD], lambda g: cols(w["q"], g, GD, D)))
            w_dmas.append((wv[:], lambda g: cols(w["q"], g, GD, 2 * D)))
        elif cross:
            w_dmas.append((wq[:, :, 0:GD], lambda g: cols(w["q"], g, GD)))
            w_dmas.append((wk[0:CW, :, 0:GD], lambda g: cols(w["k"], g, GD)))
            w_dmas.append((wv[0:CW, :, :], lambda g: cols(w["v"], g, GD)))
        else:
            w_dmas.append((wq[:, :, 0:GD], lambda g: cols(w["q"], g, GD)))
            w_dmas.append((wk[:, :, 0:GD], lambda g: cols(w["k"], g, GD)))
            w_dmas.append((wv[:], lambda g: cols(w["v"], g, GD)))
        if biased:
            w_dmas.append((bq[0:GD, :], lambda g: w["bq"][bass.ds(g * GD, GD), :]))
            if joint:
                w_dmas.append((bq[GD:2 * GD, :], lambda g: w["bq"][bass.ds(g * GD + D, GD), :]))
            else:
                w_dmas.append((bk[0:GD, :], lambda g: w["bk"][bass.ds(g * GD, GD), :]))
            w_dmas.append((bv[:, :], lambda g: w["bv"][:, bass.ds(g * GD, GD)].to_broadcast((P, GD))))
        NW = len(w_dmas)

        def stage_dmas(b):
            out = []
            for j in range(G):
                r = slice(dh * j, dh * j + dh)
                if wide:
                    q, k = q_stage[:, b, j, :, :], k_stage[:, b, j, :, 0:NK]
                    out.append((q[0:64, 0, :], q_hi[r, :]))
                    out.append((q[0:64, 1, :], q_hi[r, :]))
                    out.append((q[64:128, 0, :], q_lo[r, :]))
                    out.append((k[0:64, 0, :], k_hi[r, 0:NK]))
                    out.append((k[64:128, 0, :], k_hi[r, 0:NK]))
                    out.append((k[0:64, 1, :], k_lo[r, 0:NK]))
                else:
                    q, k = q_stage[:, b, j, 0, :], k_stage[:, b, j, 0, 0:NK]
                    s = slice(dh * j + (GD if joint else 0), dh * j + dh + (GD if joint else 0))
                    for at, src in ((0, q_hi), (1, q_lo), (2, q_hi)):
                        out.append((q[16 * at:16 * at + 16, :], src[r, :]))
                    for at, src in ((0, k_hi), (1, k_hi), (2, k_lo)):
                        out.append((k[16 * at:16 * at + 16, :], src[s, 0:NK]))
            return out

        NS = len(stage_dmas(0))

        with nc.Block() as block:
            @block.sync
            def _(sp):
                def weights(g):
                    for dst, src in w_dmas:
                        sp.dma_start(dst, src(g)).then_inc(w_in, DMA)

                def front(g, b, load=None):
                    sp.wait_ge(drained, front_chunk(g, b, len(proj) - 1) + 1)
                    for dst, src in stage_dmas(b):
                        sp.dma_start(dst.bitcast(F32), src.bitcast(F32)).then_inc(stage_in, DMA)
                    if load is not None:
                        sp.wait_ge(drained, front_chunk(g, b, IV) + 1)
                        weights(load)
                    sp.wait_ge(drained, front_chunk(g, b, NF - 1) + 1)
                    for j in range(G):
                        for part in range(2):
                            r = (j * 2 + part) * QT
                            sp.dma_start(
                                q_stage[MROW + part:MROW + part + 1, b, j, NQ - 1, :].bitcast(F32),
                                m_turned[r:r + QT, :].bitcast(F32)).then_inc(max_in, DMA)

                def both(g, b):
                    g2, b2 = after(g, b)
                    last = isinstance(g2, int) and g2 == NG - 1
                    front(g2, b2, g2 + 1 if b2 == 1 and not last else None)

                weights(0)
                sp.wait_ge(cleared, 2)
                walk(sp, front, both, lambda g, b: None)

            @block.tensor
            def _(pe):
                def front_item(g, b, item, i):
                    kind = item[0]
                    c = front_chunk(g, b, i)
                    fr = front_ps[front_bank(g, b, i)]
                    if not isinstance(c, int) or c >= 2:
                        pe.wait_ge(drained, c - 1)
                    if kind in ("q", "qk") and item[1] == 0:
                        pe.wait_ge(w_in, (g + 1) * (DMA * NW))
                    if kind in ("q", "qk", "k"):
                        wt = wk if kind == "k" else wq
                        M = P if kind == "qk" else GD
                        if kind == "k" and cross:
                            for kd in range(KC):
                                mm = pe.matmul(fr[0:M, 0:TC], wt[0:CW, kd, 0:M], ctxT[0:CW, b, kd, 0:TC],
                                               start=(kd == 0), stop=(kd == KC - 1))
                        else:
                            at = b * T + item[1] * HALF
                            for kd in range(KD):
                                mm = pe.matmul(fr[0:M, :], wt[:, kd, 0:M], hT[:, kd, at:at + HALF],
                                               start=(kd == 0), stop=(kd == KD - 1))
                    elif kind == "v":
                        if cross:
                            for kd in range(KC):
                                mm = pe.matmul(fr[0:TC, 0:GD], ctxT[0:CW, b, kd, 0:TC], wv[0:CW, kd, :],
                                               start=(kd == 0), stop=(kd == KC - 1))
                        else:
                            n = HALF // GD
                            for t in range(n):
                                at = b * T + (item[1] * n + t) * P
                                for kd in range(KD):
                                    mm = pe.matmul(fr[:, t * GD:(t + 1) * GD], hT[:, kd, at:at + P], wv[:, kd, :],
                                                   start=(kd == 0), stop=(kd == KD - 1))
                    elif kind == "m":
                        _, j, qt, half, width = item
                        if (j, qt, half) == (0, 0, 0):
                            pe.wait_ge(stage_in, lin(g, b, DMA * NS, DMA * NS))
                        if cross:
                            for t in range(4):
                                q = q_stage[0:KMAX, b, j, 0, (qt + t) * P:(qt + t + 1) * P]
                                mm = pe.matmul(fr[:, t * 80:t * 80 + TC + 1], q, k_stage[0:KMAX, b, j, 0, 0:TC + 1],
                                               start=True, stop=True)
                        else:
                            q = q_stage[0:KMAX, b, j, 0, qt * P:(qt + 1) * P]
                            k = k_stage[0:KMAX, b, j, 0, half * HALF:half * HALF + width]
                            mm = pe.matmul(fr[:, 0:width], q, k, start=True, stop=True)
                    else:
                        pe.wait_ge(m_step, lin(g, b, 3, 3))
                        parts = m_parts[:].rearrange("p g s t -> p (g s t)")
                        mm = pe.transpose(fr[0:2 * G * QT, 0:P], parts, ident[:])
                    mm.then_inc(front_full, 1)

                def back_piece(g, b, piece):
                    first = isinstance(g, int) and (g, b) == (0, 0)
                    if piece[0] == "s":
                        _, j, kt = piece
                        i = kt * G + j
                        if i == 0:
                            pe.wait_ge(max_in, lin(g, b, DMA * 2 * G, DMA * 2 * G))
                        if not (first and i < 2):
                            pe.wait_ge(exp_done, lin(g, b, NE, i - 1))
                        dst = score_ps[i % 2]
                        for lo, hi in spans(kt):
                            for s in range(NQ):
                                mm = pe.matmul(dst[:, lo:hi], k_stage[:, b, j, s, kt * P:(kt + 1) * P],
                                               q_stage[:, b, j, s, lo:hi], start=(s == 0), stop=(s == NQ - 1))
                        mm.then_inc(score_full, 1)
                    else:
                        kt = piece[1]
                        if causal:
                            pe.wait_ge(diag_done, lin(g, b, NE, (kt + 1) * G))
                        else:
                            pe.wait_ge(exp_done, lin(g, b, NE, (kt + 1) * G))
                        if kt == 0 and not first:
                            pe.wait_ge(out_done, lin(g, b, 1, 0))
                        for lo, hi in spans(kt):
                            last = kt == KT - 1 or (causal and kt == 3 and lo < HALF)
                            for j in range(G):
                                e = (b * NE + kt * G + j) % NP
                                mm = pe.matmul(out_ps[VW * j:VW * j + VW, lo:hi],
                                               v_buf[:, b, kt, VW * j:VW * j + VW], p_buf[:, e, lo:hi],
                                               start=(kt == 0), stop=last, skip_group_check=True)
                        mm.then_inc(pv_done, 1)

                def denominators(g, b):
                    if not wide:
                        return
                    for c in range(2):
                        pe.wait_ge(drained, den_chunk(g, b, c) - 1)
                        if NADD and c == 0:
                            pe.wait_ge(added, lin(g, b, NADD, NADD))
                        fr = front_ps[den_bank(g, b, c)]
                        at = slice(c * HALF, (c + 1) * HALF)
                        for j in range(G):
                            e = (b * NE + (KT - 1) * G + j) % NP
                            if NADD:
                                pe.matmul(fr[64 * j:64 * j + 64, :], ones[:, 0:64], acc[:, j, at], start=True, stop=False)
                            mm = pe.matmul(fr[64 * j:64 * j + 64, :], ones[:, 0:64], p_buf[:, e, at],
                                           start=not NADD, stop=True)
                        mm.then_inc(front_full, 1)

                def front(g, b):
                    for _, it, i in FRONT:
                        front_item(g, b, it, i)

                def both(g, b):
                    for which, it, i in WOVEN:
                        if which == "back":
                            back_piece(g, b, it)
                        else:
                            front_item(*after(g, b), it, i)
                    denominators(g, b)

                def tail(g, b):
                    for _, it, _i in BACK:
                        back_piece(g, b, it)
                    denominators(g, b)

                pe.wait_ge(cleared, 2)
                walk(pe, front, both, tail)

            @block.scalar
            def _(act):
                def front_item(g, b, item, i):
                    if item[0] not in ("q", "k", "qk"):
                        return
                    c = front_chunk(g, b, i)
                    first = isinstance(g, int) and (g, b) == (0, 0)
                    if i == 0 and not first:
                        act.wait_ge(stage_in, lin(g, b, DMA * NS, 0))
                    act.wait_ge(front_full, c + 1)
                    fr = front_ps[front_bank(g, b, i)]
                    rows = P if item[0] == "qk" else GD
                    n = TC if (cross and item[0] == "k") else HALF
                    dst = (k_hi if item[0] == "k" else q_hi)[0:rows, item[1] * HALF:item[1] * HALF + n]
                    bias = (bk if item[0] == "k" else bq)[0:rows, 0:1] if biased else 0.0
                    nc.scalar.activation(dst, fr[0:rows, 0:n], ACT.Identity, bias=bias).then_inc(hi_done, 1)

                def back_piece(g, b, piece):
                    if piece[0] != "s":
                        return
                    _, j, kt = piece
                    first = isinstance(g, int) and (g, b) == (0, 0)
                    i = kt * G + j
                    e = (b * NE + i) % NP
                    act.wait_ge(score_full, lin(g, b, NE, i + 1))
                    second = first and kt < 2 or (isinstance(g, int) and KT == 1 and (g, b) == (0, 1))
                    if not second:
                        act.wait_ge(pv_done, lin(g, b, KT, kt - 1))
                        if NADD and kt >= 2:
                            act.wait_ge(added, lin(g, b, NADD, (max(kt - 2, 1) - 1) * G + j + 1))
                        elif wide and (kt == 1 or KT == 1):
                            back_n = 1 if KT > 1 else 2
                            pg, pb = (g, 0) if b == 1 and back_n == 1 else (g - 1, b if back_n == 2 else 1)
                            act.wait_ge(front_full, lin(pg, pb, NCH, 2 * NF + 2))
                        elif NADD:
                            act.wait_ge(added, lin(g, b, NADD, 0))
                    q0 = kt * P if causal else 0
                    bias = w["key_bias"](b, kt)
                    nc.scalar.activation(p_buf[:, e, q0:T], score_ps[i % 2][:, q0:T], ACT.Exp, bias=bias,
                                         scale=SCALE).then_inc(exp_done, 1)

                def front(g, b):
                    for _, it, i in FRONT:
                        front_item(g, b, it, i)

                def both(g, b):
                    for which, it, i in WOVEN:
                        if which == "back":
                            back_piece(g, b, it)
                        else:
                            front_item(*after(g, b), it, i)

                def tail(g, b):
                    for _, it, _i in BACK:
                        back_piece(g, b, it)

                walk(act, front, both, tail)

            @block.vector
            def _(dve):
                kb = k_stage[:].bitcast(F32)
                r0 = MROW if wide and not cross else 0
                dve.memset(kb[r0:P, :, :, NQ - 1, :] if r0 else kb, 0.0).then_inc(norm, 1)
                dve.memset(v_buf[:], 1.0)
                dve.memset(mx[:], 4.0 * LOW)
                dve.wait_ge(norm, 1)
                dve.memset(kb[MROW:MROW + 2, :, :, NQ - 1, :], 1.0).then_inc(cleared, 1)

                def front_item(g, b, item, i):
                    kind = item[0]
                    c = front_chunk(g, b, i)
                    fr = front_ps[front_bank(g, b, i)]
                    first = isinstance(g, int) and (g, b) == (0, 0)
                    if kind in ("q", "k", "qk"):
                        rows = P if kind == "qk" else GD
                        n = TC if (cross and kind == "k") else HALF
                        at = slice(item[1] * HALF, item[1] * HALF + n)
                        hi, lo = (k_hi, k_lo) if kind == "k" else (q_hi, q_lo)
                        if i == 0 and not first:
                            dve.wait_ge(stage_in, lin(g, b, DMA * NS, 0))
                        dve.wait_ge(hi_done, lin(g, b, len(proj), i + 1))
                        if biased:
                            bias = (bk if kind == "k" else bq)[0:rows, 0:1]
                            ins = dve.scalar_tensor_tensor(out=lo[0:rows, at], in0=fr[0:rows, 0:n], scalar=bias,
                                                           in1=hi[0:rows, at].bitcast(F32), op0=ALU.add,
                                                           op1=ALU.subtract)
                        else:
                            ins = dve.tensor_tensor(lo[0:rows, at], fr[0:rows, 0:n], hi[0:rows, at].bitcast(F32),
                                                    ALU.subtract)
                        ins.then_inc(drained, 1)
                    elif kind == "v":
                        dve.wait_ge(front_full, c + 1)
                        rows = TC if cross else P
                        n = KT if cross else HALF // GD
                        src = fr[0:rows, 0:n * GD].rearrange("p (t j d) -> p t j d", t=n, j=G)
                        dst = v_buf[0:rows, b, item[1] * n:item[1] * n + n, :].rearrange("p t (j d) -> p t j d", j=G)
                        if n == 1:
                            src, dst = src[:, 0], dst[:, 0]
                        if biased:
                            bb = bv[0:rows, :].rearrange("p (j d) -> p j d", j=G)
                            if n > 1:
                                bb = bb.unsqueeze(1).to_broadcast((rows, n, G, dh))
                                ins = dve.tensor_tensor(dst[:, :, :, 0:dh], src, bb, ALU.add)
                            else:
                                ins = dve.tensor_tensor(dst[:, :, 0:dh], src, bb, ALU.add)
                        else:
                            ins = dve.tensor_copy(dst, src)
                        ins.then_inc(drained, 1)
                    elif kind == "m":
                        _, j, qt, half, width = item
                        dve.wait_ge(front_full, c + 1)
                        if cross:
                            src = fr[:, 0:320].rearrange("p (t k) -> p t k", k=80)[:, :, 0:TC]
                            if biased:
                                dve.wait_ge(drained, c - 1)
                                tmp = junk[:, c % 2, 0:4 * 80].rearrange("p (t k) -> p t k", k=80)[:, :, 0:TC]
                                dve.tensor_tensor(tmp, src, w["key_low"](b).unsqueeze(1).to_broadcast((P, 4, TC)),
                                                  ALU.add).then_inc(masked, 1)
                                dve.wait_ge(masked, lin(g, b, len(maxes), i - IV))
                                src = tmp
                            dve.tensor_reduce(mx[:, b, j, qt:qt + 4, 0], src, AX.X, ALU.max).then_inc(drained, 1)
                        elif causal:
                            low = w["key_low"](b, qt, half * HALF, width)
                            dve.wait_ge(drained, c - 1)
                            dve.tensor_tensor_reduce(junk[:, c % 2, 0:width], fr[:, 0:width], low, 1.0, 16.0 * LOW, ALU.add,
                                                     ALU.max, mx[:, b, j, qt, half:half + 1]).then_inc(drained, 1)
                        else:
                            dve.tensor_reduce(mx[:, b, j, qt, half:half + 1], fr[:, 0:width], AX.X,
                                              ALU.max).then_inc(drained, 1)
                    else:
                        dve.wait_ge(drained, c)
                        dve.tensor_tensor(m_row[:], mx[:, b, :, :, 0], mx[:, b, :, :, 1], ALU.max).then_inc(m_step, 1)
                        dve.wait_ge(m_step, lin(g, b, 3, 1))
                        dve.tensor_scalar(m_hi[:], m_row[:], -1.0, None, ALU.mult).then_inc(m_step, 1)
                        dve.wait_ge(m_step, lin(g, b, 3, 2))
                        dve.tensor_copy(m_parts[:, :, 0, :], m_hi[:].bitcast(F32))
                        dve.scalar_tensor_tensor(out=m_parts[:, :, 1, :], in0=m_row[:], scalar=-1.0,
                                                 in1=m_hi[:].bitcast(F32), op0=ALU.mult,
                                                 op1=ALU.subtract).then_inc(m_step, 1)
                        if not first:
                            dve.wait_ge(max_in, lin(g, b, DMA * 2 * G, 0))
                        dve.wait_ge(front_full, c + 1)
                        dve.tensor_copy(m_turned[:], fr[0:2 * G * QT, 0:P]).then_inc(drained, 1)

                def finish(g, b):
                    dst = oT[:, bass.ds(g, 1), b * T:(b + 1) * T] if not isinstance(g, int) else oT[:, g:g + 1, b * T:(b + 1) * T]
                    if wide:
                        for c in range(2):
                            at = slice(c * HALF, (c + 1) * HALF)
                            k = den_chunk(g, b, c)
                            dve.wait_ge(front_full, k + 1)
                            dve.reciprocal(recip[:, at], front_ps[den_bank(g, b, c)][:, :]).then_inc(drained, 1)
                        dve.wait_ge(drained, den_chunk(g, b, 1) + 1)
                        dve.wait_ge(pv_done, lin(g, b, KT, KT))
                        dve.tensor_tensor(dst[:, 0], out_ps[:], recip[:], ALU.mult).then_inc(out_done, 1)
                    else:
                        dve.wait_ge(pv_done, lin(g, b, KT, KT))
                        dve.reciprocal(recip[:], out_ps[:]).then_inc(norm, 1)
                        dve.wait_ge(norm, lin(g, b, 2, 2))
                        dve.stream_shuffle(recip[:], recip[:], [dh] * 32).then_inc(norm, 1)
                        dve.wait_ge(norm, lin(g, b, 2, 3))
                        dve.tensor_tensor(dst[:, 0], out_ps[:], recip[:], ALU.mult).then_inc(out_done, 1)

                def front(g, b):
                    for _, it, i in FRONT:
                        front_item(g, b, it, i)

                def both(g, b):
                    for which, it, i in WOVEN:
                        if which == "front":
                            front_item(*after(g, b), it, i)
                    finish(g, b)

                walk(dve, front, both, finish)

            @block.gpsimd
            def _(pool):
                qb = q_stage[:].bitcast(F32)
                if wide:
                    pool.memset(qb[64:P, :, :, 1, :], 0.0).then_inc(cleared, 1)
                else:
                    pool.memset(qb, 0.0).then_inc(cleared, 1)
                if causal:
                    def both(g, b):
                        for kt in range(KT):
                            for j in range(G):
                                i = kt * G + j
                                blk = p_buf[:, (b * NE + i) % NP, kt * P:(kt + 1) * P]
                                pool.wait_ge(exp_done, lin(g, b, NE, i + 1))
                                nc.gpsimd.affine_select(out=blk, in_=blk, compare_op=ALU.is_ge, fill=0.0, base=0,
                                                        pattern=[[1, P]], channel_multiplier=-1).then_inc(diag_done, 1)
                    walk(pool, lambda g, b: None, both, both)
                elif NADD:
                    def both(g, b):
                        for kt in range(1, KT - 1):
                            for j in range(G):
                                i = kt * G + j
                                cur = p_buf[:, (b * NE + i) % NP, :]
                                pool.wait_ge(exp_done, lin(g, b, NE, i + 1))
                                if kt == 1:
                                    first = isinstance(g, int) and (g, b) == (0, 0)
                                    if j == 0 and not first:
                                        pg, pb = (g, 0) if b == 1 else (g - 1, 1)
                                        pool.wait_ge(front_full, lin(pg, pb, NCH, 2 * NF + 2))
                                    prev = p_buf[:, (b * NE + i - G) % NP, :]
                                else:
                                    pool.wait_ge(added, lin(g, b, NADD, (kt - 2) * G + j + 1))
                                    prev = acc[:, j, :]
                                nc.gpsimd.tensor_tensor(acc[:, j, :], prev, cur, ALU.add).then_inc(added, 1)
                    walk(pool, lambda g, b: None, both, both)


GROUP = 4
NGRP = TT // GROUP


def project_norm(nc, name, src, rows, w_loads, bias, x, x_in, ln, hT, ident, out):
    with ExitStack() as ctx:
        def sb(n, shape, dt=F32):
            return ctx.enter_context(nc.sbuf_tensor(f"{name}_{n}", shape, dt))

        def sem(n, used=True):
            return ctx.enter_context(nc.semaphore(f"{name}_{n}")) if used else None

        KN = src.shape[1] if src is not None else 0
        wt = sb("w", [P, KN, D]) if KN else None
        bias_b = sb("bias", [P, D]) if KN else None
        stats = sb("stats", [P, 2, GROUP, 6])
        mv = sb("mean_var", [P, 2, GROUP, 2])
        ve = sb("var_eps", [P, 2, GROUP])
        sd = sb("deviation", [P, 2, GROUP])
        rs = sb("inverse", [P, 2, GROUP])
        hn = sb("normed", [P, 2, GROUP, D]) if ln else None
        lns = sb("ln", [P, 2, KD]) if ln else None
        prod = [ctx.enter_context(nc.psum_tensor(f"{name}_prod{i}", [P, GROUP, D], F32)) for i in range(2)]
        turned = [ctx.enter_context(nc.psum_tensor(f"{name}_turned{i}", [P, KD, HALF], F32)) for i in range(2)]

        loaded = sem("loaded")
        x_ready = sem("x_ready", KN)
        prod_full = sem("prod_full", KN)
        summed = sem("summed", KN)
        stat = sem("stat")
        var_done = sem("var_done", ln)
        sd_done = sem("sd_done", ln)
        normed = sem("normed", ln)
        turn_full = sem("turn_full", ln)
        h_done = sem("h_done", ln)
        stored = sem("stored", out is not None)

        loads = []
        if x_in is not None:
            loads.append((x[:], x_in))
        if KN:
            loads += [(dst(wt), s) for dst, s in w_loads]
            loads.append((bias_b[:], bias.to_broadcast((P, D))))
        if ln:
            loads += [(lns[:, i, :], ln[i]) for i in range(2)]
        clear = KN and rows is not None

        def ahead(first, second):
            first(0)
            for i in range(1, NGRP):
                first(i)
                second(i - 1)
            second(NGRP - 1)

        with nc.Block() as block:
            @block.sync
            def _(sp):
                if clear:
                    sp.wait_ge(stat, 1)
                for dst, s in loads:
                    with nc.allow_non_contiguous_dma("small vectors"):
                        sp.dma_start(dst, s).then_inc(loaded, DMA)
                if out is not None:
                    for i in range(NGRP):
                        at = slice(i * GROUP, (i + 1) * GROUP)
                        sp.wait_ge(summed, i + 1)
                        sp.dma_start(out[:, at, :], x[:, at, :]).then_inc(stored, DMA)
                    sp.wait_ge(stored, NGRP * DMA)

            @block.gpsimd
            def _(pool):
                if KN:
                    pool.wait_ge(loaded, DMA * len(loads))
                    for i in range(NGRP):
                        at = slice(i * GROUP, (i + 1) * GROUP)
                        nc.gpsimd.tensor_tensor(x[:, at, :], x[:, at, :],
                                                bias_b[:].unsqueeze(1).to_broadcast((P, GROUP, D)),
                                                ALU.add).then_inc(x_ready, 1)

            @block.tensor
            def _(pe):
                def product(i):
                    if not KN:
                        return
                    if i == 0:
                        pe.wait_ge(loaded, DMA * len(loads))
                    if i >= 2:
                        pe.wait_ge(summed, i - 1)
                    for t in range(GROUP):
                        at = (i * GROUP + t) * P
                        for k in range(KN):
                            mm = pe.matmul(prod[i % 2][:, t, :], src[:, k, at:at + P], wt[:, k, :],
                                           start=(k == 0), stop=(k == KN - 1))
                    mm.then_inc(prod_full, 1)

                def turn(i):
                    if not ln:
                        return
                    pe.wait_ge(normed, i + 1)
                    if i >= 2:
                        pe.wait_ge(h_done, i - 1)
                    for k in range(KD):
                        for t in range(GROUP):
                            mm = pe.transpose(turned[i % 2][:, k, t * P:(t + 1) * P],
                                              hn[:, i % 2, t, k * P:(k + 1) * P], ident[:])
                    mm.then_inc(turn_full, 1)

                ahead(product, turn)

            @block.vector
            def _(dve):
                step = Step(stat)
                if clear:
                    step(dve.memset(wt[:], 0.0))

                def stats_of(i):
                    at = slice(i * GROUP, (i + 1) * GROUP)
                    u = i % 2
                    if KN:
                        dve.wait_ge(x_ready, i + 1)
                        dve.wait_ge(prod_full, i + 1)
                        dve.tensor_tensor(x[:, at, :], prod[u][:], x[:, at, :], ALU.add).then_inc(summed, 1)
                        dve.wait_ge(summed, i + 1)
                    elif i == 0:
                        dve.wait_ge(loaded, DMA * len(loads))
                    if not ln:
                        return
                    for t in range(GROUP):
                        ins = dve.bn_stats(stats[:, u, t, :], x[:, i * GROUP + t, :])
                    step(ins)
                    step.wait(dve)
                    for t in range(GROUP):
                        ins = dve.bn_aggr(mv[:, u, t, :], stats[:, u, t, :])
                    step(ins)
                    step.wait(dve)
                    dve.tensor_scalar(ve[:, u, :], mv[:, u, :, 1], EPS, None, ALU.add).then_inc(var_done, 1)

                def normalise(i):
                    if not ln:
                        return
                    u = i % 2
                    dve.wait_ge(sd_done, i + 1)
                    step(dve.reciprocal(rs[:, u, :], sd[:, u, :]))
                    step.wait(dve)
                    if i >= 2:
                        dve.wait_ge(turn_full, i - 1)
                    for t in range(GROUP):
                        ins = dve.tensor_scalar(hn[:, u, t, :], x[:, i * GROUP + t, :], mv[:, u, t, 0:1],
                                                rs[:, u, t:t + 1], ALU.subtract, ALU.mult)
                    ins.then_inc(normed, 1)

                ahead(stats_of, normalise)

            @block.scalar
            def _(act):
                def root(i):
                    if ln:
                        act.wait_ge(var_done, i + 1)
                        nc.scalar.activation(sd[:, i % 2, :], ve[:, i % 2, :], ACT.Sqrt).then_inc(sd_done, 1)

                def evacuate(i):
                    if ln:
                        act.wait_ge(turn_full, i + 1)
                        for k in range(KD):
                            ins = nc.scalar.activation(hT[:, k, i * HALF:(i + 1) * HALF], turned[i % 2][:, k, :],
                                                       ACT.Identity, scale=lns[:, 0, k:k + 1],
                                                       bias=lns[:, 1, k:k + 1])
                        ins.then_inc(h_done, 1)

                ahead(root, evacuate)


def hidden_layer(nc, name, hT, w1, b1, gated, hid):
    FF = 4 * D
    MT = FF // P
    NC4 = NT // HALF
    with ExitStack() as ctx:
        def sem(n):
            return ctx.enter_context(nc.semaphore(f"{name}_{n}"))

        NB = 2 if gated else 1
        w = ctx.enter_context(nc.sbuf_tensor(f"{name}_w1", [P, 2, NB, KD, P], F32))
        bb = ctx.enter_context(nc.sbuf_tensor(f"{name}_b1", [P, 2, NB], F32))
        gate = ctx.enter_context(nc.sbuf_tensor(f"{name}_gate", [P, NC4, HALF], F32)) if gated else None
        banks = [ctx.enter_context(nc.psum_tensor(f"{name}_ps{i}", [P, HALF], F32)) for i in range(8)]
        loaded = [sem(f"loaded{u}") for u in range(2)]
        g_full = sem("g_full")
        a_full = sem("a_full")
        gelu = sem("gelu")
        done = sem("done")
        last = done if gated else gelu

        def bank(u, c, n):
            return banks[4 * n + c] if gated else banks[4 * u + c]

        def walk(eng, tile):
            for u in range(2):
                tile(0, u)
            with eng.Fori(1, MT // 2, 1) as i:
                for u in range(2):
                    tile(i, u)

        def ready(eng, s, mt, k):
            if not isinstance(mt, int) or 4 * mt + k > 0:
                eng.wait_ge(s, mt * NC4 + k)

        with nc.Block() as block:
            @block.sync
            def _(sp):
                def load(mt, u):
                    for n in range(NB):
                        col = mt * P + ((1 - n) * FF if gated else 0)
                        with nc.allow_non_contiguous_dma("bias column"):
                            sp.dma_start(w[:, u, n], w1[:, :, bass.ds(col, P)]).then_inc(loaded[u], DMA)
                            sp.dma_start(bb[:, u, n:n + 1], b1[bass.ds(col, P), :]).then_inc(loaded[u], DMA)

                load(0, 0)
                load(1, 1)
                with sp.Fori(1, MT // 2, 1) as i:
                    for u in range(2):
                        sp.wait_ge(last, i * (2 * NC4) + (u - 1) * NC4)
                        load(i * 2 + u, u)

            @block.tensor
            def _(pe):
                def tile(i, u):
                    mt = i * 2 + u
                    pe.wait_ge(loaded[u], (i + 1) * (2 * NB * DMA))
                    for c in range(NC4):
                        for n in range(NB):
                            if gated:
                                ready(pe, gelu if n == 0 else done, mt, c - NC4 + 1)
                            else:
                                ready(pe, gelu, mt, c - 2 * NC4 + 1)
                            for k in range(KD):
                                mm = pe.matmul(bank(u, c, n)[:], w[:, u, n, k, :], hT[:, k, c * HALF:(c + 1) * HALF],
                                               start=(k == 0), stop=(k == KD - 1))
                            mm.then_inc(a_full if n else g_full, 1)
                walk(pe, tile)

            @block.scalar
            def _(act):
                def tile(i, u):
                    mt = i * 2 + u
                    for c in range(NC4):
                        act.wait_ge(g_full, mt * NC4 + (c + 1))
                        if gated:
                            ready(act, done, mt, c - NC4 + 1)
                            dst = gate[:, c, :]
                        else:
                            dst = hid[:, bass.ds(mt, 1), c * HALF:(c + 1) * HALF].squeeze(1) \
                                if not isinstance(mt, int) else hid[:, mt, c * HALF:(c + 1) * HALF]
                        nc.scalar.activation(dst, bank(u, c, 0)[:], ACT.Gelu, bias=bb[:, u, 0:1]).then_inc(gelu, 1)
                walk(act, tile)

            if gated:
                @block.vector
                def _(dve):
                    def tile(i, u):
                        mt = i * 2 + u
                        for c in range(NC4):
                            dve.wait_ge(a_full, mt * NC4 + (c + 1))
                            dve.wait_ge(gelu, mt * NC4 + (c + 1))
                            dst = hid[:, bass.ds(mt, 1), c * HALF:(c + 1) * HALF].squeeze(1) \
                                if not isinstance(mt, int) else hid[:, mt, c * HALF:(c + 1) * HALF]
                            dve.scalar_tensor_tensor(out=dst, in0=bank(u, c, 1)[:], scalar=bb[:, u, 1:2],
                                                     in1=gate[:, c, :], op0=ALU.add, op1=ALU.mult).then_inc(done, 1)
                    walk(dve, tile)


def constants(nc, a, ident, ones, ctxT, key_mask, ctx_bias, pad_bias, ctx_low):
    with ExitStack() as ctx:
        def sb(n, shape, dt=F32):
            return ctx.enter_context(nc.sbuf_tensor(f"const_{n}", shape, dt))

        def sem(n):
            return ctx.enter_context(nc.semaphore(f"const_{n}"))

        c_in = sb("ctx", [P, B, DC])
        m_in = sb("mask", [P, B, QT], U8)
        e_in = sb("emask", [P, B], U8)
        r_in = sb("rmask", [P, B, TC], U8)
        ps = [ctx.enter_context(nc.psum_tensor(f"const_ps{i}", [P, HALF], F32)) for i in range(B)]
        loaded = sem("loaded")
        made = sem("made")
        step_sem = sem("step")
        turned = sem("turned")
        with nc.Block() as block:
            @block.sync
            def _(sp):
                with nc.allow_non_contiguous_dma("masks, once"):
                    sp.dma_start(c_in[0:TC], a["ctx_768"].rearrange("b t c -> t b c")).then_inc(loaded, DMA)
                    for b in range(B):
                        sp.dma_start(m_in[:, b, :], a["mask_BxS_bf0"][b].rearrange("(t p) -> p t", p=P)).then_inc(loaded, DMA)
                        sp.dma_start(e_in[0:TC, b:b + 1], a["mask_BxS2_bf0"][b].rearrange("(p o) -> p o", o=1)).then_inc(loaded, DMA)
                        sp.dma_start(r_in[:, b, :], a["mask_BxS2_bf0"][b:b + 1, :].to_broadcast((P, TC))).then_inc(loaded, DMA)
                    sp.wait_ge(loaded, DMA * 7)

            @block.gpsimd
            def _(pool):
                pool.memset(ones[:], 1.0)
                pool.memset(ident[:], 0.0).then_inc(made, 1)
                pool.wait_ge(made, 1)
                nc.gpsimd.affine_select(out=ident[:], in_=ident[:], compare_op=ALU.not_equal, fill=1.0, base=0,
                                        pattern=[[-1, P]], channel_multiplier=1).then_inc(made, 1)

            @block.tensor
            def _(pe):
                pe.wait_ge(loaded, DMA * 7)
                pe.wait_ge(made, 2)
                for b in range(B):
                    for k in range(KC):
                        mm = pe.transpose(ps[b][0:CW, k * P:k * P + TC], c_in[0:TC, b, k * CW:(k + 1) * CW],
                                          ident[0:TC, 0:TC])
                    mm.then_inc(turned, 1)

            @block.vector
            def _(dve):
                step = Step(step_sem)
                step(dve.memset(ctx_bias[:], LOW))
                step(dve.memset(pad_bias[:], LOW))
                step.wait(dve)
                dve.memset(pad_bias[0:TC, :], 0.0)
                dve.wait_ge(loaded, DMA * 7)
                dve.tensor_scalar(key_mask[:], m_in[:], -3e38, 3e38, ALU.mult, ALU.mult)
                dve.tensor_scalar(ctx_bias[0:TC, :], e_in[0:TC, :], -3e38, 3e38, ALU.mult, ALU.mult)
                dve.tensor_scalar(ctx_low[:], r_in[:], LOW, None, ALU.mult)
                for b in range(B):
                    dve.wait_ge(turned, b + 1)
                    for k in range(KC):
                        dve.tensor_copy(ctxT[0:CW, b, k, 0:TC], ps[b][0:CW, k * P:k * P + TC])


LOW_AT = [P * qt * (qt + 1) // 2 for qt in range(QT + 1)]


def causal_masks(nc, mask, low):
    with ExitStack() as ctx:
        rows = ctx.enter_context(nc.sbuf_tensor("low_rows", [P, B, T], U8))
        loaded = ctx.enter_context(nc.semaphore("low_loaded"))
        keys = ctx.enter_context(nc.semaphore("low_keys"))
        done = ctx.enter_context(nc.semaphore("low_done"))
        with nc.Block() as block:
            @block.sync
            def _(sp):
                for b in range(B):
                    sp.dma_start(rows[:, b, :], mask[b:b + 1, :].to_broadcast((P, T))).then_inc(loaded, DMA)

            @block.vector
            def _(dve):
                dve.wait_ge(loaded, DMA * B)
                for b in range(B):
                    for qt in range(QT):
                        dve.tensor_scalar(low[:, b, LOW_AT[qt]:LOW_AT[qt + 1]], rows[:, b, 0:(qt + 1) * P], LOW, None,
                                          ALU.mult).then_inc(keys, 1)

            @block.gpsimd
            def _(pool):
                for b in range(B):
                    for qt in range(QT):
                        pool.wait_ge(keys, b * QT + qt + 1)
                        blk = low[:, b, LOW_AT[qt + 1] - P:LOW_AT[qt + 1]]
                        nc.gpsimd.affine_select(out=blk, in_=blk, compare_op=ALU.is_ge, fill=LOW, base=0,
                                                pattern=[[-1, P]], channel_multiplier=1).then_inc(done, 1)
                pool.wait_ge(done, B * QT)


def decoder_blocks(nc, a, out):
    L0 = {k[len("L0_xattn_"):]: v for k, v in a.items() if k.startswith("L0_")}
    L1 = {k[len("L1_xattn_"):]: v for k, v in a.items() if k.startswith("L1_")}

    def by_rows(ap, p=P):
        return ap.rearrange("(k p) n -> p k n", p=p)

    def column(ap):
        return ap.rearrange("(n o) -> n o", o=1)

    def row(ap):
        return ap.rearrange("(o n) -> o n", o=1)

    def ln(g, b):
        return [v.rearrange("(k p) -> p k", p=P) for v in (g, b)]

    x_dram = a["x"].rearrange("b t d -> (b t) d").rearrange("(t p) d -> p t d", p=P)
    out_dram = out.rearrange("b t d -> (b t) d").rearrange("(t p) d -> p t d", p=P)

    with ExitStack() as ctx:
        def keep(n, shape, dt=F32):
            return ctx.enter_context(nc.sbuf_tensor(n, shape, dt))

        def scoped(n, shape, dt=F32):
            return nc.sbuf_tensor(n, shape, dt)

        ident, ones = keep("ident", [P, P]), keep("ones", [P, 64])
        ctxT = keep("ctxT", [P, B, KC, TC + 1])
        key_mask = keep("key_mask", [P, B, QT])
        ctx_bias, pad_bias = keep("ctx_bias", [P, B]), keep("pad_bias", [P, 1])
        ctx_low = keep("ctx_low", [P, B, TC])
        hT = keep("hT", [P, KD, NT])

        constants(nc, a, ident, ones, ctxT, key_mask, ctx_bias, pad_bias, ctx_low)
        x = keep("x", [P, TT, D])
        project_norm(nc, "ln01", None, None, None, None, x, x_dram, ln(L0["ln1_g"], L0["ln1_b"]), hT, ident, None)

        wide = {"G": 2, "dh": 64, "causal": False, "biased": False}
        NG = HEADS // 2
        with scoped("o0", [P, NG, NT]) as oT:
            attention(nc, "sa0", {**wide, "cross": False}, hT, ctxT, ident, ones,
                      {"q": by_rows(L0["sa_wq"]), "k": by_rows(L0["sa_wk"]), "v": by_rows(L0["sa_wv"]),
                       "key_bias": lambda b, kt: 0.0}, oT, spare=x)
            project_norm(nc, "po0", oT, None, [(lambda wt: wt[:], by_rows(L0["sa_wo"]))], row(L0["sa_bo"]), x, x_dram,
                         ln(L0["ln2_g"], L0["ln2_b"]), hT, ident, None)
            attention(nc, "ca0", {**wide, "cross": True}, hT, ctxT, ident, ones,
                      {"q": by_rows(L0["ca_wq"]), "k": by_rows(L0["ca_wk"], CW), "v": by_rows(L0["ca_wv"], CW),
                       "key_bias": lambda b, kt: pad_bias[:, 0:1]}, oT)
            project_norm(nc, "pc0", oT, None, [(lambda wt: wt[:], by_rows(L0["ca_wo"]))], row(L0["ca_bo"]), x, None,
                         ln(L0["ln3_g"], L0["ln3_b"]), hT, ident, None)
            hidden_layer(nc, "ff0", hT, by_rows(L0["ff_w1"]), column(L0["ff_b1"]), True, oT)
            project_norm(nc, "pf0", oT, None, [(lambda wt: wt[:], by_rows(L0["ff_w2"]))], row(L0["ff_b2"]), x, None,
                         ln(L1["ln1_w"], L1["ln1_b"]), hT, ident, None)

        thin = {"G": 4, "dh": 16, "biased": True}
        NG = HEADS // 4

        def padded(ap):
            v = ap.rearrange("(g j d) n -> j d g n", g=NG, j=4)
            return [((lambda wt, j=j: wt[32 * j:32 * j + 16, :, :]), v[j]) for j in range(4)]

        with scoped("o1", [P, NG, NT]) as oT:
            with scoped("low", [P, B, LOW_AT[QT]], BF16) as low:
                causal_masks(nc, a["mask_BxS_bf0"], low)
                attention(nc, "sa1", {**thin, "cross": False, "causal": True}, hT, ctxT, ident, ones,
                          {"q": by_rows(L1["qkv_w"]), "bq": column(L1["qkv_b"]),
                           "bv": row(L1["qkv_b"])[:, 2 * D:3 * D],
                           "key_bias": lambda b, kt: key_mask[:, b, kt:kt + 1],
                           "key_low": lambda b, qt, k0, n: low[:, b, LOW_AT[qt] + k0:LOW_AT[qt] + k0 + n]}, oT)
            project_norm(nc, "po1", oT, 1, padded(L1["proj_w"]), row(L1["proj_b"]), x, None,
                         ln(L1["ln2_w"], L1["ln2_b"]), hT, ident, None)
            attention(nc, "ca1", {**thin, "cross": True, "causal": False}, hT, ctxT, ident, ones,
                      {"q": by_rows(L1["q_w"]), "k": by_rows(L1["k_w"], CW), "v": by_rows(L1["v_w"], CW),
                       "bq": column(L1["q_b"]), "bk": column(L1["k_b"]), "bv": row(L1["v_b"]),
                       "key_bias": lambda b, kt: ctx_bias[:, b:b + 1],
                       "key_low": lambda b: ctx_low[:, b, :]}, oT)
            project_norm(nc, "pc1", oT, 1, padded(L1["out_w"]), row(L1["out_b"]), x, None,
                         ln(L1["ln3_w"], L1["ln3_b"]), hT, ident, None)
        with scoped("hid1", [P, 4 * D // P, NT]) as hid:
            hidden_layer(nc, "ff1", hT, by_rows(L1["mlp1_w"]), column(L1["mlp1_b"]), False, hid)
            project_norm(nc, "pf1", hid, None, [(lambda wt: wt[:], by_rows(L1["mlp2_w"]))], row(L1["mlp2_b"]), x, None,
                         None, hT, ident, out_dram)


def kernel(**inputs):
    import numpy as np
    import concourse.bacc as bacc
    from concourse.bass_utils import run_bass_kernel_spmd

    nc = bacc.Bacc("TRN2", target_bir_lowering=False, num_devices=1)
    arrays, aps = {}, {}
    for name, value in inputs.items():
        v = np.ascontiguousarray(value)
        arrays[f"in_{name}"] = v
        aps[name] = nc.dram_tensor(f"in_{name}", v.shape, mybir.dt.from_np(v.dtype), kind="ExternalInput").ap()
    out = nc.dram_tensor("out", (B, T, D), F32, kind="ExternalOutput").ap()
    decoder_blocks(nc, aps, out)
    r = run_bass_kernel_spmd(nc, [arrays], core_ids=[0])
    return r.results[0]["out"]
```

```python
from contextlib import ExitStack

import concourse.bass as bass
from concourse import mybir

F32 = mybir.dt.float32
F32R = mybir.dt.float32r
BF16 = mybir.dt.bfloat16
U8 = mybir.dt.uint8
ALU = mybir.AluOpType
ACT = mybir.ActivationFunctionType
AX = mybir.AxisListType

P = 128
B, T, D = 2, 1024, 256
TC, DC = 77, 192
NT = B * T
TT = NT // P
KD = D // P
KC, CW = 2, DC // 2
HEADS = 16
EPS = 1e-5
LOW = -1e30
HALF = 512
DMA = 16
QT = T // P


def lin(g, b, per, k):
    return g * (2 * per) + (b * per + k)


class Step:

    def __init__(self, sem, n=0):
        self.sem, self.n = sem, n

    def __call__(self, ins):
        self.n += 1
        return ins.then_inc(self.sem, 1)

    def wait(self, eng):
        eng.wait_ge(self.sem, self.n)


def attention(nc, name, cfg, hT, ctxT, ident, ones, w, oT, spare=None):
    G, dh, causal, cross, biased = cfg["G"], cfg["dh"], cfg["causal"], cfg["cross"], cfg["biased"]
    wide = dh == 64
    NG = HEADS // G
    GD = G * dh
    KT = 1 if cross else T // P
    KW = P if cross else T
    NK = TC if cross else T
    NQ = 2 if wide else 1
    MROW = 64 if wide else 96
    KMAX = P if wide else 96
    VW = P // G
    SCALE = float(dh) ** -0.5
    NE = G * KT
    NP = 2 * G
    NADD = G * (KT - 2) if wide and KT > 1 else 0
    joint = not wide and not cross

    proj = [("qk", c) for c in range(2)] if joint else [("q", c) for c in range(2)] + (
        [("k", 0)] if cross else [("k", c) for c in range(2)])
    vs = [("v", c) for c in range(1 if cross or not wide else 2)]
    if cross:
        maxes = [("m", j, 4 * c, 0, TC) for j in range(G) for c in range(2)]
    elif causal:
        maxes = [("m", j, qt, h, min(HALF, (qt + 1) * P - h * HALF))
                 for j in range(G) for qt in range(QT) for h in range(2) if (qt + 1) * P > h * HALF]
    else:
        maxes = [("m", j, qt, h, HALF) for j in range(G) for qt in range(QT) for h in range(2)]
    items = proj + vs + maxes + [("t",)]
    NF = len(items)
    NDEN = 2 if wide else 0
    NCH = NF + NDEN
    IV = len(proj) + len(vs) - 1

    back = []
    for kt in range(KT):
        back += [("s", j, kt) for j in range(G)]
        if kt:
            back.append(("pv", kt - 1))
    back.append(("pv", KT - 1))

    def woven():
        nb = len(back)
        lead = len(proj) + len(vs)
        first_m = 2 if cross else min(6, nb - 2)
        last_m = nb - 2 if cross else nb - 5
        out, at = [], 0
        for i, piece in enumerate(back):
            out.append(("back", piece, None))
            if i < first_m:
                want = lead * (i + 1) // first_m
            elif i >= last_m:
                want = NF
            else:
                want = lead + len(maxes) * (i - first_m + 1) // max(1, last_m - first_m)
                want = min(want, NF - 1)
            while at < want:
                out.append(("front", items[at], at))
                at += 1
        return out

    WOVEN = woven()
    FRONT = [("front", it, i) for i, it in enumerate(items)]
    BACK = [("back", piece, None) for piece in back]

    def walk(eng, front, both, tail):
        front(0, 0)
        both(0, 0)
        both(0, 1)
        if NG > 4:
            with eng.Fori(1, NG - 1, 1) as g:
                both(g, 0)
                both(g, 1)
        else:
            for g in range(1, NG - 1):
                both(g, 0)
                both(g, 1)
        both(NG - 1, 0)
        tail(NG - 1, 1)

    def after(g, b):
        return (g, 1) if b == 0 else (g + 1, 0)

    def front_chunk(g, b, i):
        if isinstance(g, int) and (g, b) == (0, 0):
            return i
        return lin(g, b, NCH, NF - NCH + i)

    def den_chunk(g, b, c):
        last = isinstance(g, int) and (g, b) == (NG - 1, 1)
        return lin(g, b, NCH, NF + (0 if last else NF) + c)

    def front_bank(g, b, i):
        return i % 2 if isinstance(g, int) and (g, b) == (0, 0) else (b * NCH + NF - NCH + i) % 2

    def den_bank(g, b, c):
        last = isinstance(g, int) and (g, b) == (NG - 1, 1)
        return (b * NCH + NF + (0 if last else NF) + c) % 2

    def spans(kt):
        q0 = kt * P if causal else 0
        return [(max(q0, lo), lo + HALF) for lo in (0, HALF) if q0 < lo + HALF]

    with ExitStack() as ctx:
        def sb(n, shape, dt=F32):
            return ctx.enter_context(nc.sbuf_tensor(f"{name}_{n}", shape, dt))

        def ps(n, shape):
            return ctx.enter_context(nc.psum_tensor(f"{name}_{n}", shape, F32))

        def sem(n):
            return ctx.enter_context(nc.semaphore(f"{name}_{n}"))

        q_stage = sb("q_stage", [P, 2, G, NQ, T], F32R)
        k_stage = sb("k_stage", [P, 2, G, NQ, KW], F32R)
        v_buf = sb("v_buf", [P, 2, KT, P])
        q_hi, q_lo = sb("q_hi", [P, T], F32R), sb("q_lo", [P, T], F32R)
        if joint:
            k_hi, k_lo = q_hi, q_lo
        else:
            k_hi, k_lo = sb("k_hi", [P, KW], F32R), sb("k_lo", [P, KW], F32R)
        p_buf = sb("p_buf", [P, NP, T])
        if spare is None:
            acc, recip = None, sb("recip", [P, T])
        else:
            acc = spare[:].rearrange("p t d -> p (t d)")[:, 0:G * T].rearrange("p (g t) -> p g t", g=G)
            recip = spare[:].rearrange("p t d -> p (t d)")[:, G * T:(G + 1) * T]
        KDk = KC if cross else KD
        wq = sb("wq", [P, KD, P])
        wk = None if joint else sb("wk", [P, KDk, P])
        wv = sb("wv", [P, KDk, GD])
        bq = sb("bq", [P, 1]) if biased else None
        bk = sb("bk", [P, 1]) if biased and cross else None
        bv = sb("bv", [P, GD]) if biased else None
        mx = sb("mx", [P, 2, G, QT, 2])
        m_row = sb("m_row", [P, G, QT])
        m_hi = sb("m_hi", [P, G, QT], F32R)
        m_parts = sb("m_parts", [P, G, 2, QT])
        m_turned = sb("m_turned", [2 * G * QT, P], F32R)
        junk = sb("junk", [P, 2, HALF], BF16 if causal else F32) if biased else None

        front_ps = [ps(f"front{i}", [P, HALF]) for i in range(2)]
        score_ps = [ps(f"score{i}", [P, T]) for i in range(2)]
        out_ps = ps("out", [P, T])

        cleared = sem("cleared")
        w_in = sem("w_in")
        front_full = sem("front_full")
        hi_done = sem("hi_done")
        drained = sem("drained")
        stage_in = sem("stage_in")
        max_in = sem("max_in")
        m_step = sem("m_step")
        score_full = sem("score_full")
        exp_done = sem("exp_done")
        diag_done = sem("diag_done") if causal else None
        added = sem("added") if NADD else None
        pv_done = sem("pv_done")
        masked = sem("masked") if cross and biased else None
        norm = sem("norm")
        out_done = sem("out_done")

        w_dmas = []

        def cols(ap, g, width, start=0):
            return ap[:, :, bass.ds(g * width + start, width)]

        if joint:
            w_dmas.append((wq[:, :, 0:GD], lambda g: cols(w["q"], g, GD)))
            w_dmas.append((wq[:, :, GD:2 * GD], lambda g: cols(w["q"], g, GD, D)))
            w_dmas.append((wv[:], lambda g: cols(w["q"], g, GD, 2 * D)))
        elif cross:
            w_dmas.append((wq[:, :, 0:GD], lambda g: cols(w["q"], g, GD)))
            w_dmas.append((wk[0:CW, :, 0:GD], lambda g: cols(w["k"], g, GD)))
            w_dmas.append((wv[0:CW, :, :], lambda g: cols(w["v"], g, GD)))
        else:
            w_dmas.append((wq[:, :, 0:GD], lambda g: cols(w["q"], g, GD)))
            w_dmas.append((wk[:, :, 0:GD], lambda g: cols(w["k"], g, GD)))
            w_dmas.append((wv[:], lambda g: cols(w["v"], g, GD)))
        if biased:
            w_dmas.append((bq[0:GD, :], lambda g: w["bq"][bass.ds(g * GD, GD), :]))
            if joint:
                w_dmas.append((bq[GD:2 * GD, :], lambda g: w["bq"][bass.ds(g * GD + D, GD), :]))
            else:
                w_dmas.append((bk[0:GD, :], lambda g: w["bk"][bass.ds(g * GD, GD), :]))
            w_dmas.append((bv[:, :], lambda g: w["bv"][:, bass.ds(g * GD, GD)].to_broadcast((P, GD))))
        NW = len(w_dmas)

        def stage_dmas(b):
            out = []
            for j in range(G):
                r = slice(dh * j, dh * j + dh)
                if wide:
                    q, k = q_stage[:, b, j, :, :], k_stage[:, b, j, :, 0:NK]
                    out.append((q[0:64, 0, :], q_hi[r, :]))
                    out.append((q[0:64, 1, :], q_hi[r, :]))
                    out.append((q[64:128, 0, :], q_lo[r, :]))
                    out.append((k[0:64, 0, :], k_hi[r, 0:NK]))
                    out.append((k[64:128, 0, :], k_hi[r, 0:NK]))
                    out.append((k[0:64, 1, :], k_lo[r, 0:NK]))
                else:
                    q, k = q_stage[:, b, j, 0, :], k_stage[:, b, j, 0, 0:NK]
                    s = slice(dh * j + (GD if joint else 0), dh * j + dh + (GD if joint else 0))
                    for at, src in ((0, q_hi), (1, q_lo), (2, q_hi)):
                        out.append((q[16 * at:16 * at + 16, :], src[r, :]))
                    for at, src in ((0, k_hi), (1, k_hi), (2, k_lo)):
                        out.append((k[16 * at:16 * at + 16, :], src[s, 0:NK]))
            return out

        NS = len(stage_dmas(0))

        with nc.Block() as block:
            @block.sync
            def _(sp):
                def weights(g):
                    for dst, src in w_dmas:
                        sp.dma_start(dst, src(g)).then_inc(w_in, DMA)

                def front(g, b, load=None):
                    sp.wait_ge(drained, front_chunk(g, b, len(proj) - 1) + 1)
                    for dst, src in stage_dmas(b):
                        sp.dma_start(dst.bitcast(F32), src.bitcast(F32)).then_inc(stage_in, DMA)
                    if load is not None:
                        sp.wait_ge(drained, front_chunk(g, b, IV) + 1)
                        weights(load)
                    sp.wait_ge(drained, front_chunk(g, b, NF - 1) + 1)
                    for j in range(G):
                        for part in range(2):
                            r = (j * 2 + part) * QT
                            sp.dma_start(
                                q_stage[MROW + part:MROW + part + 1, b, j, NQ - 1, :].bitcast(F32),
                                m_turned[r:r + QT, :].bitcast(F32)).then_inc(max_in, DMA)

                def both(g, b):
                    g2, b2 = after(g, b)
                    last = isinstance(g2, int) and g2 == NG - 1
                    front(g2, b2, g2 + 1 if b2 == 1 and not last else None)

                weights(0)
                sp.wait_ge(cleared, 2)
                walk(sp, front, both, lambda g, b: None)

            @block.tensor
            def _(pe):
                def front_item(g, b, item, i):
                    kind = item[0]
                    c = front_chunk(g, b, i)
                    fr = front_ps[front_bank(g, b, i)]
                    if not isinstance(c, int) or c >= 2:
                        pe.wait_ge(drained, c - 1)
                    if kind in ("q", "qk") and item[1] == 0:
                        pe.wait_ge(w_in, (g + 1) * (DMA * NW))
                    if kind in ("q", "qk", "k"):
                        wt = wk if kind == "k" else wq
                        M = P if kind == "qk" else GD
                        if kind == "k" and cross:
                            for kd in range(KC):
                                mm = pe.matmul(fr[0:M, 0:TC], wt[0:CW, kd, 0:M], ctxT[0:CW, b, kd, 0:TC],
                                               start=(kd == 0), stop=(kd == KC - 1))
                        else:
                            at = b * T + item[1] * HALF
                            for kd in range(KD):
                                mm = pe.matmul(fr[0:M, :], wt[:, kd, 0:M], hT[:, kd, at:at + HALF],
                                               start=(kd == 0), stop=(kd == KD - 1))
                    elif kind == "v":
                        if cross:
                            for kd in range(KC):
                                mm = pe.matmul(fr[0:TC, 0:GD], ctxT[0:CW, b, kd, 0:TC], wv[0:CW, kd, :],
                                               start=(kd == 0), stop=(kd == KC - 1))
                        else:
                            n = HALF // GD
                            for t in range(n):
                                at = b * T + (item[1] * n + t) * P
                                for kd in range(KD):
                                    mm = pe.matmul(fr[:, t * GD:(t + 1) * GD], hT[:, kd, at:at + P], wv[:, kd, :],
                                                   start=(kd == 0), stop=(kd == KD - 1))
                    elif kind == "m":
                        _, j, qt, half, width = item
                        if (j, qt, half) == (0, 0, 0):
                            pe.wait_ge(stage_in, lin(g, b, DMA * NS, DMA * NS))
                        if cross:
                            for t in range(4):
                                q = q_stage[0:KMAX, b, j, 0, (qt + t) * P:(qt + t + 1) * P]
                                mm = pe.matmul(fr[:, t * 80:t * 80 + TC + 1], q, k_stage[0:KMAX, b, j, 0, 0:TC + 1],
                                               start=True, stop=True)
                        else:
                            q = q_stage[0:KMAX, b, j, 0, qt * P:(qt + 1) * P]
                            k = k_stage[0:KMAX, b, j, 0, half * HALF:half * HALF + width]
                            mm = pe.matmul(fr[:, 0:width], q, k, start=True, stop=True)
                    else:
                        pe.wait_ge(m_step, lin(g, b, 3, 3))
                        parts = m_parts[:].rearrange("p g s t -> p (g s t)")
                        mm = pe.transpose(fr[0:2 * G * QT, 0:P], parts, ident[:])
                    mm.then_inc(front_full, 1)

                def back_piece(g, b, piece):
                    first = isinstance(g, int) and (g, b) == (0, 0)
                    if piece[0] == "s":
                        _, j, kt = piece
                        i = kt * G + j
                        if i == 0:
                            pe.wait_ge(max_in, lin(g, b, DMA * 2 * G, DMA * 2 * G))
                        if not (first and i < 2):
                            pe.wait_ge(exp_done, lin(g, b, NE, i - 1))
                        dst = score_ps[i % 2]
                        for lo, hi in spans(kt):
                            for s in range(NQ):
                                mm = pe.matmul(dst[:, lo:hi], k_stage[:, b, j, s, kt * P:(kt + 1) * P],
                                               q_stage[:, b, j, s, lo:hi], start=(s == 0), stop=(s == NQ - 1))
                        mm.then_inc(score_full, 1)
                    else:
                        kt = piece[1]
                        if causal:
                            pe.wait_ge(diag_done, lin(g, b, NE, (kt + 1) * G))
                        else:
                            pe.wait_ge(exp_done, lin(g, b, NE, (kt + 1) * G))
                        if kt == 0 and not first:
                            pe.wait_ge(out_done, lin(g, b, 1, 0))
                        for lo, hi in spans(kt):
                            last = kt == KT - 1 or (causal and kt == 3 and lo < HALF)
                            for j in range(G):
                                e = (b * NE + kt * G + j) % NP
                                mm = pe.matmul(out_ps[VW * j:VW * j + VW, lo:hi],
                                               v_buf[:, b, kt, VW * j:VW * j + VW], p_buf[:, e, lo:hi],
                                               start=(kt == 0), stop=last, skip_group_check=True)
                        mm.then_inc(pv_done, 1)

                def denominators(g, b):
                    if not wide:
                        return
                    for c in range(2):
                        pe.wait_ge(drained, den_chunk(g, b, c) - 1)
                        if NADD and c == 0:
                            pe.wait_ge(added, lin(g, b, NADD, NADD))
                        fr = front_ps[den_bank(g, b, c)]
                        at = slice(c * HALF, (c + 1) * HALF)
                        for j in range(G):
                            e = (b * NE + (KT - 1) * G + j) % NP
                            if NADD:
                                pe.matmul(fr[64 * j:64 * j + 64, :], ones[:, 0:64], acc[:, j, at], start=True, stop=False)
                            mm = pe.matmul(fr[64 * j:64 * j + 64, :], ones[:, 0:64], p_buf[:, e, at],
                                           start=not NADD, stop=True)
                        mm.then_inc(front_full, 1)

                def front(g, b):
                    for _, it, i in FRONT:
                        front_item(g, b, it, i)

                def both(g, b):
                    for which, it, i in WOVEN:
                        if which == "back":
                            back_piece(g, b, it)
                        else:
                            front_item(*after(g, b), it, i)
                    denominators(g, b)

                def tail(g, b):
                    for _, it, _i in BACK:
                        back_piece(g, b, it)
                    denominators(g, b)

                pe.wait_ge(cleared, 2)
                walk(pe, front, both, tail)

            @block.scalar
            def _(act):
                def front_item(g, b, item, i):
                    if item[0] not in ("q", "k", "qk"):
                        return
                    c = front_chunk(g, b, i)
                    first = isinstance(g, int) and (g, b) == (0, 0)
                    if i == 0 and not first:
                        act.wait_ge(stage_in, lin(g, b, DMA * NS, 0))
                    act.wait_ge(front_full, c + 1)
                    fr = front_ps[front_bank(g, b, i)]
                    rows = P if item[0] == "qk" else GD
                    n = TC if (cross and item[0] == "k") else HALF
                    dst = (k_hi if item[0] == "k" else q_hi)[0:rows, item[1] * HALF:item[1] * HALF + n]
                    bias = (bk if item[0] == "k" else bq)[0:rows, 0:1] if biased else 0.0
                    nc.scalar.activation(dst, fr[0:rows, 0:n], ACT.Identity, bias=bias).then_inc(hi_done, 1)

                def back_piece(g, b, piece):
                    if piece[0] != "s":
                        return
                    _, j, kt = piece
                    first = isinstance(g, int) and (g, b) == (0, 0)
                    i = kt * G + j
                    e = (b * NE + i) % NP
                    act.wait_ge(score_full, lin(g, b, NE, i + 1))
                    second = first and kt < 2 or (isinstance(g, int) and KT == 1 and (g, b) == (0, 1))
                    if not second:
                        act.wait_ge(pv_done, lin(g, b, KT, kt - 1))
                        if NADD and kt >= 2:
                            act.wait_ge(added, lin(g, b, NADD, (max(kt - 2, 1) - 1) * G + j + 1))
                        elif wide and (kt == 1 or KT == 1):
                            back_n = 1 if KT > 1 else 2
                            pg, pb = (g, 0) if b == 1 and back_n == 1 else (g - 1, b if back_n == 2 else 1)
                            act.wait_ge(front_full, lin(pg, pb, NCH, 2 * NF + 2))
                        elif NADD:
                            act.wait_ge(added, lin(g, b, NADD, 0))
                    q0 = kt * P if causal else 0
                    bias = w["key_bias"](b, kt)
                    nc.scalar.activation(p_buf[:, e, q0:T], score_ps[i % 2][:, q0:T], ACT.Exp, bias=bias,
                                         scale=SCALE).then_inc(exp_done, 1)

                def front(g, b):
                    for _, it, i in FRONT:
                        front_item(g, b, it, i)

                def both(g, b):
                    for which, it, i in WOVEN:
                        if which == "back":
                            back_piece(g, b, it)
                        else:
                            front_item(*after(g, b), it, i)

                def tail(g, b):
                    for _, it, _i in BACK:
                        back_piece(g, b, it)

                walk(act, front, both, tail)

            @block.vector
            def _(dve):
                kb = k_stage[:].bitcast(F32)
                r0 = MROW if wide and not cross else 0
                dve.memset(kb[r0:P, :, :, NQ - 1, :] if r0 else kb, 0.0).then_inc(norm, 1)
                dve.memset(v_buf[:], 1.0)
                dve.memset(mx[:], 4.0 * LOW)
                dve.wait_ge(norm, 1)
                dve.memset(kb[MROW:MROW + 2, :, :, NQ - 1, :], 1.0).then_inc(cleared, 1)

                def front_item(g, b, item, i):
                    kind = item[0]
                    c = front_chunk(g, b, i)
                    fr = front_ps[front_bank(g, b, i)]
                    first = isinstance(g, int) and (g, b) == (0, 0)
                    if kind in ("q", "k", "qk"):
                        rows = P if kind == "qk" else GD
                        n = TC if (cross and kind == "k") else HALF
                        at = slice(item[1] * HALF, item[1] * HALF + n)
                        hi, lo = (k_hi, k_lo) if kind == "k" else (q_hi, q_lo)
                        if i == 0 and not first:
                            dve.wait_ge(stage_in, lin(g, b, DMA * NS, 0))
                        dve.wait_ge(hi_done, lin(g, b, len(proj), i + 1))
                        if biased:
                            bias = (bk if kind == "k" else bq)[0:rows, 0:1]
                            ins = dve.scalar_tensor_tensor(out=lo[0:rows, at], in0=fr[0:rows, 0:n], scalar=bias,
                                                           in1=hi[0:rows, at].bitcast(F32), op0=ALU.add,
                                                           op1=ALU.subtract)
                        else:
                            ins = dve.tensor_tensor(lo[0:rows, at], fr[0:rows, 0:n], hi[0:rows, at].bitcast(F32),
                                                    ALU.subtract)
                        ins.then_inc(drained, 1)
                    elif kind == "v":
                        dve.wait_ge(front_full, c + 1)
                        rows = TC if cross else P
                        n = KT if cross else HALF // GD
                        src = fr[0:rows, 0:n * GD].rearrange("p (t j d) -> p t j d", t=n, j=G)
                        dst = v_buf[0:rows, b, item[1] * n:item[1] * n + n, :].rearrange("p t (j d) -> p t j d", j=G)
                        if n == 1:
                            src, dst = src[:, 0], dst[:, 0]
                        if biased:
                            bb = bv[0:rows, :].rearrange("p (j d) -> p j d", j=G)
                            if n > 1:
                                bb = bb.unsqueeze(1).to_broadcast((rows, n, G, dh))
                                ins = dve.tensor_tensor(dst[:, :, :, 0:dh], src, bb, ALU.add)
                            else:
                                ins = dve.tensor_tensor(dst[:, :, 0:dh], src, bb, ALU.add)
                        else:
                            ins = dve.tensor_copy(dst, src)
                        ins.then_inc(drained, 1)
                    elif kind == "m":
                        _, j, qt, half, width = item
                        dve.wait_ge(front_full, c + 1)
                        if cross:
                            src = fr[:, 0:320].rearrange("p (t k) -> p t k", k=80)[:, :, 0:TC]
                            if biased:
                                dve.wait_ge(drained, c - 1)
                                tmp = junk[:, c % 2, 0:4 * 80].rearrange("p (t k) -> p t k", k=80)[:, :, 0:TC]
                                dve.tensor_tensor(tmp, src, w["key_low"](b).unsqueeze(1).to_broadcast((P, 4, TC)),
                                                  ALU.add).then_inc(masked, 1)
                                dve.wait_ge(masked, lin(g, b, len(maxes), i - IV))
                                src = tmp
                            dve.tensor_reduce(mx[:, b, j, qt:qt + 4, 0], src, AX.X, ALU.max).then_inc(drained, 1)
                        elif causal:
                            low = w["key_low"](b, qt, half * HALF, width)
                            dve.wait_ge(drained, c - 1)
                            dve.tensor_tensor_reduce(junk[:, c % 2, 0:width], fr[:, 0:width], low, 1.0, 16.0 * LOW, ALU.add,
                                                     ALU.max, mx[:, b, j, qt, half:half + 1]).then_inc(drained, 1)
                        else:
                            dve.tensor_reduce(mx[:, b, j, qt, half:half + 1], fr[:, 0:width], AX.X,
                                              ALU.max).then_inc(drained, 1)
                    else:
                        dve.wait_ge(drained, c)
                        dve.tensor_tensor(m_row[:], mx[:, b, :, :, 0], mx[:, b, :, :, 1], ALU.max).then_inc(m_step, 1)
                        dve.wait_ge(m_step, lin(g, b, 3, 1))
                        dve.tensor_scalar(m_hi[:], m_row[:], -1.0, None, ALU.mult).then_inc(m_step, 1)
                        dve.wait_ge(m_step, lin(g, b, 3, 2))
                        dve.tensor_copy(m_parts[:, :, 0, :], m_hi[:].bitcast(F32))
                        dve.scalar_tensor_tensor(out=m_parts[:, :, 1, :], in0=m_row[:], scalar=-1.0,
                                                 in1=m_hi[:].bitcast(F32), op0=ALU.mult,
                                                 op1=ALU.subtract).then_inc(m_step, 1)
                        if not first:
                            dve.wait_ge(max_in, lin(g, b, DMA * 2 * G, 0))
                        dve.wait_ge(front_full, c + 1)
                        dve.tensor_copy(m_turned[:], fr[0:2 * G * QT, 0:P]).then_inc(drained, 1)

                def finish(g, b):
                    dst = oT[:, bass.ds(g, 1), b * T:(b + 1) * T] if not isinstance(g, int) else oT[:, g:g + 1, b * T:(b + 1) * T]
                    if wide:
                        for c in range(2):
                            at = slice(c * HALF, (c + 1) * HALF)
                            k = den_chunk(g, b, c)
                            dve.wait_ge(front_full, k + 1)
                            dve.reciprocal(recip[:, at], front_ps[den_bank(g, b, c)][:, :]).then_inc(drained, 1)
                        dve.wait_ge(drained, den_chunk(g, b, 1) + 1)
                        dve.wait_ge(pv_done, lin(g, b, KT, KT))
                        dve.tensor_tensor(dst[:, 0], out_ps[:], recip[:], ALU.mult).then_inc(out_done, 1)
                    else:
                        dve.wait_ge(pv_done, lin(g, b, KT, KT))
                        dve.reciprocal(recip[:], out_ps[:]).then_inc(norm, 1)
                        dve.wait_ge(norm, lin(g, b, 2, 2))
                        dve.stream_shuffle(recip[:], recip[:], [dh] * 32).then_inc(norm, 1)
                        dve.wait_ge(norm, lin(g, b, 2, 3))
                        dve.tensor_tensor(dst[:, 0], out_ps[:], recip[:], ALU.mult).then_inc(out_done, 1)

                def front(g, b):
                    for _, it, i in FRONT:
                        front_item(g, b, it, i)

                def both(g, b):
                    for which, it, i in WOVEN:
                        if which == "front":
                            front_item(*after(g, b), it, i)
                    finish(g, b)

                walk(dve, front, both, finish)

            @block.gpsimd
            def _(pool):
                qb = q_stage[:].bitcast(F32)
                if wide:
                    pool.memset(qb[64:P, :, :, 1, :], 0.0).then_inc(cleared, 1)
                else:
                    pool.memset(qb, 0.0).then_inc(cleared, 1)
                if causal:
                    def both(g, b):
                        for kt in range(KT):
                            for j in range(G):
                                i = kt * G + j
                                blk = p_buf[:, (b * NE + i) % NP, kt * P:(kt + 1) * P]
                                pool.wait_ge(exp_done, lin(g, b, NE, i + 1))
                                nc.gpsimd.affine_select(out=blk, in_=blk, compare_op=ALU.is_ge, fill=0.0, base=0,
                                                        pattern=[[1, P]], channel_multiplier=-1).then_inc(diag_done, 1)
                    walk(pool, lambda g, b: None, both, both)
                elif NADD:
                    def both(g, b):
                        for kt in range(1, KT - 1):
                            for j in range(G):
                                i = kt * G + j
                                cur = p_buf[:, (b * NE + i) % NP, :]
                                pool.wait_ge(exp_done, lin(g, b, NE, i + 1))
                                if kt == 1:
                                    first = isinstance(g, int) and (g, b) == (0, 0)
                                    if j == 0 and not first:
                                        pg, pb = (g, 0) if b == 1 else (g - 1, 1)
                                        pool.wait_ge(front_full, lin(pg, pb, NCH, 2 * NF + 2))
                                    prev = p_buf[:, (b * NE + i - G) % NP, :]
                                else:
                                    pool.wait_ge(added, lin(g, b, NADD, (kt - 2) * G + j + 1))
                                    prev = acc[:, j, :]
                                nc.gpsimd.tensor_tensor(acc[:, j, :], prev, cur, ALU.add).then_inc(added, 1)
                    walk(pool, lambda g, b: None, both, both)


def cross_attention(nc, name, cfg, hT, ctxT, ident, w, oT):
    dh, biased = cfg["dh"], cfg["biased"]
    wide = dh == 64
    HR = P // dh
    QG = HEADS // HR
    PAIRS, CH = HEADS // 2, NT // HALF
    VW = 64 if wide else 32
    ROUNDS, SR = (PAIRS, CH) if wide else (CH, PAIRS)
    PQ = 1 if wide else HR // 2
    TQ = HALF // P
    U = 2 * TQ
    SCALE = float(dh) ** -0.5
    LAST = ROUNDS * SR

    def at(n):
        g, s = n
        return g + s // SR, s % SR

    def exists(n):
        g, s = at(n)
        return not isinstance(g, int) or 0 <= g < ROUNDS

    def chunk(n):
        g, s = at(n)
        return s if wide else g

    def pair(n):
        g, s = at(n)
        return g if wide else s

    def wait(eng, sem, n, k, per=1):
        g, s = n
        if isinstance(g, int):
            v = ((g * SR + s) + k) // per if per > 1 else g * SR + s + k
            if v > 0:
                eng.wait_ge(sem, v)
        else:
            assert per == 1
            eng.wait_ge(sem, g * SR + (s + k))

    def q_first(n):
        return at(n)[1] % PQ == 0

    def run(eng, slot):
        for s in range(-3, SR):
            slot((0, s))
        if wide:
            with eng.Fori(1, ROUNDS - 1, 1) as g:
                for s in range(SR):
                    slot((g, s))
        else:
            for g in range(1, ROUNDS - 1):
                for s in range(SR):
                    slot((g, s))
        for s in range(SR + 1):
            slot((ROUNDS - 1, s))

    def ahead(n, k):
        return (n[0], n[1] + k)

    with ExitStack() as ctx:
        def sb(n, shape, dt=F32):
            return ctx.enter_context(nc.sbuf_tensor(f"{name}_{n}", shape, dt))

        def sem(n):
            return ctx.enter_context(nc.semaphore(f"{name}_{n}"))

        keys = sb("keys", [P, QG, HR, B, TC])
        v_all = sb("v_all", [P, PAIRS, B, 2, VW])
        w_in = sem("w_in")
        k_full = sem("k_full")
        k_out = sem("k_out")
        k_set = sem("k_set")
        v_full = sem("v_full")
        made = sem("made")
        cleared = sem("cleared")
        v_set = sem("v_set")

        with ExitStack() as ctx2:
            def sb2(n, shape, dt=F32):
                return ctx2.enter_context(nc.sbuf_tensor(f"{name}_{n}", shape, dt))

            DA = HEADS * dh
            wk, wv = sb2("wk", [P, KC, DA]), sb2("wv", [P, KC, DA])
            bk = sb2("bk", [P, QG]) if biased else None
            bv = sb2("bv", [P, DA]) if biased else None
            k_sb = sb2("k_sb", [P, 2, B, TC])
            own = sb2("own", [P, HR])
            VC = min(DA, HALF)
            NV = B * DA // VC
            kps = [ctx2.enter_context(nc.psum_tensor(f"{name}_kps{i}", [P, B, TC], F32)) for i in range(2)]
            vps = [ctx2.enter_context(nc.psum_tensor(f"{name}_vps{i}", [P, VC], F32)) for i in range(4)]
            with nc.Block() as block:
                @block.sync
                def _(sp):
                    sp.dma_start(wk[0:CW], w["k"]).then_inc(w_in, DMA)
                    sp.dma_start(wv[0:CW], w["v"]).then_inc(w_in, DMA)
                    if biased:
                        with nc.allow_non_contiguous_dma("bias columns"):
                            sp.dma_start(bk[:], w["bk"].rearrange("(g p) o -> p (g o)", p=P)).then_inc(w_in, DMA)
                        sp.dma_start(bv[:], w["bv"].to_broadcast((P, DA))).then_inc(w_in, DMA)

                NWD = 4 if biased else 2

                @block.gpsimd
                def _(pool):
                    pool.memset(own[:], 1.0).then_inc(made, 1)
                    pool.memset(v_all[:], 0.0).then_inc(cleared, 1)
                    pool.wait_ge(made, 1)
                    nc.gpsimd.affine_select(out=own[:], in_=own[:], compare_op=ALU.is_ge, fill=0.0, base=0,
                                            pattern=[[-dh, HR]], channel_multiplier=1).then_inc(made, 1)
                    pool.wait_ge(made, 2)
                    nc.gpsimd.affine_select(out=own[:], in_=own[:], compare_op=ALU.is_ge, fill=0.0, base=dh - 1,
                                            pattern=[[dh, HR]], channel_multiplier=-1).then_inc(made, 1)

                @block.tensor
                def _(pe):
                    pe.wait_ge(w_in, DMA * NWD)
                    for g in range(QG):
                        if g >= 2:
                            pe.wait_ge(k_out, g - 1)
                        for k in range(KC):
                            mm = pe.matmul(kps[g % 2][:], wk[0:CW, k, g * P:(g + 1) * P], ctxT[0:CW, :, k, 0:TC],
                                           start=(k == 0), stop=(k == KC - 1))
                        mm.then_inc(k_full, 1)
                    for i in range(NV):
                        b, c = i % B, i // B
                        for k in range(KC):
                            mm = pe.matmul(vps[i][0:TC, :], ctxT[0:CW, b, k, 0:TC], wv[0:CW, k, c * VC:(c + 1) * VC],
                                           start=(k == 0), stop=(k == KC - 1))
                        mm.then_inc(v_full, 1)

                @block.scalar
                def _(act):
                    if biased:
                        act.wait_ge(w_in, DMA * NWD)
                    for g in range(QG):
                        act.wait_ge(k_full, g + 1)
                        if g >= 2:
                            act.wait_ge(k_set, B * (g - 1))
                        nc.scalar.activation(k_sb[:, g % 2], kps[g % 2][:], ACT.Identity,
                                             bias=bk[:, g:g + 1] if biased else 0.0).then_inc(k_out, 1)

                @block.vector
                def _(dve):
                    dve.wait_ge(made, 3)
                    for g in range(QG):
                        dve.wait_ge(k_out, g + 1)
                        for b in range(B):
                            dve.tensor_tensor(keys[:, g, :, b, :], k_sb[:, g % 2, b, :].unsqueeze(1).to_broadcast((P, HR, TC)),
                                              own[:].unsqueeze(2).to_broadcast((P, HR, TC)), ALU.mult).then_inc(k_set, 1)
                    dve.wait_ge(cleared, 1)
                    NP_ = VC // dh // 2
                    for i in range(NV):
                        b, c = i % B, i // B
                        dve.wait_ge(v_full, i + 1)
                        src = vps[i][0:TC, :].rearrange("p (r j d) -> p r j d", r=NP_, j=2)
                        dst = v_all[0:TC, c * NP_:(c + 1) * NP_, b, :, 0:dh]
                        if biased:
                            bb = bv[0:TC, :].rearrange("p (r j d) -> p r j d", r=NP_, j=2)
                            dve.tensor_tensor(dst, src, bb, ALU.add).then_inc(v_set, 1)
                        else:
                            dve.tensor_copy(dst, src).then_inc(v_set, 1)

        wq = sb("wq", [P, KD, P if wide else D])
        v_cur = sb("v_cur", [P, B, 2, VW]) if wide else None
        bq = sb("bq", [P, QG]) if biased else None
        q_sb = sb("q_sb", [P, 2, HALF])
        s_sb = sb("s_sb", [P, 4, U, TC])
        top = sb("top", [P, 2, U])
        total = sb("total", [P, 2, U])
        inv = sb("inv", [P, 2, U])
        probs = sb("probs", [P, 2, U, P])
        turned = sb("turned", [P, 2, 2, HALF])
        q_ps = ctx.enter_context(nc.psum_tensor(f"{name}_q_ps", [P, HALF], F32))
        s_ps = [ctx.enter_context(nc.psum_tensor(f"{name}_s_ps{i}", [P, 2, HALF], F32)) for i in range(2)]
        t_ps = ctx.enter_context(nc.psum_tensor(f"{name}_t_ps", [P, 2, HALF], F32))
        o_ps = ctx.enter_context(nc.psum_tensor(f"{name}_o_ps", [P, HALF], F32))

        wq_in = sem("wq_in")
        v_in = sem("v_in") if wide else None
        zeroed = sem("zeroed")
        q_full = sem("q_full")
        q_done = sem("q_done")
        s_full = sem("s_full")
        s_taken = sem("s_taken")
        topped = sem("topped")
        shifted = s_taken if not biased else sem("shifted")
        exp_done = sem("exp_done")
        total_done = sem("total_done")
        inv_done = sem("inv_done")
        scaled = sem("scaled")
        t_full = sem("t_full")
        t_done = sem("t_done")
        o_full = sem("o_full")
        o_done = sem("o_done")

        def scores(n):
            return s_ps[n[1] % 2][:, :, 0:TQ * TC].rearrange("p h (u k) -> p h u k", u=TQ)

        def split(ap):
            return ap.rearrange("p (h u) k -> p h u k", h=2)

        def per_unit(ap):
            return ap.rearrange("p (h u) -> p h u", h=2).unsqueeze(3).to_broadcast((P, 2, TQ, TC))

        with nc.Block() as block:
            @block.sync
            def _(sp):
                def load_q(g):
                    sp.dma_start(wq[:], w["q"][:, :, bass.ds(g * P, P)]).then_inc(wq_in, DMA)

                def load_v(g):
                    sp.dma_start(v_cur[:], v_all[:, bass.ds(g, 1)].squeeze(1)).then_inc(v_in, DMA)

                if wide:
                    load_q(0)
                    load_v(0)
                    with sp.Fori(1, ROUNDS, 1) as g:
                        sp.wait_ge(q_full, g * SR)
                        load_q(g)
                        sp.wait_ge(o_full, g * SR)
                        load_v(g)
                else:
                    sp.dma_start(wq[:], w["q"]).then_inc(wq_in, DMA)
                    with nc.allow_non_contiguous_dma("bias columns"):
                        sp.dma_start(bq[:], w["bq"].rearrange("(g p) o -> p (g o)", p=P)).then_inc(wq_in, DMA)

            @block.tensor
            def _(pe):
                def slot(n):
                    a = ahead(n, 3)
                    if exists(a) and q_first(a):
                        g, s = at(a)
                        if wide:
                            if s == 0:
                                pe.wait_ge(wq_in, (g + 1) * DMA)
                        elif (g, s) == (0, 0):
                            pe.wait_ge(wq_in, 2 * DMA)
                        wait(pe, q_done, a, 0, PQ)
                        r0 = 0 if wide else s // PQ * P
                        c = chunk(a)
                        for k in range(KD):
                            mm = pe.matmul(q_ps[:], wq[:, k, r0:r0 + P], hT[:, k, c * HALF:(c + 1) * HALF],
                                           start=(k == 0), stop=(k == KD - 1))
                        mm.then_inc(q_full, 1)
                    a = ahead(n, 2)
                    if exists(a):
                        g, s = at(a)
                        b = chunk(a) * HALF // T
                        if PQ == 1:
                            wait(pe, q_done, a, 1)
                        else:
                            pe.wait_ge(q_done, (g * SR + s) // PQ + 1)
                        wait(pe, s_taken, a, -1)
                        for t in range(TQ):
                            q = q_sb[:, (s // PQ) % 2, t * P:(t + 1) * P]
                            if wide:
                                k = keys[:, bass.ds(g, 1), :, b, :].squeeze(1) if not isinstance(g, int) else keys[:, g, :, b, :]
                            else:
                                k = keys[:, s // PQ, 2 * (s % PQ):2 * (s % PQ) + 2, b, :]
                            mm = pe.matmul(scores(a)[:, t // 2, 2 * (t % 2):2 * (t % 2) + 2, :], q, k, start=True, stop=True)
                        mm.then_inc(s_full, 1)
                    if exists(n):
                        s = n[1]
                        wait(pe, scaled, n, 1)
                        wait(pe, t_done, n, 0)
                        for j in range(2):
                            for t in range(TQ):
                                mm = pe.transpose(t_ps[:, j, t * P:(t + 1) * P], probs[:, s % 2, 2 * t + j, :], ident[:])
                        mm.then_inc(t_full, 1)
                    a = ahead(n, -1)
                    if exists(a):
                        g, s = at(a)
                        b = chunk(a) * HALF // T
                        wait(pe, t_done, a, 1)
                        if wide and s == 0:
                            pe.wait_ge(v_in, (g + 1) * DMA)
                        wait(pe, o_done, a, 0)
                        r0 = 0 if wide else 64 * (s % 2)
                        for j in range(2):
                            v = v_cur[:, b, j, :] if wide else v_all[:, s, b, j, :]
                            mm = pe.matmul(o_ps[r0 + VW * j:r0 + VW * j + VW, :], v, turned[:, s % 2, j, :],
                                           start=True, stop=True, skip_group_check=True)
                        mm.then_inc(o_full, 1)

                run(pe, slot)

            @block.scalar
            def _(act):
                def slot(n):
                    a = ahead(n, 3)
                    if exists(a) and q_first(a):
                        g, s = at(a)
                        if PQ == 1:
                            wait(act, q_full, a, 1)
                        else:
                            act.wait_ge(q_full, (g * SR + s) // PQ + 1)
                        wait(act, s_full, a, -PQ)
                        nc.scalar.activation(q_sb[:, (s // PQ) % 2, :], q_ps[:], ACT.Identity,
                                             bias=bq[:, s // PQ:s // PQ + 1] if biased else 0.0).then_inc(q_done, 1)
                    if exists(n):
                        s = n[1]
                        wait(act, t_full, n, 1)
                        wait(act, o_full, n, -1)
                        nc.scalar.activation(turned[:, s % 2], t_ps[:], ACT.Identity).then_inc(t_done, 1)
                    a = ahead(n, 2)
                    if exists(a):
                        e = s_sb[:, a[1] % 4]
                        wait(act, shifted, a, 1)
                        nc.scalar.activation(e, e, ACT.Exp, scale=SCALE).then_inc(exp_done, 1)

                run(act, slot)

            @block.vector
            def _(dve):
                def slot(n):
                    a = ahead(n, 1)
                    if exists(a):
                        u = a[1] % 2
                        wait(dve, exp_done, a, 1)
                        wait(dve, inv_done, a, -1)
                        dve.tensor_reduce(total[:, u, :], s_sb[:, a[1] % 4], AX.X, ALU.add).then_inc(total_done, 1)
                        wait(dve, total_done, a, 1)
                        wait(dve, scaled, a, -1)
                        dve.reciprocal(inv[:, u, :], total[:, u, :]).then_inc(inv_done, 1)
                    a = ahead(n, 2)
                    if exists(a):
                        u = a[1] % 2
                        dst = split(s_sb[:, a[1] % 4])
                        wait(dve, s_full, a, 1)
                        if biased:
                            wait(dve, scaled, a, -3)
                            mask = w["key_low"](chunk(a) * HALF // T).unsqueeze(1).unsqueeze(1).to_broadcast((P, 2, TQ, TC))
                            dve.tensor_tensor(dst, scores(a), mask, ALU.add).then_inc(s_taken, 1)
                            wait(dve, s_taken, a, 1)
                            wait(dve, shifted, a, -1)
                            dve.tensor_reduce(top[:, u, :], s_sb[:, a[1] % 4], AX.X, ALU.max).then_inc(topped, 1)
                        else:
                            wait(dve, shifted, a, -1)
                            dve.tensor_reduce(top[:, u, :].rearrange("p (h u) -> p h u", h=2), scores(a), AX.X,
                                              ALU.max).then_inc(topped, 1)
                            wait(dve, topped, a, 1)
                            wait(dve, scaled, a, -3)
                            dve.tensor_tensor(dst, scores(a), per_unit(top[:, u, :]), ALU.subtract).then_inc(s_taken, 1)
                    a = ahead(n, -1)
                    if exists(a):
                        g, s = at(a)
                        wait(dve, o_full, a, 1)
                        if wide:
                            c = s
                            dst = oT[:, g, c * HALF:(c + 1) * HALF] if isinstance(g, int) else \
                                oT[:, bass.ds(g, 1), c * HALF:(c + 1) * HALF].squeeze(1)
                            dve.tensor_copy(dst, o_ps[:]).then_inc(o_done, 1)
                        else:
                            r = slice(64 * (s % 2), 64 * (s % 2) + 64)
                            dve.tensor_copy(oT[r, s // 2, g * HALF:(g + 1) * HALF], o_ps[r, :]).then_inc(o_done, 1)

                run(dve, slot)

            @block.gpsimd
            def _(pool):
                pool.memset(probs[:], 0.0).then_inc(zeroed, 1)
                pool.wait_ge(zeroed, 1)

                def slot(n):
                    a = ahead(n, 1)
                    if exists(a):
                        u = a[1] % 2
                        wait(pool, inv_done, a, 1)
                        wait(pool, t_full, a, -1)
                        nc.gpsimd.tensor_tensor(probs[:, u, :, 0:TC], s_sb[:, a[1] % 4],
                                                inv[:, u, :].unsqueeze(2).to_broadcast((P, U, TC)),
                                                ALU.mult).then_inc(scaled, 1)
                    a = ahead(n, 2)
                    if biased and exists(a):
                        u = a[1] % 2
                        e = s_sb[:, a[1] % 4]
                        wait(pool, topped, a, 1)
                        nc.gpsimd.tensor_tensor(e, e, top[:, u, :].unsqueeze(2).to_broadcast((P, U, TC)),
                                                ALU.subtract).then_inc(shifted, 1)

                run(pool, slot)


GROUP = 4
NGRP = TT // GROUP


class Shared:

    def __init__(self, sem):
        self.sem, self.base = sem, 0

    def since(self, value):
        return self.base + value

    def advance(self, by):
        self.base += by


NORM_SEMS = ("loaded", "x_ready", "prod_full", "summed", "stat", "var_done", "sd_done", "normed", "turn_full",
             "h_done", "stored")


def project_norm(nc, shared, name, src, rows, w_loads, bias, x, x_in, ln, hT, ident, out):
    with ExitStack() as ctx:
        def sb(n, shape, dt=F32):
            return ctx.enter_context(nc.sbuf_tensor(f"{name}_{n}", shape, dt))

        KN = src.shape[1] if src is not None else 0
        wt = sb("w", [P, KN, D]) if KN else None
        bias_b = sb("bias", [P, D]) if KN else None
        stats = sb("stats", [P, 2, GROUP, 6])
        mv = sb("mean_var", [P, 2, GROUP, 2])
        ve = sb("var_eps", [P, 2, GROUP])
        sd = sb("deviation", [P, 2, GROUP])
        rs = sb("inverse", [P, 2, GROUP])
        hn = sb("normed", [P, 2, GROUP, D]) if ln else None
        lns = sb("ln", [P, 2, KD]) if ln else None
        prod = [ctx.enter_context(nc.psum_tensor(f"{name}_prod{i}", [P, GROUP, D], F32)) for i in range(2)]
        turned = [ctx.enter_context(nc.psum_tensor(f"{name}_turned{i}", [P, KD, HALF], F32)) for i in range(2)]

        loaded = shared["loaded"]
        x_ready = shared["x_ready"]
        prod_full = shared["prod_full"]
        summed = shared["summed"]
        stat = shared["stat"]
        var_done = shared["var_done"]
        sd_done = shared["sd_done"]
        normed = shared["normed"]
        turn_full = shared["turn_full"]
        h_done = shared["h_done"]
        stored = shared["stored"]

        loads = []
        if x_in is not None:
            loads.append((x[:], x_in))
        if KN:
            loads += [(dst(wt), s) for dst, s in w_loads]
            loads.append((bias_b[:], bias.to_broadcast((P, D))))
        if ln:
            loads += [(lns[:, i, :], ln[i]) for i in range(2)]
        clear = KN and rows is not None

        def ahead(first, second):
            first(0)
            for i in range(1, NGRP):
                first(i)
                second(i - 1)
            second(NGRP - 1)

        with nc.Block() as block:
            @block.sync
            def _(sp):
                if clear:
                    sp.wait_ge(stat.sem, stat.since(1))
                for dst, s in loads:
                    with nc.allow_non_contiguous_dma("small vectors"):
                        sp.dma_start(dst, s).then_inc(loaded.sem, DMA)
                if out is not None:
                    for i in range(NGRP):
                        at = slice(i * GROUP, (i + 1) * GROUP)
                        sp.wait_ge(summed.sem, summed.since(i + 1))
                        sp.dma_start(out[:, at, :], x[:, at, :]).then_inc(stored.sem, DMA)
                    sp.wait_ge(stored.sem, stored.since(NGRP * DMA))

            @block.gpsimd
            def _(pool):
                if KN:
                    pool.wait_ge(loaded.sem, loaded.since(DMA * len(loads)))
                    for i in range(NGRP):
                        at = slice(i * GROUP, (i + 1) * GROUP)
                        nc.gpsimd.tensor_tensor(x[:, at, :], x[:, at, :],
                                                bias_b[:].unsqueeze(1).to_broadcast((P, GROUP, D)),
                                                ALU.add).then_inc(x_ready.sem, 1)

            @block.tensor
            def _(pe):
                def product(i):
                    if not KN:
                        return
                    if i == 0:
                        pe.wait_ge(loaded.sem, loaded.since(DMA * len(loads)))
                    if i >= 2:
                        pe.wait_ge(summed.sem, summed.since(i - 1))
                    for t in range(GROUP):
                        at = (i * GROUP + t) * P
                        for k in range(KN):
                            mm = pe.matmul(prod[i % 2][:, t, :], src[:, k, at:at + P], wt[:, k, :],
                                           start=(k == 0), stop=(k == KN - 1))
                    mm.then_inc(prod_full.sem, 1)

                def turn(i):
                    if not ln:
                        return
                    pe.wait_ge(normed.sem, normed.since(i + 1))
                    if i >= 2:
                        pe.wait_ge(h_done.sem, h_done.since(i - 1))
                    for k in range(KD):
                        for t in range(GROUP):
                            mm = pe.transpose(turned[i % 2][:, k, t * P:(t + 1) * P],
                                              hn[:, i % 2, t, k * P:(k + 1) * P], ident[:])
                    mm.then_inc(turn_full.sem, 1)

                ahead(product, turn)

            @block.vector
            def _(dve):
                step = Step(stat.sem, stat.base)
                if clear:
                    step(dve.memset(wt[:], 0.0))

                def stats_of(i):
                    at = slice(i * GROUP, (i + 1) * GROUP)
                    u = i % 2
                    if KN:
                        dve.wait_ge(x_ready.sem, x_ready.since(i + 1))
                        dve.wait_ge(prod_full.sem, prod_full.since(i + 1))
                        dve.tensor_tensor(x[:, at, :], prod[u][:], x[:, at, :], ALU.add).then_inc(summed.sem, 1)
                        dve.wait_ge(summed.sem, summed.since(i + 1))
                    elif i == 0:
                        dve.wait_ge(loaded.sem, loaded.since(DMA * len(loads)))
                    if not ln:
                        return
                    for t in range(GROUP):
                        ins = dve.bn_stats(stats[:, u, t, :], x[:, i * GROUP + t, :])
                    step(ins)
                    step.wait(dve)
                    for t in range(GROUP):
                        ins = dve.bn_aggr(mv[:, u, t, :], stats[:, u, t, :])
                    step(ins)
                    step.wait(dve)
                    dve.tensor_scalar(ve[:, u, :], mv[:, u, :, 1], EPS, None, ALU.add).then_inc(var_done.sem, 1)

                def normalise(i):
                    if not ln:
                        return
                    u = i % 2
                    dve.wait_ge(sd_done.sem, sd_done.since(i + 1))
                    step(dve.reciprocal(rs[:, u, :], sd[:, u, :]))
                    step.wait(dve)
                    if i >= 2:
                        dve.wait_ge(turn_full.sem, turn_full.since(i - 1))
                    for t in range(GROUP):
                        ins = dve.tensor_scalar(hn[:, u, t, :], x[:, i * GROUP + t, :], mv[:, u, t, 0:1],
                                                rs[:, u, t:t + 1], ALU.subtract, ALU.mult)
                    ins.then_inc(normed.sem, 1)

                ahead(stats_of, normalise)

            @block.scalar
            def _(act):
                def root(i):
                    if ln:
                        act.wait_ge(var_done.sem, var_done.since(i + 1))
                        nc.scalar.activation(sd[:, i % 2, :], ve[:, i % 2, :], ACT.Sqrt).then_inc(sd_done.sem, 1)

                def evacuate(i):
                    if ln:
                        act.wait_ge(turn_full.sem, turn_full.since(i + 1))
                        for k in range(KD):
                            ins = nc.scalar.activation(hT[:, k, i * HALF:(i + 1) * HALF], turned[i % 2][:, k, :],
                                                       ACT.Identity, scale=lns[:, 0, k:k + 1],
                                                       bias=lns[:, 1, k:k + 1])
                        ins.then_inc(h_done.sem, 1)

                ahead(root, evacuate)

        loaded.advance(DMA * len(loads))
        if KN:
            for s in (x_ready, prod_full, summed):
                s.advance(NGRP)
        if ln:
            for s in (var_done, sd_done, normed, turn_full, h_done):
                s.advance(NGRP)
        if out is not None:
            stored.advance(NGRP * DMA)
        stat.advance((1 if clear else 0) + (3 * NGRP if ln else 0))


def hidden_layer(nc, name, hT, w1, b1, gated, hid):
    FF = 4 * D
    MT = FF // P
    NC4 = NT // HALF
    with ExitStack() as ctx:
        def sem(n):
            return ctx.enter_context(nc.semaphore(f"{name}_{n}"))

        NB = 2 if gated else 1
        w = ctx.enter_context(nc.sbuf_tensor(f"{name}_w1", [P, 2, NB, KD, P], F32))
        bb = ctx.enter_context(nc.sbuf_tensor(f"{name}_b1", [P, 2, NB], F32))
        gate = ctx.enter_context(nc.sbuf_tensor(f"{name}_gate", [P, NC4, HALF], F32)) if gated else None
        banks = [ctx.enter_context(nc.psum_tensor(f"{name}_ps{i}", [P, HALF], F32)) for i in range(8)]
        loaded = [sem(f"loaded{u}") for u in range(2)]
        g_full = sem("g_full")
        a_full = sem("a_full")
        gelu = sem("gelu")
        done = sem("done")
        last = done if gated else gelu

        def bank(u, c, n):
            return banks[4 * n + c] if gated else banks[4 * u + c]

        def walk(eng, tile):
            for u in range(2):
                tile(0, u)
            with eng.Fori(1, MT // 2, 1) as i:
                for u in range(2):
                    tile(i, u)

        def ready(eng, s, mt, k):
            if not isinstance(mt, int) or 4 * mt + k > 0:
                eng.wait_ge(s, mt * NC4 + k)

        with nc.Block() as block:
            @block.sync
            def _(sp):
                def load(mt, u):
                    for n in range(NB):
                        col = mt * P + ((1 - n) * FF if gated else 0)
                        with nc.allow_non_contiguous_dma("bias column"):
                            sp.dma_start(w[:, u, n], w1[:, :, bass.ds(col, P)]).then_inc(loaded[u], DMA)
                            sp.dma_start(bb[:, u, n:n + 1], b1[bass.ds(col, P), :]).then_inc(loaded[u], DMA)

                load(0, 0)
                load(1, 1)
                with sp.Fori(1, MT // 2, 1) as i:
                    for u in range(2):
                        sp.wait_ge(last, i * (2 * NC4) + (u - 1) * NC4)
                        load(i * 2 + u, u)

            @block.tensor
            def _(pe):
                def tile(i, u):
                    mt = i * 2 + u
                    pe.wait_ge(loaded[u], (i + 1) * (2 * NB * DMA))
                    for c in range(NC4):
                        for n in range(NB):
                            if gated:
                                ready(pe, gelu if n == 0 else done, mt, c - NC4 + 1)
                            else:
                                ready(pe, gelu, mt, c - 2 * NC4 + 1)
                            for k in range(KD):
                                mm = pe.matmul(bank(u, c, n)[:], w[:, u, n, k, :], hT[:, k, c * HALF:(c + 1) * HALF],
                                               start=(k == 0), stop=(k == KD - 1))
                            mm.then_inc(a_full if n else g_full, 1)
                walk(pe, tile)

            @block.scalar
            def _(act):
                def tile(i, u):
                    mt = i * 2 + u
                    for c in range(NC4):
                        act.wait_ge(g_full, mt * NC4 + (c + 1))
                        if gated:
                            ready(act, done, mt, c - NC4 + 1)
                            dst = gate[:, c, :]
                        else:
                            dst = hid[:, bass.ds(mt, 1), c * HALF:(c + 1) * HALF].squeeze(1) \
                                if not isinstance(mt, int) else hid[:, mt, c * HALF:(c + 1) * HALF]
                        nc.scalar.activation(dst, bank(u, c, 0)[:], ACT.Gelu, bias=bb[:, u, 0:1]).then_inc(gelu, 1)
                walk(act, tile)

            if gated:
                @block.vector
                def _(dve):
                    def tile(i, u):
                        mt = i * 2 + u
                        for c in range(NC4):
                            dve.wait_ge(a_full, mt * NC4 + (c + 1))
                            dve.wait_ge(gelu, mt * NC4 + (c + 1))
                            dst = hid[:, bass.ds(mt, 1), c * HALF:(c + 1) * HALF].squeeze(1) \
                                if not isinstance(mt, int) else hid[:, mt, c * HALF:(c + 1) * HALF]
                            dve.scalar_tensor_tensor(out=dst, in0=bank(u, c, 1)[:], scalar=bb[:, u, 1:2],
                                                     in1=gate[:, c, :], op0=ALU.add, op1=ALU.mult).then_inc(done, 1)
                    walk(dve, tile)


def constants(nc, a, ident, ones, ctxT, key_mask, ctx_bias, pad_bias, ctx_low):
    with ExitStack() as ctx:
        def sb(n, shape, dt=F32):
            return ctx.enter_context(nc.sbuf_tensor(f"const_{n}", shape, dt))

        def sem(n):
            return ctx.enter_context(nc.semaphore(f"const_{n}"))

        c_in = sb("ctx", [P, B, DC])
        m_in = sb("mask", [P, B, QT], U8)
        e_in = sb("emask", [P, B], U8)
        r_in = sb("rmask", [P, B, TC], U8)
        ps = [ctx.enter_context(nc.psum_tensor(f"const_ps{i}", [P, HALF], F32)) for i in range(B)]
        loaded = sem("loaded")
        made = sem("made")
        step_sem = sem("step")
        turned = sem("turned")
        with nc.Block() as block:
            @block.sync
            def _(sp):
                with nc.allow_non_contiguous_dma("masks, once"):
                    sp.dma_start(c_in[0:TC], a["ctx_768"].rearrange("b t c -> t b c")).then_inc(loaded, DMA)
                    for b in range(B):
                        sp.dma_start(m_in[:, b, :], a["mask_BxS_bf0"][b].rearrange("(t p) -> p t", p=P)).then_inc(loaded, DMA)
                        sp.dma_start(e_in[0:TC, b:b + 1], a["mask_BxS2_bf0"][b].rearrange("(p o) -> p o", o=1)).then_inc(loaded, DMA)
                        sp.dma_start(r_in[:, b, :], a["mask_BxS2_bf0"][b:b + 1, :].to_broadcast((P, TC))).then_inc(loaded, DMA)
                    sp.wait_ge(loaded, DMA * 7)

            @block.gpsimd
            def _(pool):
                pool.memset(ones[:], 1.0)
                pool.memset(ident[:], 0.0).then_inc(made, 1)
                pool.wait_ge(made, 1)
                nc.gpsimd.affine_select(out=ident[:], in_=ident[:], compare_op=ALU.not_equal, fill=1.0, base=0,
                                        pattern=[[-1, P]], channel_multiplier=1).then_inc(made, 1)

            @block.tensor
            def _(pe):
                pe.wait_ge(loaded, DMA * 7)
                pe.wait_ge(made, 2)
                for b in range(B):
                    for k in range(KC):
                        mm = pe.transpose(ps[b][0:CW, k * P:k * P + TC], c_in[0:TC, b, k * CW:(k + 1) * CW],
                                          ident[0:TC, 0:TC])
                    mm.then_inc(turned, 1)

            @block.vector
            def _(dve):
                step = Step(step_sem)
                step(dve.memset(ctx_bias[:], LOW))
                step(dve.memset(pad_bias[:], LOW))
                step.wait(dve)
                dve.memset(pad_bias[0:TC, :], 0.0)
                dve.wait_ge(loaded, DMA * 7)
                dve.tensor_scalar(key_mask[:], m_in[:], -3e38, 3e38, ALU.mult, ALU.mult)
                dve.tensor_scalar(ctx_bias[0:TC, :], e_in[0:TC, :], -3e38, 3e38, ALU.mult, ALU.mult)
                dve.tensor_scalar(ctx_low[:], r_in[:], LOW, None, ALU.mult)
                for b in range(B):
                    dve.wait_ge(turned, b + 1)
                    for k in range(KC):
                        dve.tensor_copy(ctxT[0:CW, b, k, 0:TC], ps[b][0:CW, k * P:k * P + TC])


LOW_AT = [P * qt * (qt + 1) // 2 for qt in range(QT + 1)]


def causal_masks(nc, mask, low):
    with ExitStack() as ctx:
        rows = ctx.enter_context(nc.sbuf_tensor("low_rows", [P, B, T], U8))
        loaded = ctx.enter_context(nc.semaphore("low_loaded"))
        keys = ctx.enter_context(nc.semaphore("low_keys"))
        done = ctx.enter_context(nc.semaphore("low_done"))
        with nc.Block() as block:
            @block.sync
            def _(sp):
                for b in range(B):
                    sp.dma_start(rows[:, b, :], mask[b:b + 1, :].to_broadcast((P, T))).then_inc(loaded, DMA)

            @block.vector
            def _(dve):
                dve.wait_ge(loaded, DMA * B)
                for b in range(B):
                    for qt in range(QT):
                        dve.tensor_scalar(low[:, b, LOW_AT[qt]:LOW_AT[qt + 1]], rows[:, b, 0:(qt + 1) * P], LOW, None,
                                          ALU.mult).then_inc(keys, 1)

            @block.gpsimd
            def _(pool):
                for b in range(B):
                    for qt in range(QT):
                        pool.wait_ge(keys, b * QT + qt + 1)
                        blk = low[:, b, LOW_AT[qt + 1] - P:LOW_AT[qt + 1]]
                        nc.gpsimd.affine_select(out=blk, in_=blk, compare_op=ALU.is_ge, fill=LOW, base=0,
                                                pattern=[[-1, P]], channel_multiplier=1).then_inc(done, 1)
                pool.wait_ge(done, B * QT)


def decoder_blocks(nc, a, out):
    L0 = {k[len("L0_xattn_"):]: v for k, v in a.items() if k.startswith("L0_")}
    L1 = {k[len("L1_xattn_"):]: v for k, v in a.items() if k.startswith("L1_")}

    def by_rows(ap, p=P):
        return ap.rearrange("(k p) n -> p k n", p=p)

    def column(ap):
        return ap.rearrange("(n o) -> n o", o=1)

    def row(ap):
        return ap.rearrange("(o n) -> o n", o=1)

    def ln(g, b):
        return [v.rearrange("(k p) -> p k", p=P) for v in (g, b)]

    x_dram = a["x"].rearrange("b t d -> (b t) d").rearrange("(t p) d -> p t d", p=P)
    out_dram = out.rearrange("b t d -> (b t) d").rearrange("(t p) d -> p t d", p=P)

    with ExitStack() as ctx:
        def keep(n, shape, dt=F32):
            return ctx.enter_context(nc.sbuf_tensor(n, shape, dt))

        def scoped(n, shape, dt=F32):
            return nc.sbuf_tensor(n, shape, dt)

        norm_sems = {n: Shared(ctx.enter_context(nc.semaphore(f"norm_{n}"))) for n in NORM_SEMS}
        ident, ones = keep("ident", [P, P]), keep("ones", [P, 64])
        ctxT = keep("ctxT", [P, B, KC, TC + 1])
        key_mask = keep("key_mask", [P, B, QT])
        ctx_bias, pad_bias = keep("ctx_bias", [P, B]), keep("pad_bias", [P, 1])
        ctx_low = keep("ctx_low", [P, B, TC])
        hT = keep("hT", [P, KD, NT])

        constants(nc, a, ident, ones, ctxT, key_mask, ctx_bias, pad_bias, ctx_low)
        x = keep("x", [P, TT, D])
        project_norm(nc, norm_sems, "ln01", None, None, None, None, x, x_dram, ln(L0["ln1_g"], L0["ln1_b"]), hT, ident, None)

        wide = {"G": 2, "dh": 64, "causal": False, "biased": False}
        NG = HEADS // 2
        with scoped("o0", [P, NG, NT]) as oT:
            attention(nc, "sa0", {**wide, "cross": False}, hT, ctxT, ident, ones,
                      {"q": by_rows(L0["sa_wq"]), "k": by_rows(L0["sa_wk"]), "v": by_rows(L0["sa_wv"]),
                       "key_bias": lambda b, kt: 0.0}, oT, spare=x)
            project_norm(nc, norm_sems, "po0", oT, None, [(lambda wt: wt[:], by_rows(L0["sa_wo"]))], row(L0["sa_bo"]), x, x_dram,
                         ln(L0["ln2_g"], L0["ln2_b"]), hT, ident, None)
            cross_attention(nc, "ca0", wide, hT, ctxT, ident,
                            {"q": by_rows(L0["ca_wq"]), "k": by_rows(L0["ca_wk"], CW), "v": by_rows(L0["ca_wv"], CW)}, oT)
            project_norm(nc, norm_sems, "pc0", oT, None, [(lambda wt: wt[:], by_rows(L0["ca_wo"]))], row(L0["ca_bo"]), x, None,
                         ln(L0["ln3_g"], L0["ln3_b"]), hT, ident, None)
            hidden_layer(nc, "ff0", hT, by_rows(L0["ff_w1"]), column(L0["ff_b1"]), True, oT)
            project_norm(nc, norm_sems, "pf0", oT, None, [(lambda wt: wt[:], by_rows(L0["ff_w2"]))], row(L0["ff_b2"]), x, None,
                         ln(L1["ln1_w"], L1["ln1_b"]), hT, ident, None)

        thin = {"G": 4, "dh": 16, "biased": True}
        NG = HEADS // 4

        def padded(ap):
            v = ap.rearrange("(g j d) n -> j d g n", g=NG, j=4)
            return [((lambda wt, j=j: wt[32 * j:32 * j + 16, :, :]), v[j]) for j in range(4)]

        with scoped("o1", [P, NG, NT]) as oT:
            with scoped("low", [P, B, LOW_AT[QT]], BF16) as low:
                causal_masks(nc, a["mask_BxS_bf0"], low)
                attention(nc, "sa1", {**thin, "cross": False, "causal": True}, hT, ctxT, ident, ones,
                          {"q": by_rows(L1["qkv_w"]), "bq": column(L1["qkv_b"]),
                           "bv": row(L1["qkv_b"])[:, 2 * D:3 * D],
                           "key_bias": lambda b, kt: key_mask[:, b, kt:kt + 1],
                           "key_low": lambda b, qt, k0, n: low[:, b, LOW_AT[qt] + k0:LOW_AT[qt] + k0 + n]}, oT)
            project_norm(nc, norm_sems, "po1", oT, 1, padded(L1["proj_w"]), row(L1["proj_b"]), x, None,
                         ln(L1["ln2_w"], L1["ln2_b"]), hT, ident, None)
            cross_attention(nc, "ca1", thin, hT, ctxT, ident,
                            {"q": by_rows(L1["q_w"]), "k": by_rows(L1["k_w"], CW), "v": by_rows(L1["v_w"], CW),
                             "bq": column(L1["q_b"]), "bk": column(L1["k_b"]), "bv": row(L1["v_b"]),
                             "key_low": lambda b: ctx_low[:, b, :]}, oT)
            project_norm(nc, norm_sems, "pc1", oT, 1, padded(L1["out_w"]), row(L1["out_b"]), x, None,
                         ln(L1["ln3_w"], L1["ln3_b"]), hT, ident, None)
        with scoped("hid1", [P, 4 * D // P, NT]) as hid:
            hidden_layer(nc, "ff1", hT, by_rows(L1["mlp1_w"]), column(L1["mlp1_b"]), False, hid)
            project_norm(nc, norm_sems, "pf1", hid, None, [(lambda wt: wt[:], by_rows(L1["mlp2_w"]))], row(L1["mlp2_b"]), x, None,
                         None, hT, ident, out_dram)


def kernel(**inputs):
    import numpy as np
    import concourse.bacc as bacc
    from concourse.bass_utils import run_bass_kernel_spmd

    nc = bacc.Bacc("TRN2", target_bir_lowering=False, num_devices=1)
    arrays, aps = {}, {}
    for name, value in inputs.items():
        v = np.ascontiguousarray(value)
        arrays[f"in_{name}"] = v
        aps[name] = nc.dram_tensor(f"in_{name}", v.shape, mybir.dt.from_np(v.dtype), kind="ExternalInput").ap()
    out = nc.dram_tensor("out", (B, T, D), F32, kind="ExternalOutput").ap()
    decoder_blocks(nc, aps, out)
    r = run_bass_kernel_spmd(nc, [arrays], core_ids=[0])
    return r.results[0]["out"]
```

```python
from contextlib import ExitStack

import concourse.bass as bass
from concourse import mybir

F32 = mybir.dt.float32
F32R = mybir.dt.float32r
BF16 = mybir.dt.bfloat16
U8 = mybir.dt.uint8
ALU = mybir.AluOpType
ACT = mybir.ActivationFunctionType
AX = mybir.AxisListType

P = 128
B, T, D = 2, 1024, 256
TC, DC = 77, 192
NT = B * T
TT = NT // P
KD = D // P
KC, CW = 2, DC // 2
HEADS = 16
EPS = 1e-5
LOW = -1e30
HALF = 512
DMA = 16
QT = T // P


def fetch_early(sp, prefetch):
    for dst, src, sem in prefetch:
        sp.dma_start(dst, src).then_inc(sem, DMA)


def lin(g, b, per, k):
    return g * (2 * per) + (b * per + k)


class Step:

    def __init__(self, sem, n=0):
        self.sem, self.n = sem, n

    def __call__(self, ins):
        self.n += 1
        return ins.then_inc(self.sem, 1)

    def wait(self, eng):
        eng.wait_ge(self.sem, self.n)


def attention(nc, name, cfg, hT, ident, ones, w, oT, spare=None, prefetch=()):
    G, dh, causal, biased = cfg["G"], cfg["dh"], cfg["causal"], cfg["biased"]
    wide = dh == 64
    NG = HEADS // G
    GD = G * dh
    KT = T // P
    NQ = 2 if wide else 1
    MROW = 64 if wide else 96
    QS = G if wide else G // 2
    VW = P // G
    SCALE = float(dh) ** -0.5
    NE = G * KT
    NP = 2 * G
    NADD = G * (KT - 2) if wide else 0

    if wide:
        proj = [("q", c) for c in range(2)] + [("k", c) for c in range(2)]
    else:
        proj = [(s, c, r) for r in range(G // 2) for s in "qk" for c in range(2)]
    vs = [("v", c) for c in range(2 if wide else 1)]
    if causal:
        maxes = [("m", j, qt, h, min(HALF, (qt + 1) * P - h * HALF))
                 for j in range(G) for qt in range(QT) for h in range(2) if (qt + 1) * P > h * HALF]
    else:
        maxes = [("m", j, qt, h, HALF) for j in range(G) for qt in range(QT) for h in range(2)]
    items = proj + vs + maxes + [("t",)]
    NF = len(items)
    NDEN = 2 if wide else 0
    NCH = NF + NDEN
    IV = len(proj) + len(vs) - 1

    def spans(kt):
        q0 = kt * P if causal else 0
        return [(max(q0, lo), lo + HALF) for lo in (0, HALF) if q0 < lo + HALF]

    back = []
    for kt in range(KT):
        back += [("s", j, kt, h) for j in range(G) for h in range(len(spans(kt)))]
        if kt:
            back += [("pv", 0, kt - 1, h) for h in range(len(spans(kt - 1)))]
    back += [("pv", 0, KT - 1, h) for h in range(len(spans(KT - 1)))]

    def woven():
        nb = len(back)
        lead = len(proj) + len(vs)
        led, first_m, last_m = (11, 21, nb - 2) if wide else (18, 19, nb - 3)

        def columns(piece):
            lo, hi = spans(piece[2])[piece[3]]
            return (hi - lo) * (1 if piece[0] == "s" else 2)

        room = sum(columns(p) for p in back[first_m:last_m])
        chunks = [m[4] + (64 if wide else 150) for m in maxes]
        out, at, passed = [], 0, 0
        for i, piece in enumerate(back):
            out.append(("back", piece, None))
            if i < first_m:
                want = min(lead, lead * (i + 1) // led)
            elif i >= last_m:
                want = NF
            else:
                passed += columns(piece)
                want = lead
                while want < NF - 1 and sum(chunks[:want - lead + 1]) * room <= passed * sum(chunks):
                    want += 1
            while at < want:
                out.append(("front", items[at], at))
                at += 1
        return out

    WOVEN = woven()
    FRONT = [("front", it, i) for i, it in enumerate(items)]
    BACK = [("back", piece, None) for piece in back]

    def walk(eng, front, both, tail):
        front(0, 0)
        both(0, 0)
        both(0, 1)
        if NG > 4:
            with eng.Fori(1, NG - 1, 1) as g:
                both(g, 0)
                both(g, 1)
        else:
            for g in range(1, NG - 1):
                both(g, 0)
                both(g, 1)
        both(NG - 1, 0)
        tail(NG - 1, 1)

    def after(g, b):
        return (g, 1) if b == 0 else (g + 1, 0)

    def front_chunk(g, b, i):
        if isinstance(g, int) and (g, b) == (0, 0):
            return i
        return lin(g, b, NCH, NF - NCH + i)

    def den_chunk(g, b, c):
        last = isinstance(g, int) and (g, b) == (NG - 1, 1)
        return lin(g, b, NCH, NF + (0 if last else NF) + c)

    def front_bank(g, b, i):
        return i % 2 if isinstance(g, int) and (g, b) == (0, 0) else (b * NCH + NF - NCH + i) % 2

    def den_bank(g, b, c):
        last = isinstance(g, int) and (g, b) == (NG - 1, 1)
        return (b * NCH + NF + (0 if last else NF) + c) % 2

    with ExitStack() as ctx:
        def sb(n, shape, dt=F32):
            return ctx.enter_context(nc.sbuf_tensor(f"{name}_{n}", shape, dt))

        def ps(n, shape):
            return ctx.enter_context(nc.psum_tensor(f"{name}_{n}", shape, F32))

        def sem(n):
            return ctx.enter_context(nc.semaphore(f"{name}_{n}"))

        q_stage = sb("q_stage", [P, 2, QS, NQ, T], F32R)
        k_stage = sb("k_stage", [P, 2, G, NQ, T], F32R)
        v_buf = sb("v_buf", [P, 2, KT, P])
        if wide:
            q_hi, q_lo = sb("q_hi", [P, T], F32R), sb("q_lo", [P, T], F32R)
            k_hi, k_lo = sb("k_hi", [P, T], F32R), sb("k_lo", [P, T], F32R)
        else:
            k_sum = sb("k_sum", [P, 2, HALF])
        p_buf = sb("p_buf", [P, NP, T])
        if spare is None:
            acc, recip = None, sb("recip", [P, T])
        else:
            acc = spare[:].rearrange("p t d -> p (t d)")[:, 0:G * T].rearrange("p (g t) -> p g t", g=G)
            recip = spare[:].rearrange("p t d -> p (t d)")[:, G * T:(G + 1) * T]
        if wide:
            wq, wk = sb("wq", [P, KD, P]), sb("wk", [P, KD, P])
        else:
            wq, wk = [sb(n, [P, KD, HEADS // 2, 4, 32]) for n in ("wq", "wk")]
            bq, bk = sb("bq", [P, HEADS // 2]), sb("bk", [P, HEADS // 2])
            own = sb("own", [P, 2])
            bk_own = sb("bk_own", [P, 2, HEADS // 2])
        wv = sb("wv", [P, KD, GD])
        bv = sb("bv", [P, GD]) if biased else None
        mx = sb("mx", [P, 2, G, QT, 2])
        m_row = sb("m_row", [P, G, QT])
        m_hi = sb("m_hi", [P, G, QT], F32R)
        m_parts = sb("m_parts", [P, G, 2, QT])
        m_turned = sb("m_turned", [2 * G * QT, P], F32R)
        junk = sb("junk", [P, 2, HALF], BF16 if causal else F32) if biased else None

        front_ps = [ps(f"front{i}", [P, HALF]) for i in range(2)]
        score_ps = [ps(f"score{i}", [P, T]) for i in range(2)]
        out_ps = ps("out", [P, T])

        cleared = sem("cleared") if wide else None
        w_in = sem("w_in")
        front_full = sem("front_full")
        hi_done = sem("hi_done")
        drained = sem("drained")
        stage_in = sem("stage_in") if wide else None
        all_in = None if wide else sem("all_in")
        set_up = None if wide else sem("set_up")
        max_in = sem("max_in")
        m_step = sem("m_step")
        score_full = sem("score_full")
        exp_done = sem("exp_done")
        diag_done = sem("diag_done") if causal else None
        added = sem("added") if NADD else None
        pv_done = sem("pv_done")
        norm = sem("norm")
        out_done = sem("out_done")

        w_dmas = []

        def cols(ap, g, width, start=0):
            return ap[:, :, bass.ds(g * width + start, width)]

        if wide:
            w_dmas.append((wq[:], lambda g: cols(w["q"], g, GD)))
            w_dmas.append((wk[:], lambda g: cols(w["k"], g, GD)))
            w_dmas.append((wv[:], lambda g: cols(w["v"], g, GD)))
        else:
            w_dmas.append((wv[:], lambda g: cols(w["q"], g, GD, 2 * D)))
            w_dmas.append((bv[:, :], lambda g: w["bv"][:, bass.ds(g * GD, GD)].to_broadcast((P, GD))))
        NW = len(w_dmas)

        def stage_dmas(b):
            out = []
            for j in range(G):
                r = slice(dh * j, dh * j + dh)
                q, k = q_stage[:, b, j, :, :], k_stage[:, b, j, :, :]
                out.append((q[0:64, 0, :], q_hi[r, :]))
                out.append((q[0:64, 1, :], q_hi[r, :]))
                out.append((q[64:128, 0, :], q_lo[r, :]))
                out.append((k[0:64, 0, :], k_hi[r, :]))
                out.append((k[64:128, 0, :], k_hi[r, :]))
                out.append((k[0:64, 1, :], k_lo[r, :]))
            return out

        NS = len(stage_dmas(0)) if wide else 0
        NALL = 3 * 6 + 1
        ROWS = 2 * G // QS

        with nc.Block() as block:
            @block.sync
            def _(sp):
                def weights(g):
                    for dst, src in w_dmas:
                        sp.dma_start(dst, src(g)).then_inc(w_in, DMA)

                def front(g, b, load=None):
                    if wide:
                        sp.wait_ge(drained, front_chunk(g, b, len(proj) - 1) + 1)
                        for dst, src in stage_dmas(b):
                            sp.dma_start(dst.bitcast(F32), src.bitcast(F32)).then_inc(stage_in, DMA)
                    if load is not None:
                        sp.wait_ge(drained, front_chunk(g, b, IV) + 1)
                        weights(load)
                    sp.wait_ge(drained, front_chunk(g, b, NF - 1) + 1)
                    for j in range(QS):
                        r = j * ROWS * QT
                        sp.dma_start(q_stage[MROW:MROW + ROWS, b, j, NQ - 1, :].bitcast(F32),
                                     m_turned[r:r + ROWS * QT, :].bitcast(F32)).then_inc(max_in, DMA)

                def both(g, b):
                    g2, b2 = after(g, b)
                    last = isinstance(g2, int) and g2 == NG - 1
                    front(g2, b2, g2 + 1 if b2 == 1 and not last else None)

                weights(0)
                if not wide:
                    with nc.allow_non_contiguous_dma("columns of pairs of heads"):
                        for slot in range(3):
                            for t, off in ((wq, 0), (wk, D)):
                                for kd in range(KD):
                                    sp.dma_start(t[:, kd, :, slot, :], w["q"][:, kd, off:off + D].rearrange(
                                        "p (r n) -> p r n", n=32)).then_inc(all_in, DMA)
                            for t, off in ((bq, 0), (bk, D)):
                                sp.dma_start(t[32 * slot:32 * slot + 32, :], w["bq"][off:off + D, :].rearrange(
                                    "(r n) o -> n (r o)", n=32)).then_inc(all_in, DMA)
                        sp.dma_start(own[:], w["head_rows"]).then_inc(all_in, DMA)
                with nc.allow_non_contiguous_dma("small vectors"):
                    fetch_early(sp, prefetch)
                if wide:
                    sp.wait_ge(cleared, 2)
                walk(sp, front, both, lambda g, b: None)

            @block.tensor
            def _(pe):
                def front_item(g, b, item, i):
                    kind = item[0]
                    c = front_chunk(g, b, i)
                    fr = front_ps[front_bank(g, b, i)]
                    if not isinstance(c, int) or c >= 2:
                        pe.wait_ge(drained, c - 1)
                    if i == 0:
                        pe.wait_ge(w_in, (g + 1) * (DMA * NW))
                        if not wide and isinstance(g, int) and (g, b) == (0, 0):
                            pe.wait_ge(all_in, DMA * NALL)
                            pe.wait_ge(set_up, 1)
                    if kind in ("q", "k"):
                        wt = wk if kind == "k" else wq
                        at = b * T + item[1] * HALF
                        for kd in range(KD):
                            cols_of = wt[:, kd, :] if wide else wt[:, kd, g * (G // 2) + item[2]].rearrange("p s n -> p (s n)")
                            mm = pe.matmul(fr[:], cols_of, hT[:, kd, at:at + HALF], start=(kd == 0), stop=(kd == KD - 1))
                    elif kind == "v":
                        n = HALF // GD
                        for t in range(n):
                            at = b * T + (item[1] * n + t) * P
                            for kd in range(KD):
                                mm = pe.matmul(fr[:, t * GD:(t + 1) * GD], hT[:, kd, at:at + P], wv[:, kd, :],
                                               start=(kd == 0), stop=(kd == KD - 1))
                    elif kind == "m":
                        _, j, qt, half, width = item
                        if (j, qt, half) == (0, 0, 0):
                            if wide:
                                pe.wait_ge(stage_in, lin(g, b, DMA * NS, DMA * NS))
                            else:
                                pe.wait_ge(drained, front_chunk(g, b, len(proj) - 1) + 1)
                        q = q_stage[:, b, j * QS // G, 0, qt * P:(qt + 1) * P]
                        k = k_stage[:, b, j, 0, half * HALF:half * HALF + width]
                        mm = pe.matmul(fr[:, 0:width], q, k, start=True, stop=True)
                    else:
                        pe.wait_ge(m_step, lin(g, b, 3, 3))
                        parts = m_parts[:].rearrange("p g s t -> p (g s t)")
                        mm = pe.transpose(fr[0:2 * G * QT, 0:P], parts, ident[:])
                    mm.then_inc(front_full, 1)

                def back_piece(g, b, piece):
                    first = isinstance(g, int) and (g, b) == (0, 0)
                    what, j, kt, h = piece
                    lo, hi = spans(kt)[h]
                    ends = h == len(spans(kt)) - 1
                    if what == "s":
                        i = kt * G + j
                        if h == 0:
                            if i == 0:
                                pe.wait_ge(max_in, lin(g, b, DMA * QS, DMA * QS))
                            if not (first and i < 2):
                                pe.wait_ge(exp_done, lin(g, b, NE, i - 1))
                        dst = score_ps[i % 2]
                        for s in range(NQ):
                            mm = pe.matmul(dst[:, lo:hi], k_stage[:, b, j, s, kt * P:(kt + 1) * P],
                                           q_stage[:, b, j * QS // G, s, lo:hi], start=(s == 0), stop=(s == NQ - 1))
                        if ends:
                            mm.then_inc(score_full, 1)
                    else:
                        if h == 0:
                            if causal:
                                pe.wait_ge(diag_done, lin(g, b, NE, (kt + 1) * G))
                            else:
                                pe.wait_ge(exp_done, lin(g, b, NE, (kt + 1) * G))
                            if kt == 0 and not first:
                                pe.wait_ge(out_done, lin(g, b, 1, 0))
                        last = kt == KT - 1 or (causal and kt == 3 and lo < HALF)
                        for j in range(G):
                            e = (b * NE + kt * G + j) % NP
                            mm = pe.matmul(out_ps[VW * j:VW * j + VW, lo:hi],
                                           v_buf[:, b, kt, VW * j:VW * j + VW], p_buf[:, e, lo:hi],
                                           start=(kt == 0), stop=last, skip_group_check=True)
                        if ends:
                            mm.then_inc(pv_done, 1)

                def denominators(g, b):
                    if not wide:
                        return
                    for c in range(2):
                        pe.wait_ge(drained, den_chunk(g, b, c) - 1)
                        if NADD and c == 0:
                            pe.wait_ge(added, lin(g, b, NADD, NADD))
                        fr = front_ps[den_bank(g, b, c)]
                        at = slice(c * HALF, (c + 1) * HALF)
                        for j in range(G):
                            e = (b * NE + (KT - 1) * G + j) % NP
                            if NADD:
                                pe.matmul(fr[64 * j:64 * j + 64, :], ones[:, 0:64], acc[:, j, at], start=True, stop=False)
                            mm = pe.matmul(fr[64 * j:64 * j + 64, :], ones[:, 0:64], p_buf[:, e, at],
                                           start=not NADD, stop=True)
                        mm.then_inc(front_full, 1)

                def front(g, b):
                    for _, it, i in FRONT:
                        front_item(g, b, it, i)

                def both(g, b):
                    for which, it, i in WOVEN:
                        if which == "back":
                            back_piece(g, b, it)
                        else:
                            front_item(*after(g, b), it, i)
                    denominators(g, b)

                def tail(g, b):
                    for _, it, _i in BACK:
                        back_piece(g, b, it)
                    denominators(g, b)

                if wide:
                    pe.wait_ge(cleared, 2)
                walk(pe, front, both, tail)

            @block.scalar
            def _(act):
                def front_item(g, b, item, i):
                    if item[0] not in ("q", "k"):
                        return
                    c = front_chunk(g, b, i)
                    first = isinstance(g, int) and (g, b) == (0, 0)
                    if wide and i == 0 and not first:
                        act.wait_ge(stage_in, lin(g, b, DMA * NS, 0))
                    if not wide and i == 0 and first:
                        act.wait_ge(set_up, 4)
                    act.wait_ge(front_full, c + 1)
                    fr = front_ps[front_bank(g, b, i)]
                    at = slice(item[1] * HALF, item[1] * HALF + HALF)
                    if wide:
                        dst = (k_hi if item[0] == "k" else q_hi)[:, at]
                        nc.scalar.activation(dst, fr[:], ACT.Identity).then_inc(hi_done, 1)
                    elif item[0] == "q":
                        r = g * (G // 2) + item[2]
                        nc.scalar.activation(q_stage[:, b, item[2], 0, at], fr[:], ACT.Identity,
                                             bias=bq[:, r:r + 1]).then_inc(hi_done, 1)
                    else:
                        r = g * (G // 2) + item[2]
                        if i >= 4:
                            act.wait_ge(drained, c - 3)
                        nc.scalar.activation(k_sum[:, item[1], :], fr[:], ACT.Identity, bias=bk[:, r:r + 1])
                        for h in range(2):
                            ins = nc.scalar.activation(k_stage[:, b, 2 * item[2] + h, 0, at], fr[:], ACT.Identity,
                                                       bias=bk_own[:, h, r:r + 1], scale=own[:, h:h + 1])
                        ins.then_inc(hi_done, 1)

                def back_piece(g, b, piece):
                    what, j, kt, h = piece
                    if what != "s" or h < len(spans(kt)) - 1:
                        return
                    first = isinstance(g, int) and (g, b) == (0, 0)
                    i = kt * G + j
                    e = (b * NE + i) % NP
                    act.wait_ge(score_full, lin(g, b, NE, i + 1))
                    second = first and kt < 2 or (isinstance(g, int) and KT == 1 and (g, b) == (0, 1))
                    if not second:
                        act.wait_ge(pv_done, lin(g, b, KT, kt - 1))
                        if NADD and kt >= 2:
                            act.wait_ge(added, lin(g, b, NADD, (max(kt - 2, 1) - 1) * G + j + 1))
                        elif wide and (kt == 1 or KT == 1):
                            back_n = 1 if KT > 1 else 2
                            pg, pb = (g, 0) if b == 1 and back_n == 1 else (g - 1, b if back_n == 2 else 1)
                            act.wait_ge(front_full, lin(pg, pb, NCH, 2 * NF + 2))
                        elif NADD:
                            act.wait_ge(added, lin(g, b, NADD, 0))
                    q0 = kt * P if causal else 0
                    bias = w["key_bias"](b, kt)
                    nc.scalar.activation(p_buf[:, e, q0:T], score_ps[i % 2][:, q0:T], ACT.Exp, bias=bias,
                                         scale=SCALE).then_inc(exp_done, 1)

                def front(g, b):
                    for _, it, i in FRONT:
                        front_item(g, b, it, i)

                def both(g, b):
                    for which, it, i in WOVEN:
                        if which == "back":
                            back_piece(g, b, it)
                        else:
                            front_item(*after(g, b), it, i)

                def tail(g, b):
                    for _, it, _i in BACK:
                        back_piece(g, b, it)

                walk(act, front, both, tail)

            @block.vector
            def _(dve):
                dve.memset(v_buf[:], 1.0)
                dve.memset(mx[:], 4.0 * LOW)
                if wide:
                    kb = k_stage[:].bitcast(F32)
                    dve.memset(kb[MROW:P, :, :, NQ - 1, :], 0.0).then_inc(norm, 1)
                    dve.wait_ge(norm, 1)
                    dve.memset(kb[MROW:MROW + 2, :, :, NQ - 1, :], 1.0).then_inc(cleared, 1)
                else:
                    dve.memset(wq[:, :, :, 3, :], 0.0)
                    dve.memset(wk[:, :, :, 3, :], 0.0).then_inc(set_up, 1)
                    dve.memset(bq[96:P, :], 0.0).then_inc(set_up, 1)
                    dve.memset(bk[96:P, :], 1.0).then_inc(set_up, 1)
                    dve.wait_ge(set_up, 3)
                    dve.wait_ge(all_in, DMA * NALL)
                    for h in range(2):
                        ins = dve.tensor_scalar(bk_own[:, h, :], bk[:], own[:, h:h + 1], None, ALU.mult)
                    ins.then_inc(set_up, 1)
                    dve.wait_ge(set_up, 4)

                def front_item(g, b, item, i):
                    kind = item[0]
                    c = front_chunk(g, b, i)
                    fr = front_ps[front_bank(g, b, i)]
                    first = isinstance(g, int) and (g, b) == (0, 0)
                    if kind in ("q", "k"):
                        at = slice(item[1] * HALF, item[1] * HALF + HALF)
                        if wide and i == 0 and not first:
                            dve.wait_ge(stage_in, lin(g, b, DMA * NS, 0))
                        dve.wait_ge(hi_done, lin(g, b, len(proj), i + 1))
                        if wide:
                            hi, lo = (k_hi, k_lo) if kind == "k" else (q_hi, q_lo)
                            dve.tensor_tensor(lo[:, at], fr[:], hi[:, at].bitcast(F32), ALU.subtract).then_inc(drained, 1)
                        elif kind == "q":
                            r = g * (G // 2) + item[2]
                            lo = q_stage[32:64, b, item[2], 0, at]
                            dve.scalar_tensor_tensor(out=lo, in0=fr[32:64, :], scalar=bq[32:64, r:r + 1],
                                                     in1=lo.bitcast(F32), op0=ALU.add, op1=ALU.subtract).then_inc(drained, 1)
                        else:
                            for h in range(2):
                                lo = k_stage[64:96, b, 2 * item[2] + h, 0, at]
                                ins = dve.scalar_tensor_tensor(out=lo, in0=k_sum[64:96, item[1], :],
                                                               scalar=own[64:96, h:h + 1], in1=lo.bitcast(F32),
                                                               op0=ALU.mult, op1=ALU.subtract)
                            ins.then_inc(drained, 1)
                    elif kind == "v":
                        dve.wait_ge(front_full, c + 1)
                        n = HALF // GD
                        src = fr[:, 0:n * GD].rearrange("p (t j d) -> p t j d", t=n, j=G)
                        dst = v_buf[:, b, item[1] * n:item[1] * n + n, :].rearrange("p t (j d) -> p t j d", j=G)
                        if biased:
                            bb = bv[:].rearrange("p (j d) -> p j d", j=G).unsqueeze(1).to_broadcast((P, n, G, dh))
                            ins = dve.tensor_tensor(dst[:, :, :, 0:dh], src, bb, ALU.add)
                        else:
                            ins = dve.tensor_copy(dst, src)
                        ins.then_inc(drained, 1)
                    elif kind == "m":
                        _, j, qt, half, width = item
                        dve.wait_ge(front_full, c + 1)
                        if causal:
                            low = w["key_low"](b, qt, half * HALF, width)
                            dve.wait_ge(drained, c - 1)
                            dve.tensor_tensor_reduce(junk[:, c % 2, 0:width], fr[:, 0:width], low, 1.0, 16.0 * LOW, ALU.add,
                                                     ALU.max, mx[:, b, j, qt, half:half + 1]).then_inc(drained, 1)
                        else:
                            dve.tensor_reduce(mx[:, b, j, qt, half:half + 1], fr[:, 0:width], AX.X,
                                              ALU.max).then_inc(drained, 1)
                    else:
                        dve.wait_ge(drained, c)
                        dve.tensor_tensor(m_row[:], mx[:, b, :, :, 0], mx[:, b, :, :, 1], ALU.max).then_inc(m_step, 1)
                        dve.wait_ge(m_step, lin(g, b, 3, 1))
                        dve.tensor_scalar(m_hi[:], m_row[:], -1.0, None, ALU.mult).then_inc(m_step, 1)
                        dve.wait_ge(m_step, lin(g, b, 3, 2))
                        dve.tensor_copy(m_parts[:, :, 0, :], m_hi[:].bitcast(F32))
                        dve.scalar_tensor_tensor(out=m_parts[:, :, 1, :], in0=m_row[:], scalar=-1.0,
                                                 in1=m_hi[:].bitcast(F32), op0=ALU.mult,
                                                 op1=ALU.subtract).then_inc(m_step, 1)
                        if not first:
                            dve.wait_ge(max_in, lin(g, b, DMA * QS, 0))
                        dve.wait_ge(front_full, c + 1)
                        dve.tensor_copy(m_turned[:], fr[0:2 * G * QT, 0:P]).then_inc(drained, 1)

                def finish(g, b):
                    dst = oT[:, bass.ds(g, 1), b * T:(b + 1) * T] if not isinstance(g, int) else oT[:, g:g + 1, b * T:(b + 1) * T]
                    if wide:
                        for c in range(2):
                            at = slice(c * HALF, (c + 1) * HALF)
                            k = den_chunk(g, b, c)
                            dve.wait_ge(front_full, k + 1)
                            dve.reciprocal(recip[:, at], front_ps[den_bank(g, b, c)][:, :]).then_inc(drained, 1)
                        dve.wait_ge(drained, den_chunk(g, b, 1) + 1)
                        dve.wait_ge(pv_done, lin(g, b, KT, KT))
                        dve.tensor_tensor(dst[:, 0], out_ps[:], recip[:], ALU.mult).then_inc(out_done, 1)
                    else:
                        dve.wait_ge(pv_done, lin(g, b, KT, KT))
                        dve.reciprocal(recip[:], out_ps[:]).then_inc(norm, 1)
                        dve.wait_ge(norm, lin(g, b, 2, 1))
                        dve.stream_shuffle(recip[:], recip[:], [dh] * 32).then_inc(norm, 1)
                        dve.wait_ge(norm, lin(g, b, 2, 2))
                        dve.tensor_tensor(dst[:, 0], out_ps[:], recip[:], ALU.mult).then_inc(out_done, 1)

                def front(g, b):
                    for _, it, i in FRONT:
                        front_item(g, b, it, i)

                def both(g, b):
                    for which, it, i in WOVEN:
                        if which == "front":
                            front_item(*after(g, b), it, i)
                    finish(g, b)

                walk(dve, front, both, finish)

            @block.gpsimd
            def _(pool):
                if wide:
                    pool.memset(q_stage[:].bitcast(F32)[64:P, :, :, 1, :], 0.0).then_inc(cleared, 1)
                if causal:
                    def both(g, b):
                        for kt in range(KT):
                            for j in range(G):
                                i = kt * G + j
                                blk = p_buf[:, (b * NE + i) % NP, kt * P:(kt + 1) * P]
                                pool.wait_ge(exp_done, lin(g, b, NE, i + 1))
                                nc.gpsimd.affine_select(out=blk, in_=blk, compare_op=ALU.is_ge, fill=0.0, base=0,
                                                        pattern=[[1, P]], channel_multiplier=-1).then_inc(diag_done, 1)
                    walk(pool, lambda g, b: None, both, both)
                elif NADD:
                    def both(g, b):
                        for kt in range(1, KT - 1):
                            for j in range(G):
                                i = kt * G + j
                                cur = p_buf[:, (b * NE + i) % NP, :]
                                pool.wait_ge(exp_done, lin(g, b, NE, i + 1))
                                if kt == 1:
                                    first = isinstance(g, int) and (g, b) == (0, 0)
                                    if j == 0 and not first:
                                        pg, pb = (g, 0) if b == 1 else (g - 1, 1)
                                        pool.wait_ge(front_full, lin(pg, pb, NCH, 2 * NF + 2))
                                    prev = p_buf[:, (b * NE + i - G) % NP, :]
                                else:
                                    pool.wait_ge(added, lin(g, b, NADD, (kt - 2) * G + j + 1))
                                    prev = acc[:, j, :]
                                nc.gpsimd.tensor_tensor(acc[:, j, :], prev, cur, ALU.add).then_inc(added, 1)
                    walk(pool, lambda g, b: None, both, both)


def cross_attention(nc, name, cfg, hT, ctxT, ident, kv, w, oT, prefetch=()):
    dh, biased = cfg["dh"], cfg["biased"]
    wide = dh == 64
    HR = P // dh
    QG = HEADS // HR
    PAIRS, CH = HEADS // 2, NT // HALF
    VW = 64 if wide else 32
    ROUNDS, SR = (PAIRS, CH) if wide else (CH, PAIRS)
    PQ = 1 if wide else HR // 2
    TQ = HALF // P
    U = 2 * TQ
    SCALE = float(dh) ** -0.5
    LAST = ROUNDS * SR

    def at(n):
        g, s = n
        return g + s // SR, s % SR

    def exists(n):
        g, s = at(n)
        return not isinstance(g, int) or 0 <= g < ROUNDS

    def chunk(n):
        g, s = at(n)
        return s if wide else g

    def pair(n):
        g, s = at(n)
        return g if wide else s

    def wait(eng, sem, n, k, per=1):
        g, s = n
        if isinstance(g, int):
            v = ((g * SR + s) + k) // per if per > 1 else g * SR + s + k
            if v > 0:
                eng.wait_ge(sem, v)
        else:
            assert per == 1
            eng.wait_ge(sem, g * SR + (s + k))

    def q_first(n):
        return at(n)[1] % PQ == 0

    def run(eng, slot):
        for s in range(-3, SR):
            slot((0, s))
        if wide:
            with eng.Fori(1, ROUNDS - 1, 1) as g:
                for s in range(SR):
                    slot((g, s))
        else:
            for g in range(1, ROUNDS - 1):
                for s in range(SR):
                    slot((g, s))
        for s in range(SR + 1):
            slot((ROUNDS - 1, s))

    def ahead(n, k):
        return (n[0], n[1] + k)

    with ExitStack() as ctx:
        def sb(n, shape, dt=F32):
            return ctx.enter_context(nc.sbuf_tensor(f"{name}_{n}", shape, dt))

        def sem(n):
            return ctx.enter_context(nc.semaphore(f"{name}_{n}"))

        keys = sb("keys", [P, QG, HR, B, TC])
        v_all = sb("v_all", [P, PAIRS, B, 2, VW])
        w_in = kv["sem"]
        k_full = sem("k_full")
        k_out = sem("k_out")
        k_set = sem("k_set")
        v_full = sem("v_full")
        made = sem("made")
        cleared = sem("cleared")
        v_set = sem("v_set")

        with ExitStack() as ctx2:
            def sb2(n, shape, dt=F32):
                return ctx2.enter_context(nc.sbuf_tensor(f"{name}_{n}", shape, dt))

            DA = HEADS * dh
            wk, wv, bk, bv = kv["wk"], kv["wv"], kv.get("bk"), kv.get("bv")
            k_sb = sb2("k_sb", [P, 2, B, TC])
            own = sb2("own", [P, HR])
            VC = min(DA, HALF)
            NV = B * DA // VC
            kps = [ctx2.enter_context(nc.psum_tensor(f"{name}_kps{i}", [P, B, TC], F32)) for i in range(2)]
            vps = [ctx2.enter_context(nc.psum_tensor(f"{name}_vps{i}", [P, VC], F32)) for i in range(4)]
            with nc.Block() as block:
                NWD = 4 if biased else 2

                @block.gpsimd
                def _(pool):
                    pool.memset(own[:], 1.0).then_inc(made, 1)
                    pool.memset(v_all[:], 0.0).then_inc(cleared, 1)
                    pool.wait_ge(made, 1)
                    nc.gpsimd.affine_select(out=own[:], in_=own[:], compare_op=ALU.is_ge, fill=0.0, base=0,
                                            pattern=[[-dh, HR]], channel_multiplier=1).then_inc(made, 1)
                    pool.wait_ge(made, 2)
                    nc.gpsimd.affine_select(out=own[:], in_=own[:], compare_op=ALU.is_ge, fill=0.0, base=dh - 1,
                                            pattern=[[dh, HR]], channel_multiplier=-1).then_inc(made, 1)

                @block.tensor
                def _(pe):
                    pe.wait_ge(w_in, DMA * NWD)
                    for g in range(QG):
                        if g >= 2:
                            pe.wait_ge(k_out, g - 1)
                        for k in range(KC):
                            mm = pe.matmul(kps[g % 2][:], wk[0:CW, k, g * P:(g + 1) * P], ctxT[0:CW, :, k, 0:TC],
                                           start=(k == 0), stop=(k == KC - 1))
                        mm.then_inc(k_full, 1)
                    for i in range(NV):
                        b, c = i % B, i // B
                        for k in range(KC):
                            mm = pe.matmul(vps[i][0:TC, :], ctxT[0:CW, b, k, 0:TC], wv[0:CW, k, c * VC:(c + 1) * VC],
                                           start=(k == 0), stop=(k == KC - 1))
                        mm.then_inc(v_full, 1)

                @block.scalar
                def _(act):
                    if biased:
                        act.wait_ge(w_in, DMA * NWD)
                    for g in range(QG):
                        act.wait_ge(k_full, g + 1)
                        if g >= 2:
                            act.wait_ge(k_set, B * (g - 1))
                        nc.scalar.activation(k_sb[:, g % 2], kps[g % 2][:], ACT.Identity,
                                             bias=bk[:, g:g + 1] if biased else 0.0).then_inc(k_out, 1)

                @block.vector
                def _(dve):
                    dve.wait_ge(made, 3)
                    for g in range(QG):
                        dve.wait_ge(k_out, g + 1)
                        for b in range(B):
                            dve.tensor_tensor(keys[:, g, :, b, :], k_sb[:, g % 2, b, :].unsqueeze(1).to_broadcast((P, HR, TC)),
                                              own[:].unsqueeze(2).to_broadcast((P, HR, TC)), ALU.mult).then_inc(k_set, 1)
                    dve.wait_ge(cleared, 1)
                    NP_ = VC // dh // 2
                    for i in range(NV):
                        b, c = i % B, i // B
                        dve.wait_ge(v_full, i + 1)
                        src = vps[i][0:TC, :].rearrange("p (r j d) -> p r j d", r=NP_, j=2)
                        dst = v_all[0:TC, c * NP_:(c + 1) * NP_, b, :, 0:dh]
                        if biased:
                            bb = bv[0:TC, :].rearrange("p (r j d) -> p r j d", r=NP_, j=2)
                            dve.tensor_tensor(dst, src, bb, ALU.add).then_inc(v_set, 1)
                        else:
                            dve.tensor_copy(dst, src).then_inc(v_set, 1)

        wq = sb("wq", [P, KD, P if wide else D])
        wq_next = sb("wq_next", [P, KD, P]) if wide else None
        v_cur = sb("v_cur", [P, B, 2, VW]) if wide else None
        bq = sb("bq", [P, QG]) if biased else None
        q_sb = sb("q_sb", [P, 2, HALF])
        s_sb = sb("s_sb", [P, 4, U, TC])
        top = sb("top", [P, 2, U])
        total = sb("total", [P, 2, U])
        inv = sb("inv", [P, 2, U])
        probs = sb("probs", [P, 2, U, P])
        turned = sb("turned", [P, 2, 2, HALF])
        q_ps = ctx.enter_context(nc.psum_tensor(f"{name}_q_ps", [P, HALF], F32))
        s_ps = [ctx.enter_context(nc.psum_tensor(f"{name}_s_ps{i}", [P, 2, HALF], F32)) for i in range(2)]
        t_ps = ctx.enter_context(nc.psum_tensor(f"{name}_t_ps", [P, 2, HALF], F32))
        o_ps = ctx.enter_context(nc.psum_tensor(f"{name}_o_ps", [P, HALF], F32))

        wq_in = sem("wq_in")
        wq_set = sem("wq_set") if wide else None
        v_in = sem("v_in") if wide else None
        zeroed = sem("zeroed")
        q_full = sem("q_full")
        q_done = sem("q_done")
        s_full = sem("s_full")
        s_taken = sem("s_taken")
        topped = sem("topped")
        shifted = s_taken if not biased else sem("shifted")
        exp_done = sem("exp_done")
        total_done = sem("total_done")
        inv_done = sem("inv_done")
        scaled = sem("scaled")
        t_full = sem("t_full")
        t_done = sem("t_done")
        o_full = sem("o_full")
        o_done = sem("o_done")

        def scores(n):
            return s_ps[n[1] % 2][:, :, 0:TQ * TC].rearrange("p h (u k) -> p h u k", u=TQ)

        def split(ap):
            return ap.rearrange("p (h u) k -> p h u k", h=2)

        def per_unit(ap):
            return ap.rearrange("p (h u) -> p h u", h=2).unsqueeze(3).to_broadcast((P, 2, TQ, TC))

        with nc.Block() as block:
            @block.sync
            def _(sp):
                def load_q(g):
                    sp.dma_start(wq_next[:], w["q"][:, :, bass.ds(g * P, P)]).then_inc(wq_in, DMA)

                def load_v(g):
                    sp.dma_start(v_cur[:], v_all[:, bass.ds(g, 1)].squeeze(1)).then_inc(v_in, DMA)

                if wide:
                    load_q(0)
                    load_v(0)
                    with nc.allow_non_contiguous_dma("small vectors"):
                        fetch_early(sp, prefetch)
                    sp.wait_ge(wq_set, 1)
                    load_q(1)
                    with sp.Fori(1, ROUNDS - 1, 1) as g:
                        sp.wait_ge(wq_set, g + 1)
                        load_q(g + 1)
                        sp.wait_ge(o_full, g * SR)
                        load_v(g)
                    sp.wait_ge(o_full, (ROUNDS - 1) * SR)
                    load_v(ROUNDS - 1)
                else:
                    sp.dma_start(wq[:], w["q"]).then_inc(wq_in, DMA)
                    with nc.allow_non_contiguous_dma("bias columns"):
                        sp.dma_start(bq[:], w["bq"].rearrange("(g p) o -> p (g o)", p=P)).then_inc(wq_in, DMA)
                        fetch_early(sp, prefetch)

            @block.tensor
            def _(pe):
                def slot(n):
                    a = ahead(n, 3)
                    if exists(a) and q_first(a):
                        g, s = at(a)
                        if wide:
                            if s == 0:
                                pe.wait_ge(wq_set, g + 1)
                        elif (g, s) == (0, 0):
                            pe.wait_ge(wq_in, 2 * DMA)
                        wait(pe, q_done, a, 0, PQ)
                        r0 = 0 if wide else s // PQ * P
                        c = chunk(a)
                        for k in range(KD):
                            mm = pe.matmul(q_ps[:], wq[:, k, r0:r0 + P], hT[:, k, c * HALF:(c + 1) * HALF],
                                           start=(k == 0), stop=(k == KD - 1))
                        mm.then_inc(q_full, 1)
                    a = ahead(n, 2)
                    if exists(a):
                        g, s = at(a)
                        b = chunk(a) * HALF // T
                        if PQ == 1:
                            wait(pe, q_done, a, 1)
                        else:
                            pe.wait_ge(q_done, (g * SR + s) // PQ + 1)
                        wait(pe, s_taken, a, -1)
                        for t in range(TQ):
                            q = q_sb[:, (s // PQ) % 2, t * P:(t + 1) * P]
                            if wide:
                                k = keys[:, bass.ds(g, 1), :, b, :].squeeze(1) if not isinstance(g, int) else keys[:, g, :, b, :]
                            else:
                                k = keys[:, s // PQ, 2 * (s % PQ):2 * (s % PQ) + 2, b, :]
                            mm = pe.matmul(scores(a)[:, t // 2, 2 * (t % 2):2 * (t % 2) + 2, :], q, k, start=True, stop=True)
                        mm.then_inc(s_full, 1)
                    if exists(n):
                        s = n[1]
                        wait(pe, scaled, n, 1)
                        wait(pe, t_done, n, 0)
                        for j in range(2):
                            for t in range(TQ):
                                mm = pe.transpose(t_ps[:, j, t * P:(t + 1) * P], probs[:, s % 2, 2 * t + j, :], ident[:])
                        mm.then_inc(t_full, 1)
                    a = ahead(n, -1)
                    if exists(a):
                        g, s = at(a)
                        b = chunk(a) * HALF // T
                        wait(pe, t_done, a, 1)
                        if wide and s == 0:
                            pe.wait_ge(v_in, (g + 1) * DMA)
                        wait(pe, o_done, a, 0)
                        r0 = 0 if wide else 64 * (s % 2)
                        for j in range(2):
                            v = v_cur[:, b, j, :] if wide else v_all[:, s, b, j, :]
                            mm = pe.matmul(o_ps[r0 + VW * j:r0 + VW * j + VW, :], v, turned[:, s % 2, j, :],
                                           start=True, stop=True, skip_group_check=True)
                        mm.then_inc(o_full, 1)

                run(pe, slot)

            @block.scalar
            def _(act):
                def slot(n):
                    a = ahead(n, 3)
                    if exists(a) and q_first(a):
                        g, s = at(a)
                        if PQ == 1:
                            wait(act, q_full, a, 1)
                        else:
                            act.wait_ge(q_full, (g * SR + s) // PQ + 1)
                        wait(act, s_full, a, -PQ)
                        nc.scalar.activation(q_sb[:, (s // PQ) % 2, :], q_ps[:], ACT.Identity,
                                             bias=bq[:, s // PQ:s // PQ + 1] if biased else 0.0).then_inc(q_done, 1)
                    if exists(n):
                        s = n[1]
                        wait(act, t_full, n, 1)
                        wait(act, o_full, n, -1)
                        nc.scalar.activation(turned[:, s % 2], t_ps[:], ACT.Identity).then_inc(t_done, 1)
                    a = ahead(n, 2)
                    if exists(a):
                        e = s_sb[:, a[1] % 4]
                        wait(act, shifted, a, 1)
                        nc.scalar.activation(e, e, ACT.Exp, scale=SCALE).then_inc(exp_done, 1)

                run(act, slot)

            @block.vector
            def _(dve):
                def slot(n):
                    a = ahead(n, 2)
                    if exists(a):
                        u = a[1] % 2
                        dst = split(s_sb[:, a[1] % 4])
                        wait(dve, s_full, a, 1)
                        if biased:
                            wait(dve, scaled, a, -3)
                            mask = w["key_low"](chunk(a) * HALF // T).unsqueeze(1).unsqueeze(1).to_broadcast((P, 2, TQ, TC))
                            dve.tensor_tensor(dst, scores(a), mask, ALU.add).then_inc(s_taken, 1)
                            wait(dve, s_taken, a, 1)
                            wait(dve, shifted, a, -1)
                            dve.tensor_reduce(top[:, u, :], s_sb[:, a[1] % 4], AX.X, ALU.max).then_inc(topped, 1)
                        else:
                            wait(dve, shifted, a, -1)
                            dve.tensor_reduce(top[:, u, :].rearrange("p (h u) -> p h u", h=2), scores(a), AX.X,
                                              ALU.max).then_inc(topped, 1)
                            wait(dve, topped, a, 1)
                            wait(dve, scaled, a, -3)
                            dve.tensor_tensor(dst, scores(a), per_unit(top[:, u, :]), ALU.subtract).then_inc(s_taken, 1)
                    a = ahead(n, 1)
                    if exists(a):
                        u = a[1] % 2
                        wait(dve, exp_done, a, 1)
                        wait(dve, inv_done, a, -1)
                        dve.tensor_reduce(total[:, u, :], s_sb[:, a[1] % 4], AX.X, ALU.add).then_inc(total_done, 1)
                        wait(dve, total_done, a, 1)
                        wait(dve, scaled, a, -1)
                        dve.reciprocal(inv[:, u, :], total[:, u, :]).then_inc(inv_done, 1)
                    a = ahead(n, -1)
                    if exists(a):
                        g, s = at(a)
                        wait(dve, o_full, a, 1)
                        if wide:
                            c = s
                            dst = oT[:, g, c * HALF:(c + 1) * HALF] if isinstance(g, int) else \
                                oT[:, bass.ds(g, 1), c * HALF:(c + 1) * HALF].squeeze(1)
                            dve.tensor_copy(dst, o_ps[:]).then_inc(o_done, 1)
                        else:
                            r = slice(64 * (s % 2), 64 * (s % 2) + 64)
                            dve.tensor_copy(oT[r, s // 2, g * HALF:(g + 1) * HALF], o_ps[r, :]).then_inc(o_done, 1)
                    a = ahead(n, 4)
                    if wide and at(a)[1] == 0 and exists(a):
                        wait(dve, q_full, a, 0)
                        dve.wait_ge(wq_in, (at(a)[0] + 1) * DMA)
                        dve.tensor_copy(wq[:], wq_next[:]).then_inc(wq_set, 1)

                if wide:
                    dve.wait_ge(wq_in, DMA)
                    dve.tensor_copy(wq[:], wq_next[:]).then_inc(wq_set, 1)
                run(dve, slot)

            @block.gpsimd
            def _(pool):
                pool.memset(probs[:], 0.0).then_inc(zeroed, 1)
                pool.wait_ge(zeroed, 1)

                def slot(n):
                    a = ahead(n, 2)
                    if biased and exists(a):
                        u = a[1] % 2
                        e = s_sb[:, a[1] % 4]
                        wait(pool, topped, a, 1)
                        nc.gpsimd.tensor_tensor(e, e, top[:, u, :].unsqueeze(2).to_broadcast((P, U, TC)),
                                                ALU.subtract).then_inc(shifted, 1)
                    a = ahead(n, 1)
                    if exists(a):
                        u = a[1] % 2
                        wait(pool, inv_done, a, 1)
                        wait(pool, t_full, a, -1)
                        nc.gpsimd.tensor_tensor(probs[:, u, :, 0:TC], s_sb[:, a[1] % 4],
                                                inv[:, u, :].unsqueeze(2).to_broadcast((P, U, TC)),
                                                ALU.mult).then_inc(scaled, 1)

                run(pool, slot)


GROUP = 4
NGRP = TT // GROUP


class Shared:

    def __init__(self, sem):
        self.sem, self.base = sem, 0

    def since(self, value):
        return self.base + value

    def advance(self, by):
        self.base += by


NORM_SEMS = ("loaded", "x_ready", "prod_full", "summed", "stat", "var_done", "sd_done", "normed", "turn_full",
             "h_done", "stored")


def project_norm(nc, shared, name, src, wts, loads, early, x, ln, hT, ident, out, prefetch=()):
    with ExitStack() as ctx:
        def sb(n, shape, dt=F32):
            return ctx.enter_context(nc.sbuf_tensor(f"{name}_{n}", shape, dt))

        KN = src.shape[1] if src is not None else 0
        wt, bias_b, lns = wts.get("w"), wts.get("bias"), wts["ln"]
        stats = sb("stats", [P, 2, GROUP, 6])
        mv = sb("mean_var", [P, 2, GROUP, 2])
        ve = sb("var_eps", [P, 2, GROUP])
        sd = sb("deviation", [P, 2, GROUP])
        rs = sb("inverse", [P, 2, GROUP])
        hn = sb("normed", [P, 2, GROUP, D]) if ln else None
        prod = [ctx.enter_context(nc.psum_tensor(f"{name}_prod{i}", [P, GROUP, D], F32)) for i in range(2)]
        turned = [ctx.enter_context(nc.psum_tensor(f"{name}_turned{i}", [P, KD, HALF], F32)) for i in range(2)]

        loaded = shared["loaded"]
        x_ready = shared["x_ready"]
        prod_full = shared["prod_full"]
        summed = shared["summed"]
        stat = shared["stat"]
        var_done = shared["var_done"]
        sd_done = shared["sd_done"]
        normed = shared["normed"]
        turn_full = shared["turn_full"]
        h_done = shared["h_done"]
        stored = shared["stored"]

        def ahead(first, second):
            first(0)
            for i in range(1, NGRP):
                first(i)
                second(i - 1)
            second(NGRP - 1)

        with nc.Block() as block:
            @block.sync
            def _(sp):
                with nc.allow_non_contiguous_dma("small vectors"):
                    if not early:
                        fetch_early(sp, loads)
                    fetch_early(sp, prefetch)
                if out is not None:
                    for i in range(NGRP):
                        at = slice(i * GROUP, (i + 1) * GROUP)
                        sp.wait_ge(summed.sem, summed.since(i + 1))
                        sp.dma_start(out[:, at, :], x[:, at, :]).then_inc(stored.sem, DMA)
                    sp.wait_ge(stored.sem, stored.since(NGRP * DMA))

            @block.gpsimd
            def _(pool):
                if KN:
                    pool.wait_ge(loaded.sem, loaded.since(DMA * len(loads)))
                    for i in range(NGRP):
                        at = slice(i * GROUP, (i + 1) * GROUP)
                        nc.gpsimd.tensor_tensor(x[:, at, :], x[:, at, :],
                                                bias_b[:].unsqueeze(1).to_broadcast((P, GROUP, D)),
                                                ALU.add).then_inc(x_ready.sem, 1)

            @block.tensor
            def _(pe):
                def product(i):
                    if not KN:
                        return
                    if i == 0:
                        pe.wait_ge(loaded.sem, loaded.since(DMA * len(loads)))
                    if i >= 2:
                        pe.wait_ge(summed.sem, summed.since(i - 1))
                    for t in range(GROUP):
                        at = (i * GROUP + t) * P
                        for k in range(KN):
                            mm = pe.matmul(prod[i % 2][:, t, :], src[:, k, at:at + P], wt[:, k, :],
                                           start=(k == 0), stop=(k == KN - 1))
                    mm.then_inc(prod_full.sem, 1)

                def turn(i):
                    if not ln:
                        return
                    pe.wait_ge(normed.sem, normed.since(i + 1))
                    if i >= 2:
                        pe.wait_ge(h_done.sem, h_done.since(i - 1))
                    for k in range(KD):
                        for t in range(GROUP):
                            mm = pe.transpose(turned[i % 2][:, k, t * P:(t + 1) * P],
                                              hn[:, i % 2, t, k * P:(k + 1) * P], ident[:])
                    mm.then_inc(turn_full.sem, 1)

                ahead(product, turn)

            @block.vector
            def _(dve):
                step = Step(stat.sem, stat.base)
                def stats_of(i):
                    at = slice(i * GROUP, (i + 1) * GROUP)
                    u = i % 2
                    if KN:
                        dve.wait_ge(x_ready.sem, x_ready.since(i + 1))
                        dve.wait_ge(prod_full.sem, prod_full.since(i + 1))
                        dve.tensor_tensor(x[:, at, :], prod[u][:], x[:, at, :], ALU.add).then_inc(summed.sem, 1)
                        dve.wait_ge(summed.sem, summed.since(i + 1))
                    elif i == 0:
                        dve.wait_ge(loaded.sem, loaded.since(DMA * len(loads)))
                    if not ln:
                        return
                    for t in range(GROUP):
                        ins = dve.bn_stats(stats[:, u, t, :], x[:, i * GROUP + t, :])
                    step(ins)
                    step.wait(dve)
                    for t in range(GROUP):
                        ins = dve.bn_aggr(mv[:, u, t, :], stats[:, u, t, :])
                    step(ins)
                    step.wait(dve)
                    dve.tensor_scalar(ve[:, u, :], mv[:, u, :, 1], EPS, None, ALU.add).then_inc(var_done.sem, 1)

                def normalise(i):
                    if not ln:
                        return
                    u = i % 2
                    dve.wait_ge(sd_done.sem, sd_done.since(i + 1))
                    step(dve.reciprocal(rs[:, u, :], sd[:, u, :]))
                    step.wait(dve)
                    if i >= 2:
                        dve.wait_ge(turn_full.sem, turn_full.since(i - 1))
                    for t in range(GROUP):
                        ins = dve.tensor_scalar(hn[:, u, t, :], x[:, i * GROUP + t, :], mv[:, u, t, 0:1],
                                                rs[:, u, t:t + 1], ALU.subtract, ALU.mult)
                    ins.then_inc(normed.sem, 1)

                ahead(stats_of, normalise)

            @block.scalar
            def _(act):
                def root(i):
                    if ln:
                        act.wait_ge(var_done.sem, var_done.since(i + 1))
                        nc.scalar.activation(sd[:, i % 2, :], ve[:, i % 2, :], ACT.Sqrt).then_inc(sd_done.sem, 1)

                def evacuate(i):
                    if ln:
                        act.wait_ge(turn_full.sem, turn_full.since(i + 1))
                        for k in range(KD):
                            ins = nc.scalar.activation(hT[:, k, i * HALF:(i + 1) * HALF], turned[i % 2][:, k, :],
                                                       ACT.Identity, scale=lns[:, 0, k:k + 1],
                                                       bias=lns[:, 1, k:k + 1])
                        ins.then_inc(h_done.sem, 1)

                ahead(root, evacuate)

        loaded.advance(DMA * len(loads))
        if KN:
            for s in (x_ready, prod_full, summed):
                s.advance(NGRP)
        if ln:
            for s in (var_done, sd_done, normed, turn_full, h_done):
                s.advance(NGRP)
        if out is not None:
            stored.advance(NGRP * DMA)
        stat.advance(3 * NGRP if ln else 0)


def hidden_layer(nc, name, hT, w1, b1, gated, hid, prefetch=()):
    FF = 4 * D
    MT = FF // P
    NC4 = NT // HALF
    with ExitStack() as ctx:
        def sem(n):
            return ctx.enter_context(nc.semaphore(f"{name}_{n}"))

        NB = 2 if gated else 1
        w = ctx.enter_context(nc.sbuf_tensor(f"{name}_w1", [P, 2, NB, KD, P], F32))
        w_hi, w_lo = [ctx.enter_context(nc.sbuf_tensor(f"{name}_w1_{n}", [P, 2, NB, KD, P], F32R)) for n in ("hi", "lo")]
        h_hi, h_lo = [ctx.enter_context(nc.sbuf_tensor(f"{name}_h_{n}", [P, KD, NT], F32R)) for n in ("hi", "lo")]
        bb = ctx.enter_context(nc.sbuf_tensor(f"{name}_b1", [P, 2, NB], F32))
        gate = ctx.enter_context(nc.sbuf_tensor(f"{name}_gate", [P, NC4, HALF], F32)) if gated else None
        banks = [ctx.enter_context(nc.psum_tensor(f"{name}_ps{i}", [P, HALF], F32)) for i in range(8)]
        loaded = [sem(f"loaded{u}") for u in range(2)]
        w_high = sem("w_high")
        w_split = sem("w_split")
        h_high = sem("h_high")
        h_split = sem("h_split")
        g_full = sem("g_full")
        a_full = sem("a_full")
        gelu = sem("gelu")
        done = sem("done")
        last = done if gated else gelu

        def bank(u, c, n):
            return banks[4 * n + c] if gated else banks[4 * u + c]

        def walk(eng, tile):
            tile(0, 0, (0, 1))
            tile(0, 1, (1, 0))
            with eng.Fori(1, MT // 2 - 1, 1) as i:
                tile(i, 0, (i, 1))
                tile(i, 1, (i + 1, 0))
            tile(MT // 2 - 1, 0, (MT // 2 - 1, 1))
            tile(MT // 2 - 1, 1, None)

        def ready(eng, s, mt, k):
            if not isinstance(mt, int) or 4 * mt + k > 0:
                eng.wait_ge(s, mt * NC4 + k)

        with nc.Block() as block:
            @block.sync
            def _(sp):
                def load(mt, u):
                    for n in range(NB):
                        col = mt * P + ((1 - n) * FF if gated else 0)
                        with nc.allow_non_contiguous_dma("bias column"):
                            sp.dma_start(w[:, u, n], w1[:, :, bass.ds(col, P)]).then_inc(loaded[u], DMA)
                            sp.dma_start(bb[:, u, n:n + 1], b1[bass.ds(col, P), :]).then_inc(loaded[u], DMA)

                load(0, 0)
                load(1, 1)
                with nc.allow_non_contiguous_dma("small vectors"):
                    fetch_early(sp, prefetch)
                with sp.Fori(1, MT // 2, 1) as i:
                    for u in range(2):
                        sp.wait_ge(last, i * (2 * NC4) + (u - 1) * NC4)
                        load(i * 2 + u, u)

            @block.tensor
            def _(pe):
                def tile(i, u, _split):
                    mt = i * 2 + u
                    pe.wait_ge(w_split, mt + 1)
                    for c in range(NC4):
                        if isinstance(mt, int) and mt == 0:
                            pe.wait_ge(h_split, KD * (c + 1))
                        for n in range(NB):
                            if gated:
                                ready(pe, gelu if n == 0 else done, mt, c - NC4 + 1)
                            else:
                                ready(pe, gelu, mt, c - 2 * NC4 + 1)
                            at = slice(c * HALF, (c + 1) * HALF)
                            parts = [(ws[:, u, n, k, :], hs[:, k, at]) for k in range(KD)
                                     for ws, hs in ((w_hi, h_hi), (w_hi, h_lo), (w_lo, h_hi))]
                            for p, (ws, hs) in enumerate(parts):
                                mm = pe.matmul(bank(u, c, n)[:], ws, hs, start=(p == 0), stop=(p == len(parts) - 1))
                            mm.then_inc(a_full if n else g_full, 1)
                walk(pe, tile)

            @block.scalar
            def _(act):
                def split(i, u):
                    act.wait_ge(loaded[u], (i + 1) * (2 * NB * DMA))
                    nc.scalar.activation(w_hi[:, u], w[:, u], ACT.Identity).then_inc(w_high, 1)

                def tile(i, u, ahead):
                    mt = i * 2 + u
                    for c in range(NC4):
                        if c == NC4 - 1 and ahead:
                            split(*ahead)
                        act.wait_ge(g_full, mt * NC4 + (c + 1))
                        if gated:
                            ready(act, done, mt, c - NC4 + 1)
                            dst = gate[:, c, :]
                        else:
                            dst = hid[:, bass.ds(mt, 1), c * HALF:(c + 1) * HALF].squeeze(1) \
                                if not isinstance(mt, int) else hid[:, mt, c * HALF:(c + 1) * HALF]
                        nc.scalar.activation(dst, bank(u, c, 0)[:], ACT.Gelu, bias=bb[:, u, 0:1]).then_inc(gelu, 1)
                split(0, 0)
                for c in range(NC4):
                    for k in range(KD):
                        at = slice(c * HALF, (c + 1) * HALF)
                        nc.scalar.activation(h_hi[:, k, at], hT[:, k, at], ACT.Identity).then_inc(h_high, 1)
                walk(act, tile)

            @block.vector
            def _(dve):
                def split(i, u):
                    dve.wait_ge(w_high, i * 2 + (u + 1))
                    dve.tensor_tensor(w_lo[:, u], w[:, u], w_hi[:, u].bitcast(F32), ALU.subtract).then_inc(w_split, 1)

                def tile(i, u, ahead):
                    mt = i * 2 + u
                    if not gated:
                        if ahead:
                            split(*ahead)
                        return
                    for c in range(NC4):
                        if c == NC4 - 1 and ahead:
                            split(*ahead)
                        dve.wait_ge(a_full, mt * NC4 + (c + 1))
                        dve.wait_ge(gelu, mt * NC4 + (c + 1))
                        dst = hid[:, bass.ds(mt, 1), c * HALF:(c + 1) * HALF].squeeze(1) \
                            if not isinstance(mt, int) else hid[:, mt, c * HALF:(c + 1) * HALF]
                        dve.scalar_tensor_tensor(out=dst, in0=bank(u, c, 1)[:], scalar=bb[:, u, 1:2],
                                                 in1=gate[:, c, :], op0=ALU.add, op1=ALU.mult).then_inc(done, 1)
                split(0, 0)
                for c in range(NC4):
                    for k in range(KD):
                        at = slice(c * HALF, (c + 1) * HALF)
                        dve.wait_ge(h_high, c * KD + k + 1)
                        dve.tensor_tensor(h_lo[:, k, at], hT[:, k, at], h_hi[:, k, at].bitcast(F32),
                                          ALU.subtract).then_inc(h_split, 1)
                walk(dve, tile)


def constants(nc, a, ident, ones, ctxT, key_mask, ctx_low, prefetch):
    with ExitStack() as ctx:
        def sb(n, shape, dt=F32):
            return ctx.enter_context(nc.sbuf_tensor(f"const_{n}", shape, dt))

        def sem(n):
            return ctx.enter_context(nc.semaphore(f"const_{n}"))

        c_in = sb("ctx", [P, B, DC])
        m_in = sb("mask", [P, B, QT], U8)
        r_in = sb("rmask", [P, B, TC], U8)
        ps = [ctx.enter_context(nc.psum_tensor(f"const_ps{i}", [P, HALF], F32)) for i in range(B)]
        LOADS = 1 + 2 * B
        loaded = sem("loaded")
        made = sem("made")
        turned = sem("turned")
        with nc.Block() as block:
            @block.sync
            def _(sp):
                with nc.allow_non_contiguous_dma("masks, once"):
                    sp.dma_start(c_in[0:TC], a["ctx_768"].rearrange("b t c -> t b c")).then_inc(loaded, DMA)
                    for b in range(B):
                        sp.dma_start(m_in[:, b, :], a["mask_BxS_bf0"][b].rearrange("(t p) -> p t", p=P)).then_inc(loaded, DMA)
                        sp.dma_start(r_in[:, b, :], a["mask_BxS2_bf0"][b:b + 1, :].to_broadcast((P, TC))).then_inc(loaded, DMA)
                    fetch_early(sp, prefetch)
                    sp.wait_ge(loaded, DMA * LOADS)

            @block.gpsimd
            def _(pool):
                pool.memset(ones[:], 1.0)
                pool.memset(ident[:], 0.0).then_inc(made, 1)
                pool.wait_ge(made, 1)
                nc.gpsimd.affine_select(out=ident[:], in_=ident[:], compare_op=ALU.not_equal, fill=1.0, base=0,
                                        pattern=[[-1, P]], channel_multiplier=1).then_inc(made, 1)

            @block.tensor
            def _(pe):
                pe.wait_ge(loaded, DMA * LOADS)
                pe.wait_ge(made, 2)
                for b in range(B):
                    for k in range(KC):
                        mm = pe.transpose(ps[b][0:CW, k * P:k * P + TC], c_in[0:TC, b, k * CW:(k + 1) * CW],
                                          ident[0:TC, 0:TC])
                    mm.then_inc(turned, 1)

            @block.vector
            def _(dve):
                dve.wait_ge(loaded, DMA * LOADS)
                dve.tensor_scalar(key_mask[:], m_in[:], -3e38, 3e38, ALU.mult, ALU.mult)
                dve.tensor_scalar(ctx_low[:], r_in[:], -3e38, 3e38, ALU.mult, ALU.mult)
                for b in range(B):
                    dve.wait_ge(turned, b + 1)
                    for k in range(KC):
                        dve.tensor_copy(ctxT[0:CW, b, k, 0:TC], ps[b][0:CW, k * P:k * P + TC])


LOW_AT = [P * qt * (qt + 1) // 2 for qt in range(QT + 1)]


def causal_masks(nc, mask, low, spare_rows):
    with ExitStack() as ctx:
        rows = ctx.enter_context(nc.sbuf_tensor("low_rows", [P, B, T], U8))
        loaded = ctx.enter_context(nc.semaphore("low_loaded"))
        keys = ctx.enter_context(nc.semaphore("low_keys"))
        done = ctx.enter_context(nc.semaphore("low_done"))
        with nc.Block() as block:
            @block.sync
            def _(sp):
                for b in range(B):
                    sp.dma_start(rows[:, b, :], mask[b:b + 1, :].to_broadcast((P, T))).then_inc(loaded, DMA)

            @block.vector
            def _(dve):
                dve.memset(spare_rows, 0.0)
                dve.wait_ge(loaded, DMA * B)
                for b in range(B):
                    for qt in range(QT):
                        dve.tensor_scalar(low[:, b, LOW_AT[qt]:LOW_AT[qt + 1]], rows[:, b, 0:(qt + 1) * P], LOW, None,
                                          ALU.mult).then_inc(keys, 1)

            @block.gpsimd
            def _(pool):
                for b in range(B):
                    for qt in range(QT):
                        pool.wait_ge(keys, b * QT + qt + 1)
                        blk = low[:, b, LOW_AT[qt + 1] - P:LOW_AT[qt + 1]]
                        nc.gpsimd.affine_select(out=blk, in_=blk, compare_op=ALU.is_ge, fill=LOW, base=0,
                                                pattern=[[-1, P]], channel_multiplier=1).then_inc(done, 1)
                pool.wait_ge(done, B * QT)


def decoder_blocks(nc, a, out):
    L0 = {k[len("L0_xattn_"):]: v for k, v in a.items() if k.startswith("L0_")}
    L1 = {k[len("L1_xattn_"):]: v for k, v in a.items() if k.startswith("L1_")}

    def by_rows(ap, p=P):
        return ap.rearrange("(k p) n -> p k n", p=p)

    def column(ap):
        return ap.rearrange("(n o) -> n o", o=1)

    def row(ap):
        return ap.rearrange("(o n) -> o n", o=1)

    x_dram = a["x"].rearrange("b t d -> (b t) d").rearrange("(t p) d -> p t d", p=P)
    out_dram = out.rearrange("b t d -> (b t) d").rearrange("(t p) d -> p t d", p=P)

    with ExitStack() as ctx:
        def keep(n, shape, dt=F32):
            return ctx.enter_context(nc.sbuf_tensor(n, shape, dt))

        def scoped(n, shape, dt=F32):
            return nc.sbuf_tensor(n, shape, dt)

        norm_sems = {n: Shared(ctx.enter_context(nc.semaphore(f"norm_{n}"))) for n in NORM_SEMS}
        norm_in = norm_sems["loaded"].sem
        kv_in = [ctx.enter_context(nc.semaphore(f"kv_in{i}")) for i in range(2)]
        ident, ones = keep("ident", [P, P]), keep("ones", [P, 64])
        ctxT = keep("ctxT", [P, B, KC, TC + 1])
        key_mask = keep("key_mask", [P, B, QT])
        ctx_low = keep("ctx_low", [P, B, TC])
        lns = keep("ln", [P, 2, KD])
        hT = keep("hT", [P, KD, NT])
        x = keep("x", [P, TT, D])

        def ln_loads(g, b):
            return [(lns[:, i, :], v.rearrange("(k p) -> p k", p=P), norm_in) for i, v in enumerate((g, b))]

        def norm_loads(wts, pieces, bias, ln):
            out = [(dst, src, norm_in) for dst, src in pieces]
            out.append((wts["bias"][:], row(bias).to_broadcast((P, D)), norm_in))
            return out + (ln_loads(*ln) if ln else [])

        first = [(x[:], x_dram, norm_in)] + ln_loads(L0["ln1_g"], L0["ln1_b"])
        constants(nc, a, ident, ones, ctxT, key_mask, ctx_low, first)
        project_norm(nc, norm_sems, "ln01", None, {"ln": lns}, first, True, x, True, hT, ident, None)

        wide = {"G": 2, "dh": 64, "biased": False}
        NG = HEADS // 2
        with scoped("o0", [P, NG, NT]) as oT:
            attention(nc, "sa0", {**wide, "causal": False}, hT, ident, ones,
                      {"q": by_rows(L0["sa_wq"]), "k": by_rows(L0["sa_wk"]), "v": by_rows(L0["sa_wv"]),
                       "key_bias": lambda b, kt: 0.0}, oT, spare=x)
            with scoped("w_out0", [P, NG, D]) as w_out, scoped("bias_out0", [P, D]) as bias_out:
                wts = {"w": w_out, "bias": bias_out, "ln": lns}
                with scoped("wk0", [P, KC, HEADS * 64]) as wk, scoped("wv0", [P, KC, HEADS * 64]) as wv:
                    kv = {"wk": wk, "wv": wv, "sem": kv_in[0]}
                    fetch_kv = [(wk[0:CW], by_rows(L0["ca_wk"], CW), kv_in[0]), (wv[0:CW], by_rows(L0["ca_wv"], CW), kv_in[0])]
                    loads = norm_loads(wts, [(w_out[:], by_rows(L0["sa_wo"]))], L0["sa_bo"], (L0["ln2_g"], L0["ln2_b"]))
                    project_norm(nc, norm_sems, "po0", oT, wts, loads + [(x[:], x_dram, norm_in)], False, x, True, hT, ident,
                                 None, fetch_kv)
                    loads = norm_loads(wts, [(w_out[:], by_rows(L0["ca_wo"]))], L0["ca_bo"], (L0["ln3_g"], L0["ln3_b"]))
                    cross_attention(nc, "ca0", wide, hT, ctxT, ident, kv, {"q": by_rows(L0["ca_wq"])}, oT, loads)
                project_norm(nc, norm_sems, "pc0", oT, wts, loads, True, x, True, hT, ident, None)
                loads = norm_loads(wts, [(w_out[:], by_rows(L0["ff_w2"]))], L0["ff_b2"], (L1["ln1_w"], L1["ln1_b"]))
                hidden_layer(nc, "ff0", hT, by_rows(L0["ff_w1"]), column(L0["ff_b1"]), True, oT, loads)
                project_norm(nc, norm_sems, "pf0", oT, wts, loads, True, x, True, hT, ident, None)

        thin = {"G": 4, "dh": 16, "biased": True}
        NG = HEADS // 4

        with scoped("w_out1", [P, NG, D]) as w_out, scoped("bias_out1", [P, D]) as bias_out, \
                scoped("o1", [P, NG, NT]) as oT:
            wts = {"w": w_out, "bias": bias_out, "ln": lns}

            def padded(ap):
                v = ap.rearrange("(g j d) n -> j d g n", g=NG, j=4)
                return [(w_out[32 * j:32 * j + 16, :, :], v[j]) for j in range(4)]

            loads = norm_loads(wts, padded(L1["proj_w"]), L1["proj_b"], (L1["ln2_w"], L1["ln2_b"]))
            with scoped("low", [P, B, LOW_AT[QT]], BF16) as low:
                causal_masks(nc, a["mask_BxS_bf0"], low, w_out[:])
                attention(nc, "sa1", {**thin, "causal": True}, hT, ident, ones,
                          {"q": by_rows(L1["qkv_w"]), "bq": column(L1["qkv_b"]),
                           "bv": row(L1["qkv_b"])[:, 2 * D:3 * D],
                           "head_rows": a["head_rows"], "key_bias": lambda b, kt: key_mask[:, b, kt:kt + 1],
                           "key_low": lambda b, qt, k0, n: low[:, b, LOW_AT[qt] + k0:LOW_AT[qt] + k0 + n]}, oT,
                          prefetch=loads)
            with scoped("wk1", [P, KC, D]) as wk, scoped("wv1", [P, KC, D]) as wv, \
                    scoped("bk1", [P, D // P]) as bk, scoped("bv1", [P, D]) as bv:
                kv = {"wk": wk, "wv": wv, "bk": bk, "bv": bv, "sem": kv_in[1]}
                fetch_kv = [(wk[0:CW], by_rows(L1["k_w"], CW), kv_in[1]), (wv[0:CW], by_rows(L1["v_w"], CW), kv_in[1]),
                            (bk[:], L1["k_b"].rearrange("(g p) -> p g", p=P), kv_in[1]),
                            (bv[:], row(L1["v_b"]).to_broadcast((P, D)), kv_in[1])]
                project_norm(nc, norm_sems, "po1", oT, wts, loads, True, x, True, hT, ident, None, fetch_kv)
                loads = norm_loads(wts, padded(L1["out_w"]), L1["out_b"], (L1["ln3_w"], L1["ln3_b"]))
                cross_attention(nc, "ca1", thin, hT, ctxT, ident, kv,
                                {"q": by_rows(L1["q_w"]), "bq": column(L1["q_b"]), "key_low": lambda b: ctx_low[:, b, :]},
                                oT, loads)
            project_norm(nc, norm_sems, "pc1", oT, wts, loads, True, x, True, hT, ident, None)
        with scoped("w_out2", [P, 4 * D // P, D]) as w_out, scoped("bias_out2", [P, D]) as bias_out, \
                scoped("hid1", [P, 4 * D // P, NT]) as hid:
            wts = {"w": w_out, "bias": bias_out, "ln": lns}
            loads = norm_loads(wts, [(w_out[:], by_rows(L1["mlp2_w"]))], L1["mlp2_b"], None)
            hidden_layer(nc, "ff1", hT, by_rows(L1["mlp1_w"]), column(L1["mlp1_b"]), False, hid, loads)
            project_norm(nc, norm_sems, "pf1", hid, wts, loads, True, x, False, hT, ident, out_dram)


def head_rows():
    import numpy as np
    rows = np.zeros((P, 2), np.float32)
    for h in range(2):
        for slot in range(3):
            rows[32 * slot + 16 * h:32 * slot + 16 * h + 16, h] = 1.0
        rows[96 + 2 * h:96 + 2 * h + 2, h] = 1.0
    return rows


def kernel(**inputs):
    import numpy as np
    import concourse.bacc as bacc
    from concourse.bass_utils import run_bass_kernel_spmd

    nc = bacc.Bacc("TRN2", target_bir_lowering=False, num_devices=1)
    arrays, aps = {}, {}
    for name, value in inputs.items():
        v = np.ascontiguousarray(value)
        arrays[f"in_{name}"] = v
        aps[name] = nc.dram_tensor(f"in_{name}", v.shape, mybir.dt.from_np(v.dtype), kind="ExternalInput").ap()
    rows = head_rows()
    arrays["in_head_rows"] = rows
    aps["head_rows"] = nc.dram_tensor("in_head_rows", rows.shape, F32, kind="ExternalInput").ap()
    out = nc.dram_tensor("out", (B, T, D), F32, kind="ExternalOutput").ap()
    decoder_blocks(nc, aps, out)
    r = run_bass_kernel_spmd(nc, [arrays], core_ids=[0])
    return r.results[0]["out"]
```
